# Optimizing a Trainium2 kernel written in Bass

```python
import numpy as np
import jax
import jax.numpy as jnp

def _softmax(x, axis=-1):
    return jax.nn.softmax(x, axis=axis)

def _gelu(x):
    return jax.nn.gelu(x, approximate=True)

def _silu(x):
    return jax.nn.silu(x)

def _sigmoid(x):
    return jax.nn.sigmoid(x)

def _layernorm(x, axis=-1, eps=1e-05):
    m = jnp.mean(x, axis=axis, keepdims=True)
    v = jnp.var(x, axis=axis, keepdims=True)
    return (x - m) / jnp.sqrt(v + eps)

def _scatter_add(tgt, idx, src, axis=0):
    return tgt.at[idx].add(src)

def _segment_sum(src, seg, n):
    return jax.ops.segment_sum(src, seg, n)
kernel_name = 'mk_gnn_preln_d4_gnn_r64_f64978'

def setup_inputs(seed: int=0):
    np.random.seed(seed)
    _w = jnp.asarray

    def _rec_inputs():
        import jax
        import jax.numpy as jnp
        _gk = jax.random.key(seed)
        x = -0.0003713 + 1 * jax.random.normal(jax.random.fold_in(_gk, 1), (50000, 128), jnp.float32)
        src = jax.random.randint(jax.random.fold_in(_gk, 2), (25000,), 0, 50000, jnp.int32)
        dst = jnp.minimum((50000 * jax.random.uniform(jax.random.fold_in(_gk, 3), (25000,)) ** 2.0).astype(jnp.int32), 49999)
        _o = jnp.argsort(dst, stable=True)
        src = src[_o]
        dst = dst[_o]
        edge_attr_16 = 0.000254156 + 0.999948 * jax.random.normal(jax.random.fold_in(_gk, 11), (25000, 16), jnp.float32)
        return (x, src, dst, edge_attr_16)
    x, src, dst, edge_attr_16 = _rec_inputs()

    def _L0_gnn_setup():
        import jax, jax.numpy as jnp
        import numpy as np
        N_NODES = 100000
        N_EDGES = 50000
        IN_DIM, HID_DIM, OUT_DIM = (128, 256, 128)

        def gcn_conv(x, W, b, src, dst, n_nodes):
            xw = x @ W
            ones = jnp.ones(src.shape[0], dtype=xw.dtype)
            deg = jax.ops.segment_sum(ones, dst, num_segments=n_nodes)
            dis = jnp.where(deg > 0, jax.lax.rsqrt(jnp.maximum(deg, 1e-12)), 0.0)
            norm = dis[src] * dis[dst]
            msgs = norm[:, None] * xw[src]
            out = jax.ops.segment_sum(msgs, dst, num_segments=n_nodes)
            return out + b
        key = jax.random.key(seed)
        k1, k2, k3, k4, k5, k6 = jax.random.split(key, 6)
        x = jax.random.normal(k1, (N_NODES, IN_DIM), dtype=jnp.float32)
        edge_index = jax.random.randint(k2, (2, N_EDGES), 0, N_NODES, dtype=jnp.int64)
        s1 = 1.0 / np.sqrt(IN_DIM)
        s2 = 1.0 / np.sqrt(HID_DIM)
        W1 = jax.random.uniform(k3, (IN_DIM, HID_DIM), jnp.float32, -s1, s1)
        b1 = jax.random.uniform(k4, (HID_DIM,), jnp.float32, -s1, s1)
        W2 = jax.random.uniform(k5, (HID_DIM, OUT_DIM), jnp.float32, -s2, s2)
        b2 = jax.random.uniform(k6, (OUT_DIM,), jnp.float32, -s2, s2)
        return {'x': x, 'edge_index': edge_index, 'W1': W1, 'b1': b1, 'W2': W2, 'b2': b2}
    _L0_gnn_all = _L0_gnn_setup()
    _L0_gnn_in = {k: v for k, v in _L0_gnn_all.items() if k in ('W1', 'b1', 'W2', 'b2')}
    del _L0_gnn_all

    def _L1_gnn_setup():
        import jax, jax.numpy as jnp
        import numpy as np
        N = 100000
        E = 25000
        DIN = 128
        DH = 128

        def sage_conv(x, edge_index, wl, bl, wr):
            row, col = (edge_index[0], edge_index[1])
            num_nodes = x.shape[0]
            agg = jax.ops.segment_sum(x[row], col, num_segments=num_nodes)
            deg = jax.ops.segment_sum(jnp.ones((row.shape[0],), x.dtype), col, num_segments=num_nodes)
            mean = agg / jnp.maximum(deg, 1.0)[:, None]
            return mean @ wl + bl + x @ wr
        key = jax.random.key(seed)
        ks = jax.random.split(key, 8)
        x = jax.random.normal(ks[0], (N, DIN), dtype=jnp.float32)
        edge_index = jax.random.randint(ks[1], (2, E), 0, N, dtype=jnp.int32)
        s_in = 1.0 / np.sqrt(DIN)
        s_h = 1.0 / np.sqrt(DH)
        w1l = jax.random.normal(ks[2], (DIN, DH), dtype=jnp.float32) * s_in
        b1l = jnp.zeros((DH,), dtype=jnp.float32)
        w1r = jax.random.normal(ks[3], (DIN, DH), dtype=jnp.float32) * s_in
        w2l = jax.random.normal(ks[4], (DH, DH), dtype=jnp.float32) * s_h
        b2l = jnp.zeros((DH,), dtype=jnp.float32)
        w2r = jax.random.normal(ks[5], (DH, DH), dtype=jnp.float32) * s_h
        return {'x': x, 'edge_index': edge_index, 'w1l': w1l, 'b1l': b1l, 'w1r': w1r, 'w2l': w2l, 'b2l': b2l, 'w2r': w2r}
    _L1_gnn_all = _L1_gnn_setup()
    _L1_gnn_in = {k: v for k, v in _L1_gnn_all.items() if k in ('w1l', 'b1l', 'w1r', 'w2l', 'b2l', 'w2r')}
    del _L1_gnn_all

    def _L2_gnn_setup():
        import jax, jax.numpy as jnp
        import numpy as np
        N, E, D_IN, D_H, D_E, L = (50000, 12500, 128, 128, 16, 3)
        LN_EPS = 1e-05
        key = jax.random.key(seed)
        ks = jax.random.split(key, 8)
        x = jax.random.normal(ks[0], (N, D_IN), jnp.float32)
        edge_index = jax.random.randint(ks[1], (2, E), 0, N, jnp.int32)
        edge_attr = jax.random.normal(ks[2], (E, D_E), jnp.float32)
        s = lambda d: 1.0 / np.sqrt(d)
        lin_w = jax.random.normal(ks[3], (L, D_IN, D_H), jnp.float32) * s(D_IN)
        edge_w1 = jax.random.normal(ks[4], (L, D_E, D_H), jnp.float32) * s(D_E)
        edge_b1 = jnp.zeros((L, D_H), jnp.float32)
        edge_w2 = jax.random.normal(ks[5], (L, D_H, D_H), jnp.float32) * s(D_H)
        edge_b2 = jnp.zeros((L, D_H), jnp.float32)
        bias = jnp.zeros((L, D_H), jnp.float32)
        ln_w = jnp.ones((L, D_H), jnp.float32)
        ln_b = jnp.zeros((L, D_H), jnp.float32)
        return dict(x=x, edge_attr=edge_attr, lin_w=lin_w, edge_w1=edge_w1, edge_b1=edge_b1, edge_w2=edge_w2, edge_b2=edge_b2, bias=bias, ln_w=ln_w, ln_b=ln_b, edge_index=edge_index)
    _L2_gnn_all = _L2_gnn_setup()
    _L2_gnn_in = {k: v for k, v in _L2_gnn_all.items() if k in ('lin_w', 'edge_w1', 'edge_b1', 'edge_w2', 'edge_b2', 'bias', 'ln_w', 'ln_b')}
    del _L2_gnn_all

    def _L3_gnn_setup():
        import jax, jax.numpy as jnp
        import numpy as np
        N, E, IN, C, H = (50000, 25000, 128, 64, 2)
        HC = H * C
        NEG_SLOPE = 0.2

        def gat_layer(xf, src, dst, W, a_src, a_dst, b, heads, out_ch):
            n = xf.shape[0]
            h = (xf @ W).reshape(n, heads, out_ch)
            e_src = jnp.einsum('nhc,hc->nh', h, a_src)
            e_dst = jnp.einsum('nhc,hc->nh', h, a_dst)
            e = jax.nn.leaky_relu(e_src[src] + e_dst[dst], NEG_SLOPE)
            m = jax.ops.segment_max(e, dst, num_segments=n)
            p = jnp.exp(e - m[dst])
            s = jax.ops.segment_sum(p, dst, num_segments=n)
            alpha = p / (s[dst] + 1e-16)
            out = jax.ops.segment_sum(alpha[:, :, None] * h[src], dst, num_segments=n)
            return out.reshape(n, heads * out_ch) + b
        key = jax.random.key(seed)
        ks = jax.random.split(key, 16)
        x = jax.random.normal(ks[0], (N, IN), dtype=jnp.float32)
        edge_index = jax.random.randint(ks[1], (2, E), 0, N, dtype=jnp.int64)

        def gat_params(k, fan_in, heads, out_ch):
            k1, k2, k3 = jax.random.split(k, 3)
            sc = 1.0 / np.sqrt(fan_in)
            W = jax.random.normal(k1, (fan_in, heads * out_ch), dtype=jnp.float32) * sc
            a_src = jax.random.normal(k2, (heads, out_ch), dtype=jnp.float32) * 0.1
            a_dst = jax.random.normal(k3, (heads, out_ch), dtype=jnp.float32) * 0.1
            b = jnp.zeros((heads * out_ch,), dtype=jnp.float32)
            return (W, a_src, a_dst, b)
        W_in, a_src_in, a_dst_in, b_in = gat_params(ks[2], IN, H, C)
        Wh, ash, adh, bh = ([], [], [], [])
        for i in range(2):
            W, a_s, a_d, b = gat_params(ks[3 + i], HC, H, C)
            Wh.append(W)
            ash.append(a_s)
            adh.append(a_d)
            bh.append(b)
        W_h = jnp.stack(Wh)
        a_src_h = jnp.stack(ash)
        a_dst_h = jnp.stack(adh)
        b_h = jnp.stack(bh)
        W_out, a_src_out, a_dst_out, b_out = gat_params(ks[6], HC, H, C)
        return dict(x=x, edge_index=edge_index, W_in=W_in, a_src_in=a_src_in, a_dst_in=a_dst_in, b_in=b_in, W_h=W_h, a_src_h=a_src_h, a_dst_h=a_dst_h, b_h=b_h, W_out=W_out, a_src_out=a_src_out, a_dst_out=a_dst_out, b_out=b_out)
    _L3_gnn_all = _L3_gnn_setup()
    _L3_gnn_in = {k: v for k, v in _L3_gnn_all.items() if k in ('W_in', 'a_src_in', 'a_dst_in', 'b_in', 'W_h', 'a_src_h', 'a_dst_h', 'b_h', 'W_out', 'a_src_out', 'a_dst_out', 'b_out')}
    del _L3_gnn_all
    return {'x': x, 'src': src, 'dst': dst, 'edge_attr_16': edge_attr_16, 'L0_gnn_W1': _L0_gnn_in['W1'], 'L0_gnn_b1': _L0_gnn_in['b1'], 'L0_gnn_W2': _L0_gnn_in['W2'], 'L0_gnn_b2': _L0_gnn_in['b2'], 'L1_gnn_w1l': _L1_gnn_in['w1l'], 'L1_gnn_b1l': _L1_gnn_in['b1l'], 'L1_gnn_w1r': _L1_gnn_in['w1r'], 'L1_gnn_w2l': _L1_gnn_in['w2l'], 'L1_gnn_b2l': _L1_gnn_in['b2l'], 'L1_gnn_w2r': _L1_gnn_in['w2r'], 'L2_gnn_lin_w': _L2_gnn_in['lin_w'], 'L2_gnn_edge_w1': _L2_gnn_in['edge_w1'], 'L2_gnn_edge_b1': _L2_gnn_in['edge_b1'], 'L2_gnn_edge_w2': _L2_gnn_in['edge_w2'], 'L2_gnn_edge_b2': _L2_gnn_in['edge_b2'], 'L2_gnn_bias': _L2_gnn_in['bias'], 'L2_gnn_ln_w': _L2_gnn_in['ln_w'], 'L2_gnn_ln_b': _L2_gnn_in['ln_b'], 'L3_gnn_W_in': _L3_gnn_in['W_in'], 'L3_gnn_a_src_in': _L3_gnn_in['a_src_in'], 'L3_gnn_a_dst_in': _L3_gnn_in['a_dst_in'], 'L3_gnn_b_in': _L3_gnn_in['b_in'], 'L3_gnn_W_h': _L3_gnn_in['W_h'], 'L3_gnn_a_src_h': _L3_gnn_in['a_src_h'], 'L3_gnn_a_dst_h': _L3_gnn_in['a_dst_h'], 'L3_gnn_b_h': _L3_gnn_in['b_h'], 'L3_gnn_W_out': _L3_gnn_in['W_out'], 'L3_gnn_a_src_out': _L3_gnn_in['a_src_out'], 'L3_gnn_a_dst_out': _L3_gnn_in['a_dst_out'], 'L3_gnn_b_out': _L3_gnn_in['b_out']}

def reference(x, src, dst, edge_attr_16, L0_gnn_W1, L0_gnn_b1, L0_gnn_W2, L0_gnn_b2, L1_gnn_w1l, L1_gnn_b1l, L1_gnn_w1r, L1_gnn_w2l, L1_gnn_b2l, L1_gnn_w2r, L2_gnn_lin_w, L2_gnn_edge_w1, L2_gnn_edge_b1, L2_gnn_edge_w2, L2_gnn_edge_b2, L2_gnn_bias, L2_gnn_ln_w, L2_gnn_ln_b, L3_gnn_W_in, L3_gnn_a_src_in, L3_gnn_a_dst_in, L3_gnn_b_in, L3_gnn_W_h, L3_gnn_a_src_h, L3_gnn_a_dst_h, L3_gnn_b_h, L3_gnn_W_out, L3_gnn_a_src_out, L3_gnn_a_dst_out, L3_gnn_b_out):
    import jax
    import jax.numpy as jnp

    def _L0_gnn_ref(x, edge_index, W1, b1, W2, b2):
        import jax, jax.numpy as jnp
        import numpy as np
        N_NODES = 100000
        N_EDGES = 50000
        IN_DIM, HID_DIM, OUT_DIM = (128, 256, 128)

        def gcn_conv(x, W, b, src, dst, n_nodes):
            xw = x @ W
            ones = jnp.ones(src.shape[0], dtype=xw.dtype)
            deg = jax.ops.segment_sum(ones, dst, num_segments=n_nodes)
            dis = jnp.where(deg > 0, jax.lax.rsqrt(jnp.maximum(deg, 1e-12)), 0.0)
            norm = dis[src] * dis[dst]
            msgs = norm[:, None] * xw[src]
            out = jax.ops.segment_sum(msgs, dst, num_segments=n_nodes)
            return out + b
        n = x.shape[0]
        loop = jnp.arange(n, dtype=edge_index.dtype)
        src = jnp.concatenate([edge_index[0], loop])
        dst = jnp.concatenate([edge_index[1], loop])
        h = gcn_conv(x, W1, b1, src, dst, n)
        h = jax.nn.relu(h)
        out = gcn_conv(h, W2, b2, src, dst, n)
        return out

    def _L1_gnn_ref(x, edge_index, w1l, b1l, w1r, w2l, b2l, w2r):
        import jax, jax.numpy as jnp
        import numpy as np
        N = 100000
        E = 25000
        DIN = 128
        DH = 128

        def sage_conv(x, edge_index, wl, bl, wr):
            row, col = (edge_index[0], edge_index[1])
            num_nodes = x.shape[0]
            agg = jax.ops.segment_sum(x[row], col, num_segments=num_nodes)
            deg = jax.ops.segment_sum(jnp.ones((row.shape[0],), x.dtype), col, num_segments=num_nodes)
            mean = agg / jnp.maximum(deg, 1.0)[:, None]
            return mean @ wl + bl + x @ wr
        h = jax.nn.relu(sage_conv(x, edge_index, w1l, b1l, w1r))
        return jax.nn.relu(sage_conv(h, edge_index, w2l, b2l, w2r))

    def _L2_gnn_ref(x, edge_attr, lin_w, edge_w1, edge_b1, edge_w2, edge_b2, bias, ln_w, ln_b, edge_index):
        import jax, jax.numpy as jnp
        import numpy as np
        N, E, D_IN, D_H, D_E, L = (50000, 12500, 128, 128, 16, 3)
        LN_EPS = 1e-05
        row, col = (edge_index[0], edge_index[1])
        n = x.shape[0]
        deg = jax.ops.segment_sum(jnp.ones(row.shape, x.dtype), col, num_segments=n)
        dis = jnp.where(deg > 0, jax.lax.rsqrt(jnp.maximum(deg, 1e-30)), 0.0)
        w = dis[row] * dis[col]
        h = x
        for l in range(L):
            hx = h @ lin_w[l]
            ea = jax.nn.relu(edge_attr @ edge_w1[l] + edge_b1[l]) @ edge_w2[l] + edge_b2[l]
            msg = hx[row] * w[:, None] + ea
            out = jax.ops.segment_sum(msg, col, num_segments=n) + bias[l]
            mu = out.mean(-1, keepdims=True)
            var = ((out - mu) ** 2).mean(-1, keepdims=True)
            h = jax.nn.relu((out - mu) * jax.lax.rsqrt(var + LN_EPS) * ln_w[l] + ln_b[l])
        return h

    def _L3_gnn_ref(x, edge_index, W_in, a_src_in, a_dst_in, b_in, W_h, a_src_h, a_dst_h, b_h, W_out, a_src_out, a_dst_out, b_out):
        import jax, jax.numpy as jnp
        import numpy as np
        N, E, IN, C, H = (50000, 25000, 128, 64, 2)
        HC = H * C
        NEG_SLOPE = 0.2

        def gat_layer(xf, src, dst, W, a_src, a_dst, b, heads, out_ch):
            n = xf.shape[0]
            h = (xf @ W).reshape(n, heads, out_ch)
            e_src = jnp.einsum('nhc,hc->nh', h, a_src)
            e_dst = jnp.einsum('nhc,hc->nh', h, a_dst)
            e = jax.nn.leaky_relu(e_src[src] + e_dst[dst], NEG_SLOPE)
            m = jax.ops.segment_max(e, dst, num_segments=n)
            p = jnp.exp(e - m[dst])
            s = jax.ops.segment_sum(p, dst, num_segments=n)
            alpha = p / (s[dst] + 1e-16)
            out = jax.ops.segment_sum(alpha[:, :, None] * h[src], dst, num_segments=n)
            return out.reshape(n, heads * out_ch) + b
        loops = jnp.arange(N, dtype=edge_index.dtype)
        src = jnp.concatenate([edge_index[0], loops])
        dst = jnp.concatenate([edge_index[1], loops])
        h = jax.nn.relu(gat_layer(x, src, dst, W_in, a_src_in, a_dst_in, b_in, H, C))
        for i in range(2):
            h = jax.nn.relu(gat_layer(h, src, dst, W_h[i], a_src_h[i], a_dst_h[i], b_h[i], H, C))
        out = gat_layer(h, src, dst, W_out, a_src_out, a_dst_out, b_out, H, C)
        return out
    edge_index = jnp.stack([src, dst])
    h = jnp.maximum(_layernorm(x, axis=-1), 0.0)
    x = x + _L0_gnn_ref(h, edge_index, L0_gnn_W1, L0_gnn_b1, L0_gnn_W2, L0_gnn_b2)
    h = jnp.maximum(_layernorm(x, axis=-1), 0.0)
    x = x + _L1_gnn_ref(h, edge_index, L1_gnn_w1l, L1_gnn_b1l, L1_gnn_w1r, L1_gnn_w2l, L1_gnn_b2l, L1_gnn_w2r)
    h = jnp.maximum(_layernorm(x, axis=-1), 0.0)
    x = x + _L2_gnn_ref(h, edge_attr_16, L2_gnn_lin_w, L2_gnn_edge_w1, L2_gnn_edge_b1, L2_gnn_edge_w2, L2_gnn_edge_b2, L2_gnn_bias, L2_gnn_ln_w, L2_gnn_ln_b, edge_index)
    h = jnp.maximum(_layernorm(x, axis=-1), 0.0)
    x = x + _L3_gnn_ref(h, edge_index, L3_gnn_W_in, L3_gnn_a_src_in, L3_gnn_a_dst_in, L3_gnn_b_in, L3_gnn_W_h, L3_gnn_a_src_h, L3_gnn_a_dst_h, L3_gnn_b_h, L3_gnn_W_out, L3_gnn_a_src_out, L3_gnn_a_dst_out, L3_gnn_b_out)
    return x

_drawn_inputs = setup_inputs


def setup_inputs(seed=0):
    import zlib

    import numpy as np

    out = dict(_drawn_inputs(seed))
    spreads = {'L1_gnn_b1l': (0.0, 0.1),
     'L1_gnn_b2l': (0.0, 0.1),
     'L2_gnn_edge_b1': (0.0, 0.1),
     'L2_gnn_edge_b2': (0.0, 0.1),
     'L2_gnn_bias': (0.0, 0.1),
     'L2_gnn_ln_w': (1.0, 0.2),
     'L2_gnn_ln_b': (0.0, 0.1),
     'L3_gnn_b_in': (0.0, 0.38),
     'L3_gnn_b_h': (0.0, 0.1),
     'L3_gnn_b_out': (0.0, 0.1)}
    factors = {'L0_gnn_b1': 3.622,
     'L3_gnn_a_src_in': 36.0,
     'L3_gnn_a_dst_in': 200.0,
     'L3_gnn_a_src_h': 50.064,
     'L3_gnn_a_dst_h': 200.0,
     'L3_gnn_a_src_out': 181.034,
     'L3_gnn_a_dst_out': 200.0}
    for name, (base, spread) in spreads.items():
        noise = np.random.default_rng([zlib.crc32(name.encode()), seed]).standard_normal(out[name].shape)
        drawn = base * np.exp(spread * noise) if base else spread * noise
        out[name] = jnp.asarray(drawn.astype(out[name].dtype))
    for name, factor in factors.items():
        out[name] = (out[name] * factor).astype(out[name].dtype)
    return out
```

```python
import concourse.bass as bass
from concourse import mybir
from contextlib import ExitStack

P = 128
N = 50000
E = 25000
D = 128
ED = 16
T = -(-E // P)
EP = T * P
QUADS = T // 4
QR = 4 * P
HALF = T // 2
NROW = EP + N
GW = D + 2
BIG = 1.0e30
FAR = 1.0e6
LN_EPS = 1e-5
PLAIN_QUADS = -(-N // QR)
PLAIN_TURNS = PLAIN_QUADS // 2

KINDS = ["X", "C1", "C2", "S1", "S2", "LA", "LA", "LB", "GA", "GA", "GA", "GZ"]


class Steps:

    def __init__(self, sem, order, by=1, start=0, stages=KINDS, turns=QUADS):
        self.sem, self.order, self.by, self.start, self.stages, self.turns = sem, order, by, start, stages, turns

    def at(self, stage, turn, step=None):
        names = self.order.get(self.stages[stage], ())
        before = self.turns * sum(len(self.order.get(k, ())) for k in self.stages[:stage])
        k = 0 if step is None else names.index(step) + 1
        return turn * (self.by * len(names)) + (self.start + self.by * (before + k))

    def last(self, stage, turn, step):
        return self.at(stage, turn, step) - self.by * len(self.order[self.stages[stage]])


def gnn_program(nc, a, out):
    f32, i32 = mybir.dt.float32, mybir.dt.int32
    ALU, ACT, AX = mybir.AluOpType, mybir.ActivationFunctionType, mybir.AxisListType
    ds = bass.ds
    ctx = ExitStack()
    with ctx:
        def sb(name, shape, dt=f32):
            return ctx.enter_context(nc.sbuf_tensor(name, shape, dt))

        def sem(name):
            return ctx.enter_context(nc.semaphore(name))

        def dram(name, shape, dt=f32):
            return nc.dram_tensor(name, shape, dt, kind="Internal").ap()

        TAB = {s: dram(f"table{s}", (NROW, D)) for s in (1, 2, 3, 4)}
        TAB.update({s: dram(f"table{s}", (EP, D)) for s in (5, 6, 7)})
        TAB.update({s: dram(f"table{s}", (NROW, GW)) for s in (8, 9, 10, 11)})
        XR = {s: dram(f"xrows{s}", (EP, D)) for s in (0, 2, 4, 7)}
        SELF = dram("sage_self", (EP, D))
        NODE = dram("node_info", (N, 2))
        EAT = dram("edge_attr_t", (ED, EP))

        ident = sb("ident", [P, P])
        iota_row = sb("iota_row", [P, P])
        eps = sb("eps", [P, 1])
        ones_row = sb("ones_row", [1, P])
        w1 = sb("w1", [P, 256])
        w2 = sb("w2", [P, 2, D])
        b1 = sb("b1", [P, 2])
        w1l, w1r, w2l, w2r = (sb(n, [P, D]) for n in ("w1l", "w1r", "w2l", "w2r"))
        b1l = sb("b1l", [P, 1])
        linw = sb("linw", [P, 3, D])
        ew1 = sb("ew1", [ED, 3, D])
        ew2 = sb("ew2", [P, 3, D])
        eb1 = sb("eb1", [P, 3])
        eb2 = sb("eb2", [1, 3, 4, D])
        lnw_c = sb("lnw_c", [P, 3])
        lnb_c = sb("lnb_c", [P, 3])
        WX = sb("WX", [P, 4, GW + 2])
        gb_c = sb("gb_c", [P, 4])
        b2_r, b2l_r, lnw_r, lnb_r, gout_r, c2_r = (
            sb(n, [P, D]) for n in ("b2_r", "b2l_r", "lnw_r", "lnb_r", "gout_r", "c2_r"))
        bias_r = sb("bias_r", [P, 3, D])

        rel, deg, wgcn, winv, wl2, dis2, te1, te2, te3, te4 = (
            sb(n, [P, T]) for n in ("rel", "deg", "wgcn", "winv", "wl2", "dis2", "te1", "te2", "te3", "te4"))
        idx_all, idx_l2, idx_dst, idx_x, idx_src = (
            sb(n, [P, T], i32) for n in ("idx_all", "idx_l2", "idx_dst", "idx_x", "idx_src"))
        node_val = sb("node_val", [P, T, 2])
        node_src = sb("node_src", [P, T, 2])
        relL = sb("relL", [1, T])
        cont = sb("cont", [1, T])

        A4 = sb("A4", [HALF, 4, 2, P])
        FI4 = sb("FI4", [HALF, 4, 2, P])
        CM = sb("CM", [HALF, 2, P])
        LMB = sb("LMB", [HALF, 2, P])
        R2 = sb("R2", [HALF, 2, 2, P])
        V = sb("V", [HALF, 6, 2, P])
        W4 = sb("W4", [HALF, 4, 2, P])
        HS = sb("HS", [HALF, 4, 2, P])
        ends = sb("ends", [HALF, 2, 12])
        rfa = sb("rfa", [4, T])
        rb = sb("rb", [2, T])
        crow = sb("crow", [4, T + 1])
        brow = sb("brow", [2, T + 1])
        cb = sb("cb", [HALF, 2, 4])

        G = sb("G", [P, T, GW])
        NV = sb("NV", [P, 4, T])
        ES = sb("ES", [P, 2, T])
        PT = sb("PT", [P, 4, T])

        M = sb("M", [P, 4, GW])
        idx_slot = sb("idx_slot", [P, 4], i32)
        node_slot = sb("node_slot", [P, 4, 2])
        MP = sb("MP", [P, 4, GW])
        S = sb("S", [P, 4, P])
        LO = sb("LO", [1, 4, P])
        C = sb("C", [1, GW])
        OWN = sb("OWN", [P, 4, GW])
        XIN = sb("XIN", [P, 4, D])
        U = sb("U", [P, 4, D])
        GN = sb("GN", [P, 4, D])
        UT = sb("UT", [P, QR])
        OT = sb("OT", [P, QR])
        H1T = sb("H1T", [P, 2, QR])
        RO = sb("RO", [P, 4, GW])
        RB = sb("RB", [P, 4, D])
        stat = sb("stat", [P, 4, 6])
        mv = sb("mv", [P, 4, 2])
        sd, rs, nb = (sb(n, [P, 4]) for n in ("sd", "rs", "nb"))
        den = sb("den", [P, 4, 2])
        ea_in = sb("ea_in", [P, 4, ED])
        ea_last = sb("ea_last", [P, 4, ED])
        eat = sb("eat", [ED, QR])

        Gf = G[:, :, :].rearrange("p t c -> p (t c)")

        def lend(at, *shape):
            size = 1
            for n in shape:
                size *= n
            v = Gf[:, at:at + size]
            return v if len(shape) == 1 else v.rearrange("p (x y) -> p x y", x=shape[0])

        ROOM = 6144
        PXT = [lend(b * ROOM, 4, D) for b in (0, 1)]
        PGN = [lend(b * ROOM + 512, 4, D) for b in (0, 1)]
        PTT = [lend(b * ROOM + 1024, QR) for b in (0, 1)]
        PHT = [lend(b * ROOM + 1536, 2, QR) for b in (0, 1)]
        PRO = [[lend(b * ROOM + 2560 + r * 520, 4, GW) for r in (0, 1)] for b in (0, 1)]
        PYT = [lend(b * ROOM + 3600, 4, D) for b in (0, 1)]
        PST = [lend(b * ROOM + 4112, 4, 6) for b in (0, 1)]
        PMV = [lend(b * ROOM + 4136, 4, 2) for b in (0, 1)]
        PSD = [lend(b * ROOM + 4144, 4) for b in (0, 1)]
        PRS = [lend(b * ROOM + 4148, 4) for b in (0, 1)]
        PNB = [lend(b * ROOM + 4152, 4) for b in (0, 1)]
        av = [lend(2 * ROOM + v * D, D) for v in range(8)]
        avt = lend(2 * ROOM + 8 * D, D)
        FILL = lend(2 * ROOM + 9 * D, 1000)
        raw2 = lend(2 * ROOM + 3000, 2, P + 2)[0:HALF].bitcast(i32)
        srcraw = lend(2 * ROOM + 4000, 2, P)[0:HALF].bitcast(i32)
        x2f = lend(2 * ROOM + 5000, 2, P + 2)[0:HALF]

        PS = ctx.enter_context(nc.psum_tensor("PS", [P, 8, 512], f32))

        def bank(b, w=D, k=4):
            return PS[:, b, 0:k * w].rearrange("p (j c) -> p j c", j=k)

        def pair(b, w=GW):
            return PS[:, b:b + 2, :].rearrange("p b (j c) -> p (b j) c", j=2)[:, :, 0:w]

        def wide(v, n):
            return v.unsqueeze(2).to_broadcast([v.shape[0], v.shape[1], n])

        def on4(v):
            return v.unsqueeze(1).to_broadcast([P, 4, D])

        c_load = sem("c_load")
        c_pool = sem("c_pool")
        p_set = sem("p_set")
        p_raw = sem("p_raw")
        p_fill = sem("p_fill")
        p_dve = sem("p_dve")
        p_v = sem("p_v")
        p_p = sem("p_p")
        p_va = sem("p_va")
        p_a = sem("p_a")
        p_ready = sem("p_ready")
        e_ld = sem("e_ld")
        e_tr = sem("e_tr")
        e_cp = sem("e_cp")
        e_st = sem("e_st")
        n_idx = sem("n_idx")
        n_val = sem("n_val")
        n_sc = [sem(f"n_sc{j}") for j in range(4)]
        n_g = [sem(f"n_g{j}") for j in range(4)]
        n_cp = sem("n_cp")

        def psteps(name, order, by=1):
            return [Steps(sem(f"{name}{b}"), {"P": order}, by, 0, ["P"], PLAIN_TURNS) for b in (0, 1)]

        q_ld = psteps("q_ld", ("x",), 16)
        q_v = psteps("q_v", ("stats1", "aggr1", "rs1", "nb1", "h1b", "xb", "x1", "stats2", "aggr2", "rs2", "nb2",
                             "y", "yx", "x3", "stats3", "aggr3", "rs3", "nb3", "r8", "r9", "r10", "r11", "xo", "xf"))
        q_p = psteps("q_p", ("gT1", "h1a", "h1b", "t1", "gT2", "h2", "rA", "rB", "gT3", "h8", "r8", "h9", "r9",
                             "h10", "r10", "r11"))
        q_a = psteps("q_a", ("sd1", "g1", "gT1", "h1a", "t1", "sd2", "g2", "gT2", "h2", "rA", "sd3", "g3", "gT3",
                             "h8", "h9", "h10"))
        q_st = {t: psteps(f"q_st{t}_", (t,), 16) for t in ("t1", "t2", "t3", "t4", "t8", "t9", "t10", "t11", "out")}

        AGG = ("C1", "C2", "S1", "S2", "LA", "LB", "GA", "GZ")
        four = ("t3", "t2", "t1", "t0")

        def steps(name, order, by=1, start=0):
            return Steps(sem(name), order, by, start)

        idxed = steps("idxed", {k: ("slots",) for k in KINDS})
        gat = [steps(f"gat{j}", {k: ("rows",) for k in KINDS}, 16) for j in range(4)]
        m_free = steps("m_free", {k: four for k in ("C1", "C2", "S1", "S2", "GA", "GZ")}, 1, 4)
        sel = steps("sel", {k: four for k in AGG})
        agg = steps("agg", {k: four for k in AGG}, 1, 4)
        carry = steps("carry", {k: four for k in AGG})
        mprod = steps("mprod", {"LA": four, "LB": four, "GA": ("quad",), "GZ": ("quad",)}, 1, 4)
        own = steps("own", {k: ("rows",) for k in ("C1", "C2", "S1", "S2", "GA", "GZ")}, 16)
        xin = steps("xin", {k: ("rows",) for k in ("C2", "S2", "LB", "GZ")}, 16)
        eas = steps("eas", {k: ("attr",) for k in ("LA", "LB")}, 16)
        st_t = steps("st_t", {k: ("table",) for k in KINDS if k != "GZ"}, 16)
        st_x = steps("st_x", {k: ("rows",) for k in ("X", "C2", "S1", "S2", "LB")}, 16)
        st_o = [steps(f"st_o{j}", {"GZ": ("rows",)}, 16) for j in range(4)]
        vd = steps("vd", {
            "X": ("copy", "stats", "aggr", "rs", "nb"),
            "C1": ("own", "comb", "h1b"),
            "C2": ("own", "comb", "bias", "x", "stats", "aggr", "rs", "nb"),
            "S1": ("comb",),
            "S2": ("comb", "bias", "x", "stats", "aggr", "rs", "nb"),
            "LA": ("comb", "stats", "aggr", "rs", "nb"),
            "LB": ("comb", "stats", "aggr", "rs", "nb", "lnw", "lnb", "x", "stats2", "aggr2", "rs2", "nb2"),
            "GA": ("den", "dene", "rden", "comb", "norm"),
            "GZ": ("den", "dene", "rden", "comb", "norm", "bias", "x")})
        pd = steps("pd", {
            "C1": ("uT", "h1a", "h1b", "rows"), "S1": ("uT", "oT", "hT", "rA", "rB"), "S2": ("gT", "rows"),
            "LA": ("rT", "em", "nT", "rows"), "LB": ("rT", "em", "gT", "rows"), "GA": ("uT", "rows")})
        ad = steps("ad", {
            "X": ("sd", "g"), "C1": ("uT", "h1a", "rows"), "C2": ("sd", "g"),
            "S1": ("uT", "oT", "hT", "rA", "rB"), "S2": ("sd", "g", "gT", "rows"),
            "LA": ("rT", "sd", "n", "nT", "rows"), "LB": ("rT", "sd", "n", "sd2", "g", "gT", "rows", "nv"),
            "GA": ("uT", "rows", "nv")})
        hself = steps("hself", {"GA": ("own",), "GZ": ("own",)})
        m_p = Steps(sem("m_p"), {"mid": ("scan", "rowmax", "getmax", "rowown", "getown", "tile")}, 1, 0, ["mid"], 0)
        m_v = Steps(sem("m_v"), {"mid": ("es", "max", "maxes", "own", "owns", "power", "weights")}, 1, 0, ["mid"], 0)
        m_a = Steps(sem("m_a"), {"mid": ("exp",)}, 1, 0, ["mid"], 0)
        m_idx = sem("m_idx")
        ATTENTION = [s for s, k in enumerate(KINDS) if k in ("GA", "GZ")]

        OWN_SRC = {1: TAB[1], 2: TAB[2], 3: TAB[3], 4: SELF, 8: TAB[8], 9: TAB[9], 10: TAB[10], 11: TAB[11]}
        X_SRC = {2: XR[0], 4: XR[2], 7: XR[4], 11: XR[7]}
        X_DST = {0: XR[0], 2: XR[2], 3: SELF, 4: XR[4], 7: XR[7]}
        STAGES = list(enumerate(KINDS))
        LAST = QUADS - 1

        def quad_rows(t, Q):
            return t[ds(Q * QR, QR), :].rearrange("(j p) c -> p j c", p=P)

        def plain_rows(t, base):
            return t[ds(base, QR), :].rearrange("(p j) c -> p j c", j=4)

        def stage_stored(eng, s):
            for st in (st_t, st_x):
                if KINDS[s] in st.order:
                    eng.wait_ge(st.sem, st.at(s, LAST, st.order[KINDS[s]][-1]))

        def alone(eng, *waits):
            for _, value in waits:
                eng.compute_val(value)
            eng.wait_ge(c_pool, 13)
            for sm, value in waits:
                eng.wait_ge(sm, value)

        loads = [(w1[:, :], a["L0_gnn_W1"]), (w2[:, :, :], a["L0_gnn_W2"].rearrange("(b p) c -> p b c", p=P)),
                 (b1[:, :], a["L0_gnn_b1"].rearrange("(b p) -> p b", p=P)),
                 (w1l[:, :], a["L1_gnn_w1l"]), (w1r[:, :], a["L1_gnn_w1r"]),
                 (w2l[:, :], a["L1_gnn_w2l"]), (w2r[:, :], a["L1_gnn_w2r"]),
                 (b1l[:, :], a["L1_gnn_b1l"].rearrange("(p o) -> p o", o=1)),
                 (linw[:, :, :], a["L2_gnn_lin_w"].rearrange("l p c -> p l c")),
                 (ew1[:, :, :], a["L2_gnn_edge_w1"].rearrange("l p c -> p l c")),
                 (ew2[:, :, :], a["L2_gnn_edge_w2"].rearrange("l p c -> p l c")),
                 (eb1[:, :], a["L2_gnn_edge_b1"].rearrange("l p -> p l")),
                 (lnw_c[:, :], a["L2_gnn_ln_w"].rearrange("l p -> p l")),
                 (lnb_c[:, :], a["L2_gnn_ln_b"].rearrange("l p -> p l")),
                 (WX[:, 0, 0:D], a["L3_gnn_W_in"]), (WX[:, 1, 0:D], a["L3_gnn_W_h"][0]),
                 (WX[:, 2, 0:D], a["L3_gnn_W_h"][1]), (WX[:, 3, 0:D], a["L3_gnn_W_out"]),
                 (gb_c[:, 0:1], a["L3_gnn_b_in"].rearrange("(p o) -> p o", o=1)),
                 (gb_c[:, 1:3], a["L3_gnn_b_h"].rearrange("l p -> p l")),
                 (b2_r[:, :], a["L0_gnn_b2"].partition_broadcast(P)),
                 (b2l_r[:, :], a["L1_gnn_b2l"].partition_broadcast(P)),
                 (lnw_r[:, :], a["L2_gnn_ln_w"][2].partition_broadcast(P)),
                 (lnb_r[:, :], a["L2_gnn_ln_b"][2].partition_broadcast(P)),
                 (gout_r[:, :], a["L3_gnn_b_out"].partition_broadcast(P))]
        loads += [(bias_r[:, l, :], a["L2_gnn_bias"][l].partition_broadcast(P)) for l in range(3)]
        loads += [(eb2[0:1, l, j, :], a["L2_gnn_edge_b2"][l:l + 1, :]) for l in range(3) for j in range(4)]
        attn = [a["L3_gnn_a_src_in"], a["L3_gnn_a_dst_in"], a["L3_gnn_a_src_h"][0], a["L3_gnn_a_dst_h"][0],
                a["L3_gnn_a_src_h"][1], a["L3_gnn_a_dst_h"][1], a["L3_gnn_a_src_out"], a["L3_gnn_a_dst_out"]]
        loads += [(av[v], attn[v].rearrange("h c -> (h c)").partition_broadcast(P)) for v in range(8)]
        LOADED = 16 * len(loads)

        x, src, dst, ea = a["x"], a["src"], a["dst"], a["edge_attr_16"]
        BLOCK1 = HALF * P
        TAIL = (T - 1) * P

        def span(t, start, rows, step, cols):
            return bass.AP(tensor=t.tensor, offset=start, ap=[[step, rows], [1, cols]])


        def attention_middle(dve, v, link, s):
            mid = ATTENTION.index(s)

            def flat(t):
                return t.rearrange("q k b p -> q (k b p)")

            def leaky(t):
                link(v.scalar_tensor_tensor(t, t, 0.2, t, ALU.mult, ALU.max))

            dve.wait_ge(m_free.sem, m_free.at(s, LAST, "t0"))
            v.tensor_copy(ES[:, :, :], G[:, :, D:GW].rearrange("p t h -> p h t")).then_inc(m_v.sem, 1)
            dve.wait_ge(m_p.sem, m_p.at(0, mid, "scan"))
            link(v.tensor_copy(V[:, :, :, :].rearrange("q k b p -> q (k b p)"),
                               PS[0:HALF, 4:7, :].rearrange("q x c -> q (x c)")))
            v.tensor_tensor_scan(flat(HS[:, 0:2])[:, ::-1], flat(R2[:, :])[:, ::-1], flat(V[:, 0:2])[:, ::-1], -BIG,
                                 ALU.add, ALU.max).then_inc(m_v.sem, 1)
            dve.wait_ge(m_p.sem, m_p.at(0, mid, "rowmax"))
            v.tensor_tensor_scan(brow[:, 0:T][:, ::-1], rb[:, :][:, ::-1], PS[0:2, 7, 0:T][:, ::-1], -BIG,
                                 ALU.add, ALU.max).then_inc(m_v.sem, 1)
            dve.wait_ge(m_p.sem, m_p.at(0, mid, "getmax"))
            for b in (0, 1):
                link(v.tensor_copy(cb[:, b, 0:2], PS[0:HALF, 4, 4 * b:4 * b + 2]))
            for k in (0, 1):
                for b in (0, 1):
                    i = v.scalar_tensor_tensor(HS[:, k, b], LMB[:, b, :], cb[:, b, k:k + 1], HS[:, k, b],
                                               ALU.add, ALU.max)
            link(i)
            top, own_ = W4[:, 0:2], V[:, 2:4]
            link(v.tensor_tensor(top, HS[:, 0:2], own_, ALU.max))
            v.tensor_copy(W4[:, 2:4], V[:, 4:6])
            link(v.tensor_tensor(top, top, V[:, 4:6], ALU.add))
            leaky(flat(top))
            link(v.tensor_tensor(own_, own_, V[:, 4:6], ALU.add))
            leaky(flat(own_))
            link(v.tensor_tensor(own_, own_, top, ALU.subtract))
            link(v.tensor_tensor(flat(W4[:, :]), flat(W4[:, :]), flat(FI4[:, :]), ALU.mult))
            v.tensor_tensor_scan(flat(HS[:, :]), flat(A4[:, :]), flat(W4[:, :]), 0.0, ALU.mult,
                                 ALU.add).then_inc(m_v.sem, 1)
            dve.wait_ge(m_p.sem, m_p.at(0, mid, "rowown"))
            v.tensor_tensor_scan(crow[:, 1:T + 1], rfa[:, :], PS[0:4, 7, 0:T], 0.0, ALU.mult,
                                 ALU.add).then_inc(m_v.sem, 1)
            dve.wait_ge(m_p.sem, m_p.at(0, mid, "getown"))
            for b in (0, 1):
                link(v.tensor_copy(cb[:, b, :], PS[0:HALF, 4, 4 * b:4 * b + 4]))
            for k in range(4):
                for b in (0, 1):
                    i = v.scalar_tensor_tensor(HS[:, k, b], CM[:, b, :], cb[:, b, k:k + 1], HS[:, k, b],
                                               ALU.mult, ALU.add)
            link(i)
            es = V[:, 0:2]
            link(v.tensor_tensor(es, es, HS[:, 2:4], ALU.add))
            leaky(flat(es))
            v.tensor_tensor(es, es, HS[:, 0:2], ALU.subtract).then_inc(m_v.sem, 1)
            dve.wait_ge(m_p.sem, m_p.at(0, mid, "tile"))
            v.tensor_copy(PT[:, 0:2, :].rearrange("p k t -> p (k t)"), PS[:, 4, 0:2 * T])
            v.tensor_copy(PT[:, 2:4, :].rearrange("p k t -> p (k t)"), PS[:, 5, 0:2 * T]).then_inc(m_v.sem, 1)

        def attention_turns(pe, turn, s):
            mid = ATTENTION.index(s)
            pe.wait_ge(m_v.sem, m_v.at(0, mid, "es"))
            for k in range(6):
                for b in (0, 1):
                    c = 2 * k + b
                    row = (ES[:, k, :] if k < 2 else NV[:, k - 2, :])[:, HALF * b:HALF * b + HALF]
                    i = turn(PS[0:HALF, 4 + c // 4, P * (c % 4):P * (c % 4) + P], row)
            i.then_inc(m_p.sem, 1)
            pe.wait_ge(m_v.sem, m_v.at(0, mid, "max"))
            for b in (0, 1):
                i = turn(PS[0:2, 7, HALF * b:HALF * b + HALF], HS[:, 0:2, b, 0])
            i.then_inc(m_p.sem, 1)
            pe.wait_ge(m_v.sem, m_v.at(0, mid, "maxes"))
            for b in (0, 1):
                i = turn(PS[0:HALF, 4, 4 * b:4 * b + 2], brow[:, HALF * b + 1:HALF * b + HALF + 1])
            i.then_inc(m_p.sem, 1)
            pe.wait_ge(m_v.sem, m_v.at(0, mid, "own"))
            for b in (0, 1):
                i = turn(PS[0:4, 7, HALF * b:HALF * b + HALF], HS[:, :, b, P - 1])
            i.then_inc(m_p.sem, 1)
            pe.wait_ge(m_v.sem, m_v.at(0, mid, "owns"))
            for b in (0, 1):
                i = turn(PS[0:HALF, 4, 4 * b:4 * b + 4], crow[:, HALF * b:HALF * b + HALF])
            i.then_inc(m_p.sem, 1)
            pe.wait_ge(m_a.sem, m_a.at(0, mid, "exp"))
            for k in range(4):
                for b in (0, 1):
                    at = T * (k % 2) + HALF * b
                    i = turn(PS[:, 4 + k // 2, at:at + HALF], W4[:, k, b])
            i.then_inc(m_p.sem, 1)
            pe.wait_ge(m_v.sem, m_v.at(0, mid, "weights"))

        def attention_exp(act, f, s):
            mid = ATTENTION.index(s)
            act.wait_ge(m_v.sem, m_v.at(0, mid, "power"))
            f(W4[:, :, :, :].rearrange("q k b p -> q (k b p)"), V[:, 0:4].rearrange("q k b p -> q (k b p)"),
              ACT.Exp).then_inc(m_a.sem, 1)

        block = ctx.enter_context(nc.Block())

        @block.sync
        def _(sp):
            for o, i in loads:
                sp.dma_start(o, i, allow_slow_non_contiguous=True).then_inc(c_load, 16)
            sp.wait_ge(p_set, 3)
            sp.dma_start(raw2[0:1, 0, 1:P + 2], span(dst, 0, 1, 1, P + 1)).then_inc(p_raw, 16)
            sp.dma_start(raw2[1:HALF, 0, :], span(dst, P - 1, HALF - 1, P, P + 2)).then_inc(p_raw, 16)
            sp.dma_start(raw2[0:HALF - 1, 1, :], span(dst, BLOCK1 - 1, HALF - 1, P, P + 2)).then_inc(p_raw, 16)
            sp.dma_start(raw2[HALF - 1:HALF, 1, 0:E - TAIL + 1],
                         span(dst, TAIL - 1, 1, 1, E - TAIL + 1)).then_inc(p_raw, 16)
            sp.dma_start(srcraw[:, 0, :], span(src, 0, HALF, P, P)).then_inc(p_raw, 16)
            sp.dma_start(srcraw[0:HALF - 1, 1, :], span(src, BLOCK1, HALF - 1, P, P)).then_inc(p_raw, 16)
            sp.dma_start(srcraw[HALF - 1:HALF, 1, 0:E - TAIL], span(src, TAIL, 1, 1, E - TAIL)).then_inc(p_raw, 16)
            sp.wait_ge(c_pool, 11)
            sp.dma_start(NODE.rearrange("(p a) c -> p (a c)", p=100), FILL[0:100, :]).then_inc(p_fill, 16)

            with sp.Fori(0, LAST) as n:
                sp.wait_ge(e_tr, n)
                sp.dma_start(ea_in[:, :, :], ea[ds(n * QR, QR), :].rearrange("(p j) c -> p j c", j=4)).then_inc(e_ld, 16)
                alone(sp, (e_cp, n + 1))
                sp.dma_start(EAT[:, ds(n * QR, QR)], eat[:, :]).then_inc(e_st, 16)
            sp.dma_start(ea_last[0:(E - LAST * QR) // 4, :, :],
                         ea[LAST * QR:E, :].rearrange("(p j) c -> p j c", j=4)).then_inc(e_ld, 16)
            sp.wait_ge(e_cp, QUADS)
            sp.dma_start(EAT[:, LAST * QR:EP], eat[:, :]).then_inc(e_st, 16)
            sp.wait_ge(e_st, 16 * QUADS)

            def plain(m, bases):
                for b in (0, 1):
                    alone(sp, (q_v[b].sem, q_v[b].at(0, m)), (q_st["out"][b].sem, q_st["out"][b].at(0, m)))
                    sp.dma_start(PXT[b], plain_rows(x, bases[b])).then_inc(q_ld[b].sem, 16)

                def keep(name, tab, b, ready, rows, shift=EP):
                    sp.wait_ge(*ready)
                    if b and isinstance(m, int):
                        sp.wait_ge(q_st[name][0].sem, q_st[name][0].at(0, m, name))
                    sp.dma_start(plain_rows(tab, bases[b] + shift), rows).then_inc(q_st[name][b].sem, 16)

                for b in (0, 1):
                    keep("t1", TAB[1], b, (q_a[b].sem, q_a[b].at(0, m, "g1")), PGN[b])
                for b in (0, 1):
                    keep("t2", TAB[2], b, (q_a[b].sem, q_a[b].at(0, m, "t1")), PRO[b][0][:, :, 0:D])
                for b in (0, 1):
                    keep("t3", TAB[3], b, (q_a[b].sem, q_a[b].at(0, m, "g2")), PGN[b])
                for b in (0, 1):
                    keep("t4", TAB[4], b, (q_a[b].sem, q_a[b].at(0, m, "rA")), PRO[b][1][:, :, 0:D])
                for t, r in ((8, 0), (9, 1), (10, 0), (11, 1)):
                    for b in (0, 1):
                        keep(f"t{t}", TAB[t], b, (q_v[b].sem, q_v[b].at(0, m, f"r{t}")), PRO[b][r])
                for b in (0, 1):
                    keep("out", out, b, (q_v[b].sem, q_v[b].at(0, m, "xf")), PXT[b], 0)

            with sp.Fori(0, PLAIN_TURNS - 1) as m:
                plain(m, (m * (2 * QR), m * (2 * QR) + QR))
            for t in q_st.values():
                for b in (0, 1):
                    sp.wait_ge(t[b].sem, 16 * (PLAIN_TURNS - 1))
            plain(PLAIN_TURNS - 1, ((PLAIN_QUADS - 2) * QR, N - QR))

            for s, kind in STAGES:
                if s:
                    stage_stored(sp, s - 1)

                def load(n):
                    Q = LAST - n if isinstance(n, int) else n * (-1) + LAST
                    if kind in own.order:
                        used, step = {"C1": (vd, "own"), "C2": (vd, "own"), "S1": (pd, "oT"), "S2": (vd, "comb"),
                                      "GA": (hself, "own"), "GZ": (hself, "own")}[kind]
                        sp.wait_ge(used.sem, used.at(s, n) if kind in hself.order or isinstance(n, int)
                                   else used.last(s, n, step))
                        w = GW if kind in hself.order else D
                        sp.dma_start(OWN[:, :, 0:w], quad_rows(OWN_SRC[s], Q)).then_inc(own.sem, 16)
                    if kind in xin.order:
                        sp.wait_ge(vd.sem, vd.at(s, n) if isinstance(n, int) else vd.last(s, n, "x"))
                        sp.dma_start(XIN[:, :, :], quad_rows(X_SRC[s], Q)).then_inc(xin.sem, 16)
                    if kind in eas.order:
                        alone(sp, (pd.sem, pd.at(s, n) if isinstance(n, int) else pd.last(s, n, "rT")))
                        sp.dma_start(eat[:, :], EAT[:, ds(Q * QR, QR)]).then_inc(eas.sem, 16)

                def store(n):
                    Q = LAST - n if isinstance(n, int) else n * (-1) + LAST
                    xstep = {"X": "copy", "C2": "x", "S2": "x", "LB": "x"}.get(kind)
                    if xstep:
                        sp.wait_ge(vd.sem, vd.at(s, n, xstep))
                        sp.dma_start(quad_rows(X_DST[s], Q), U[:, :, :]).then_inc(st_x.sem, 16)
                    if kind == "S1":
                        sp.wait_ge(ad.sem, ad.at(s, n, "rB"))
                        sp.dma_start(quad_rows(X_DST[s], Q), RB[:, :, :]).then_inc(st_x.sem, 16)
                    astep, rows = {"X": ("g", GN[:, :, :]), "C2": ("g", GN[:, :, :]), "C1": ("rows", RO[:, :, 0:D]),
                                   "S1": ("rA", RO[:, :, 0:D]), "S2": ("rows", RO[:, :, 0:D]),
                                   "LA": ("rows", RO[:, :, 0:D]), "LB": ("rows", RO[:, :, :]),
                                   "GA": ("rows", RO[:, :, :])}[kind]
                    sp.wait_ge(ad.sem, ad.at(s, n, astep))
                    sp.dma_start(quad_rows(TAB[s + 1], Q), rows).then_inc(st_t.sem, 16)

                if kind == "X":
                    with sp.Fori(0, QUADS) as n:
                        store(n)
                elif kind == "GZ":
                    with sp.Fori(0, QUADS) as n:
                        load(n)
                else:
                    load(0)
                    with sp.Fori(0, LAST) as n:
                        load(n + 1)
                        store(n)
                    store(LAST)

        @block.gpsimd
        def _(pool):
            g = nc.gpsimd
            g.memset(ident[:, :], 0.0).then_inc(c_pool, 1)
            g.iota(iota_row[:, :], [[1, P]], base=0, channel_multiplier=0,
                   allow_small_or_imprecise_dtypes=True).then_inc(c_pool, 1)
            g.memset(eps[:, :], LN_EPS).then_inc(c_pool, 1)
            g.memset(ones_row[:, :], 1.0).then_inc(c_pool, 1)
            pool.wait_ge(c_pool, 4)
            g.affine_select(out=ident[:, :], in_=ident[:, :], compare_op=ALU.not_equal, fill=1.0, base=0,
                            pattern=[[-1, P]], channel_multiplier=1).then_inc(c_pool, 1)
            g.memset(raw2[:, :, :], 60000).then_inc(p_set, 1)
            g.memset(srcraw[:, :, :], 0).then_inc(p_set, 1)
            pool.wait_ge(p_set, 2)
            g.memset(raw2[:, 1, P + 1:P + 2], 70000).then_inc(p_set, 1)
            g.iota(W4[:, 0, :, :], [[BLOCK1, 2], [1, P]], base=0, channel_multiplier=P,
                   allow_small_or_imprecise_dtypes=True).then_inc(c_pool, 1)
            g.iota(W4[:, 1, :, :], [[BLOCK1, 2], [0, P]], base=0, channel_multiplier=P,
                   allow_small_or_imprecise_dtypes=True).then_inc(c_pool, 1)
            g.iota(te1[:, :], [[P, T]], base=0, channel_multiplier=1,
                   allow_small_or_imprecise_dtypes=True).then_inc(c_pool, 1)
            g.memset(ea_last[:, :, :], 0.0).then_inc(c_pool, 1)
            fill2 = FILL[0:100, :].rearrange("p (a c) -> p a c", c=2)
            g.memset(fill2[:, :, 0:1], -1.0).then_inc(c_pool, 1)
            g.memset(fill2[:, :, 1:2], 0.0).then_inc(c_pool, 1)
            g.memset(crow[:, :], 0.0).then_inc(c_pool, 1)
            g.memset(brow[:, :], -BIG).then_inc(c_pool, 1)
            g.memset(C[:, :], 0.0).then_inc(m_free.sem, 4)
            g.memset(M[:, :, :], 0.0).then_inc(agg.sem, 4)
            g.memset(den[:, :, :], 0.0).then_inc(mprod.sem, 4)

            pool.wait_ge(p_ready, 1)
            pool.wait_ge(p_fill, 16)
            with pool.Fori(0, QUADS) as n:
                for j in range(4):
                    pool.wait_ge(n_sc[j], n * 16)
                g.tensor_copy(idx_slot[:, :], idx_dst[:, ds(n * 4, 4)]).then_inc(n_idx, 1)
                g.tensor_copy(node_slot[:, :, :], node_val[:, ds(n * 4, 4), :]).then_inc(n_val, 1)
                alone(pool, (n_idx, n + 1), (n_val, n + 1))
                for j in range(4):
                    g.indirect_dma_start(NODE, bass.IndirectOffsetOnAxis(ap=idx_slot[:, j:j + 1], axis=0),
                                         node_slot[:, j, :], None, bounds_check=N - 1,
                                         oob_is_err=False).then_inc(n_sc[j], 16)
            for j in range(4):
                pool.wait_ge(n_sc[j], 16 * QUADS)
            with pool.Fori(0, QUADS) as n:
                g.tensor_copy(idx_slot[:, :], idx_src[:, ds(n * 4, 4)]).then_inc(n_idx, 1)
                alone(pool, (n_idx, n + (QUADS + 1)))
                for j in range(4):
                    g.indirect_dma_start(node_slot[:, j, :], None, NODE,
                                         bass.IndirectOffsetOnAxis(ap=idx_slot[:, j:j + 1], axis=0)).then_inc(n_g[j], 16)
                for j in range(4):
                    pool.wait_ge(n_g[j], n * 16 + 16)
                g.tensor_copy(node_src[:, ds(n * 4, 4), :], node_slot[:, :, :]).then_inc(n_cp, 1)
                pool.wait_ge(n_cp, n + 1)

            def gathers(s, table, idx, w):
                with pool.Fori(0, QUADS) as n:
                    Q4 = n * (-4) + 4 * LAST
                    if s:
                        for j in range(4):
                            pool.wait_ge(gat[j].sem, gat[j].at(s, n))
                    else:
                        for j in range(4):
                            pool.wait_ge(gat[j].sem, n * 16)
                    g.tensor_copy(idx_slot[:, :], idx[:, ds(Q4, 4)]).then_inc(idxed.sem, 1)
                    for j in (3, 2, 1, 0):
                        if KINDS[s] == "X":
                            used = (vd.sem, vd.at(s, n))
                        else:
                            free = mprod if KINDS[s] in ("LA", "LB") else m_free
                            used = (free.sem, free.last(s, n, f"t{j}"))
                        alone(pool, used, *([(idxed.sem, idxed.at(s, n, "slots"))] if j == 3 else []))
                        g.indirect_dma_start(M[:, j, 0:w], None, table,
                                             bass.IndirectOffsetOnAxis(ap=idx_slot[:, j:j + 1], axis=0)).then_inc(gat[j].sem, 16)

            gathers(0, x, idx_x, D)
            pool.wait_ge(p_ready, 2)
            for t in q_st.values():
                for b in (0, 1):
                    pool.wait_ge(t[b].sem, 16 * PLAIN_TURNS)
            for s, kind in STAGES[1:]:
                stage_stored(pool, s - 1)
                if kind not in hself.order:
                    gathers(s, TAB[s], idx_l2 if kind in ("LA", "LB") else idx_all, D)
                    continue
                gathers(s, TAB[s], idx_all, GW)
                pool.wait_ge(m_v.sem, m_v.at(0, ATTENTION.index(s), "weights"))
                with pool.Fori(0, QUADS) as n:
                    Q4 = n * (-4) + 4 * LAST
                    pool.wait_ge(agg.sem, agg.at(s, n))
                    pw = PT[:, 0:2, ds(Q4, 4)].rearrange("p h j -> p j h")
                    for h in (0, 1):
                        g.tensor_tensor(MP[:, :, 64 * h:64 * h + 64], G[:, ds(Q4, 4), 64 * h:64 * h + 64],
                                        wide(PT[:, h, ds(Q4, 4)], 64), ALU.mult)
                    g.tensor_copy(MP[:, :, D:GW], pw).then_inc(mprod.sem, 1)
                    pool.wait_ge(own.sem, own.at(s, n, "rows"))
                    pool.wait_ge(vd.sem, vd.at(s, n))
                    if kind == "GA":
                        pool.wait_ge(pd.sem, pd.at(s, n))
                    else:
                        for j in range(4):
                            pool.wait_ge(st_o[j].sem, st_o[j].at(s, n))
                    for h in (0, 1):
                        last = g.tensor_tensor(U[:, :, 64 * h:64 * h + 64], OWN[:, :, 64 * h:64 * h + 64],
                                               wide(PT[:, 2 + h, ds(Q4, 4)], 64), ALU.mult)
                    last.then_inc(hself.sem, 1)
                    if kind == "GZ":
                        g.tensor_copy(idx_slot[:, :], idx_dst[:, ds(Q4, 4)]).then_inc(m_idx, 1)
                        alone(pool, (m_idx, n + 1), (vd.sem, vd.at(s, n, "x")))
                        for j in range(4):
                            g.indirect_dma_start(out, bass.IndirectOffsetOnAxis(ap=idx_slot[:, j:j + 1], axis=0),
                                                 U[:, j, :], None, bounds_check=N - 1,
                                                 oob_is_err=False).then_inc(st_o[j].sem, 16)
            for j in range(4):
                pool.wait_ge(st_o[j].sem, 16 * QUADS)

        @block.vector
        def _(dve):
            v = nc.vector
            count = [0]

            def link(ins):
                count[0] += 1
                ins.then_inc(p_dve, 1)
                dve.wait_ge(p_dve, count[0])

            def two(t):
                return t.rearrange("q b p -> q (b p)")

            dve.wait_ge(p_raw, 7 * 16)
            dve.wait_ge(c_pool, 13)
            link(v.tensor_copy(x2f[:, :, :], raw2[:, :, :]))
            dst2 = x2f[:, :, 1:P + 1]
            FI, A, last, cm0, lm1, lm0, lm = FI4[:, 0], A4[:, 0], V[:, 0], V[:, 1], V[:, 2], V[:, 3], V[:, 4]
            v.tensor_tensor(FI, dst2, x2f[:, :, 0:P], ALU.not_equal)
            v.tensor_tensor(last, dst2, x2f[:, :, 2:P + 2], ALU.not_equal)
            v.memset(cm0, 0.0)
            link(v.memset(lm0, 0.0))
            v.tensor_scalar(A, FI, -1.0, 1.0, ALU.mult, ALU.add)
            v.tensor_scalar(lm1, last, -1.0, 1.0, ALU.mult, ALU.add)
            v.tensor_scalar(R2[:, 0], last, -BIG, None, ALU.mult)
            link(v.tensor_tensor(W4[:, 2], FI, W4[:, 0], ALU.mult))
            v.tensor_copy(cm0[:, :, 0:1], A[:, :, 0:1])
            link(v.tensor_copy(lm0[:, :, P - 1:P], lm1[:, :, P - 1:P]))
            v.memset(A[:, :, 0:1], 0.0)
            v.memset(lm1[:, :, P - 1:P], 0.0)
            link(v.memset(R2[:, 0, :, P - 1:P], -BIG))
            v.tensor_tensor_scan(two(CM[:, :, :]), two(A), two(cm0), 0.0, ALU.mult, ALU.add)
            v.tensor_tensor_scan(two(lm)[:, ::-1], two(lm1)[:, ::-1], two(lm0)[:, ::-1], 0.0, ALU.mult, ALU.add)
            v.tensor_tensor_scan(two(HS[:, 0]), two(A), two(W4[:, 2]), 0.0, ALU.mult, ALU.add)
            v.tensor_tensor_scan(two(HS[:, 1])[:, ::-1], two(R2[:, 0])[:, ::-1], two(W4[:, 0])[:, ::-1], -BIG,
                                 ALU.add, ALU.max)
            for k in (1, 2, 3):
                v.tensor_copy(FI4[:, k], FI)
                v.tensor_copy(A4[:, k], A)
            link(v.tensor_copy(R2[:, 1], R2[:, 0]))
            link(v.tensor_scalar(LMB[:, :, :], lm, BIG, -BIG, ALU.mult, ALU.add))
            v.tensor_copy(ends[:, :, 0:1], HS[:, 0, :, P - 1:P])
            v.tensor_copy(ends[:, :, 1:2], HS[:, 1, :, 0:1])
            v.tensor_copy(ends[:, :, 2:6], CM[:, :, P - 1:P].to_broadcast([HALF, 2, 4]))
            v.tensor_copy(ends[:, :, 6:8], LMB[:, :, 0:1].to_broadcast([HALF, 2, 2]))
            v.tensor_copy(ends[:, :, 8:9], lm[:, :, P - 1:P]).then_inc(p_v, 1)
            dve.wait_ge(p_p, 1)
            v.tensor_copy(rfa[:, :], PS[0:4, 2, 0:T])
            v.tensor_copy(rb[:, :], PS[0:2, 3, 0:T])
            link(v.tensor_copy(cont[:, :], PS[0:1, 4, 0:T]))
            v.tensor_tensor_scan(crow[0:1, 1:T + 1], rfa[0:1, :], PS[0:1, 0, 0:T], 0.0, ALU.mult, ALU.add)
            v.tensor_tensor_scan(brow[0:1, 0:T][:, ::-1], rb[0:1, :][:, ::-1], PS[0:1, 1, 0:T][:, ::-1], -BIG,
                                 ALU.add, ALU.max).then_inc(p_v, 1)
            dve.wait_ge(p_p, 2)
            link(v.tensor_copy(cb[:, 0, 0:2], PS[0:HALF, 5, 0:2]))
            link(v.tensor_copy(cb[:, 1, 0:2], PS[0:HALF, 6, 0:2]))
            for b in (0, 1):
                v.scalar_tensor_tensor(W4[:, 2, b], CM[:, b, :], cb[:, 0, b:b + 1], HS[:, 0, b], ALU.mult, ALU.add)
                last_ = v.scalar_tensor_tensor(W4[:, 3, b], LMB[:, b, :], cb[:, 1, b:b + 1], HS[:, 1, b],
                                               ALU.add, ALU.max)
            link(last_)
            v.scalar_tensor_tensor(V[:, 1], W4[:, 3], 1.0, W4[:, 2], ALU.add, ALU.subtract)
            link(v.tensor_tensor(V[:, 0], W4[:, 2], W4[:, 1], ALU.subtract))
            v.tensor_scalar_max(V[:, 2], V[:, 0], 0.0)
            v.tensor_copy(V[:, 3], dst2)
            v.tensor_copy(V[:, 4], srcraw[:, :, :]).then_inc(p_v, 1)

            dve.wait_ge(c_load, LOADED)
            for l in range(4):
                for k in (0, 1):
                    link(v.tensor_tensor(avt, WX[:, l, 0:D], av[2 * l + k], ALU.mult))
                    link(v.tensor_reduce(WX[:, l, D + 2 * k:D + 2 * k + 2], avt.rearrange("p (h c) -> p h c", h=2),
                                         AX.X, ALU.add))
            link(v.bn_stats(stat[:, 0, :], bias_r[:, 2, :]))
            link(v.bn_aggr(mv[:, 0, :], stat[:, 0, :]))
            v.tensor_copy(te4[:, 0:1], mv[:, 0, 1:2]).then_inc(p_va, 1)
            dve.wait_ge(p_a, 1)
            link(v.reciprocal(rs[:, 0:1], sd[:, 0:1]))
            link(v.tensor_scalar(c2_r[:, :], bias_r[:, 2, :], mv[:, 0, 0:1], rs[:, 0:1], ALU.subtract, ALU.mult))
            link(v.tensor_tensor(c2_r[:, :], c2_r[:, :], lnw_r[:, :], ALU.mult))
            link(v.tensor_tensor(c2_r[:, :], c2_r[:, :], lnb_r[:, :], ALU.add))
            link(v.tensor_scalar_max(c2_r[:, :], c2_r[:, :], 0.0))

            dve.wait_ge(p_p, 3)
            v.tensor_copy(deg[:, :], PS[:, 0, 0:T])
            v.tensor_copy(rel[:, :], PS[:, 1, 0:T])
            v.tensor_copy(te3[:, :], PS[:, 3, 0:T])
            v.tensor_copy(idx_src[:, :], PS[:, 4, 0:T])
            v.tensor_copy(relL[:, :], PS[0:1, 5, 0:T])
            link(v.tensor_scalar(te2[:, :], PS[:, 2, 0:T], -FAR, FAR, ALU.mult, ALU.add))
            v.tensor_tensor(idx_dst[:, :], te2[:, :], te3[:, :], ALU.add)
            v.tensor_scalar_min(idx_x[:, :], te3[:, :], float(N - 1))
            v.tensor_copy(node_val[:, :, 0], te1[:, :])
            v.tensor_copy(node_val[:, :, 1], deg[:, :]).then_inc(p_ready, 1)

            def norm_sums(q, m, b, x_, k):
                for j in range(4):
                    i = v.bn_stats(PST[b][:, j, :], x_[:, j, :])
                i.then_inc(q.sem, 1)
                alone(dve, (q.sem, q.at(0, m, f"stats{k}")))
                for j in range(4):
                    i = v.bn_aggr(PMV[b][:, j, :], PST[b][:, j, :])
                i.then_inc(q.sem, 1)

            def norm_coef(q, m, b, k):
                dve.wait_ge(q_a[b].sem, q_a[b].at(0, m, f"sd{k}"))
                v.reciprocal(PRS[b], PSD[b]).then_inc(q.sem, 1)
                dve.wait_ge(q.sem, q.at(0, m, f"rs{k}"))
                v.scalar_tensor_tensor(PNB[b], PMV[b][:, :, 0], -1.0, PRS[b], ALU.mult, ALU.mult).then_inc(q.sem, 1)

            def plain(m):
                for b in (0, 1):
                    dve.wait_ge(q_ld[b].sem, q_ld[b].at(0, m, "x"))
                    norm_sums(q_v[b], m, b, PXT[b], 1)
                for b in (0, 1):
                    norm_coef(q_v[b], m, b, 1)
                for b in (0, 1):
                    q = q_v[b]
                    dve.wait_ge(q_p[b].sem, q_p[b].at(0, m, "h1b"))
                    v.tensor_scalar(PHT[b][:, 1, :], PS[:, 4 * b + 2, :], b1[:, 1:2], 0.0, ALU.add,
                                    ALU.max).then_inc(q.sem, 1)
                for b in (0, 1):
                    q = q_v[b]
                    dve.wait_ge(q_a[b].sem, q_a[b].at(0, m, "g1"))
                    v.tensor_tensor(PXT[b], PXT[b], on4(b2_r[:, :]), ALU.add).then_inc(q.sem, 1)
                    dve.wait_ge(q.sem, q.at(0, m, "xb"))
                    dve.wait_ge(q_a[b].sem, q_a[b].at(0, m, "t1"))
                    v.tensor_tensor(PXT[b], PXT[b], PRO[b][0][:, :, 0:D], ALU.add).then_inc(q.sem, 1)
                    dve.wait_ge(q.sem, q.at(0, m, "x1"))
                    norm_sums(q, m, b, PXT[b], 2)
                for b in (0, 1):
                    norm_coef(q_v[b], m, b, 2)
                for b in (0, 1):
                    q = q_v[b]
                    dve.wait_ge(q_p[b].sem, q_p[b].at(0, m, "rB"))
                    v.tensor_tensor(PYT[b], bank(4 * b + 3), on4(b2l_r[:, :]), ALU.add).then_inc(q.sem, 1)
                    dve.wait_ge(q.sem, q.at(0, m, "y"))
                    dve.wait_ge(q_a[b].sem, q_a[b].at(0, m, "g2"))
                    v.scalar_tensor_tensor(PXT[b], PYT[b], 0.0, PXT[b], ALU.max, ALU.add).then_inc(q.sem, 1)
                    dve.wait_ge(q.sem, q.at(0, m, "yx"))
                    v.tensor_tensor(PXT[b], PXT[b], on4(c2_r[:, :]), ALU.add).then_inc(q.sem, 1)
                    dve.wait_ge(q.sem, q.at(0, m, "x3"))
                    norm_sums(q, m, b, PXT[b], 3)
                for b in (0, 1):
                    norm_coef(q_v[b], m, b, 3)
                for t, r, before in ((8, 0, "t2"), (9, 1, "t4"), (10, 0, "t8"), (11, 1, "t9")):
                    for b in (0, 1):
                        q = q_v[b]
                        st = q_st[before][b]
                        dve.wait_ge(st.sem, st.at(0, m, before))
                        dve.wait_ge(q_p[b].sem, q_p[b].at(0, m, f"r{t}"))
                        v.tensor_copy(PRO[b][r], pair(4 * b + 2)).then_inc(q.sem, 1)
                for b in (0, 1):
                    q = q_v[b]
                    dve.wait_ge(q_a[b].sem, q_a[b].at(0, m, "g3"))
                    v.tensor_tensor(PXT[b], PXT[b], on4(gout_r[:, :]), ALU.add).then_inc(q.sem, 1)
                    dve.wait_ge(q.sem, q.at(0, m, "xo"))
                    v.tensor_tensor(PXT[b], PXT[b], PRO[b][1][:, :, 0:D], ALU.add).then_inc(q.sem, 1)

            with dve.Fori(0, PLAIN_TURNS - 1) as m:
                plain(m)
            plain(PLAIN_TURNS - 1)

            dve.wait_ge(n_cp, QUADS)
            pos, degs = node_src[:, :, 0], node_src[:, :, 1]
            v.tensor_copy(te4[:, :], idx_src[:, :])
            link(v.tensor_scalar(te2[:, :], pos, 0.0, None, ALU.is_lt))
            link(v.scalar_tensor_tensor(te3[:, :], te4[:, :], float(EP + 1), te2[:, :], ALU.add, ALU.mult))
            link(v.tensor_tensor(idx_all[:, :], pos, te3[:, :], ALU.add))
            link(v.scalar_tensor_tensor(te3[:, :], te1[:, :], 1.0, te2[:, :], ALU.add, ALU.mult))
            link(v.tensor_tensor(idx_l2[:, :], pos, te3[:, :], ALU.add))
            link(v.tensor_scalar_add(dis2[:, :], deg[:, :], 1.0))
            link(v.scalar_tensor_tensor(te3[:, :], degs, 1.0, dis2[:, :], ALU.add, ALU.mult))
            link(v.scalar_tensor_tensor(te4[:, :], degs, 1.0, deg[:, :], ALU.max, ALU.mult))
            v.tensor_scalar(te2[:, :], te2[:, :], -1.0, 1.0, ALU.mult, ALU.add).then_inc(p_va, 1)
            dve.wait_ge(p_a, 2)
            link(v.reciprocal(wgcn[:, :], te3[:, :]))
            link(v.reciprocal(te4[:, :], te4[:, :]))
            link(v.tensor_tensor(wl2[:, :], te4[:, :], te2[:, :], ALU.mult))
            link(v.reciprocal(winv[:, :], deg[:, :]))
            link(v.reciprocal(dis2[:, :], dis2[:, :]))
            v.memset(te4[:, 0:1], 0.0).then_inc(p_ready, 1)

            def selectors(s, n, weight):
                for j in (3, 2, 1, 0):
                    i = ds(n * (-4) + (4 * LAST + j), 1)
                    dve.wait_ge(agg.sem, agg.last(s, n, f"t{j}"))
                    if weight is None:
                        v.tensor_scalar(S[:, j, :], iota_row[:, :], rel[:, i], None, ALU.is_equal)
                    else:
                        v.tensor_scalar(S[:, j, :], iota_row[:, :], rel[:, i], weight[:, i], ALU.is_equal, ALU.mult)
                    v.tensor_scalar(LO[:, j, :], iota_row[0:1, :], relL[:, i], cont[:, i], ALU.is_equal,
                                    ALU.mult).then_inc(sel.sem, 1)

            def chain(s, n, ins, name):
                ins.then_inc(vd.sem, 1)
                alone(dve, (vd.sem, vd.at(s, n, name)))

            def sums(s, n, x_, k=""):
                for j in range(4):
                    i = v.bn_stats(stat[:, j, :], x_[:, j, :])
                chain(s, n, i, "stats" + k)
                for j in range(4):
                    i = v.bn_aggr(mv[:, j, :], stat[:, j, :])
                i.then_inc(vd.sem, 1)

            def coef(s, n, k=""):
                dve.wait_ge(ad.sem, ad.at(s, n, "sd" + k))
                chain(s, n, v.reciprocal(rs[:, :], sd[:, :]), "rs" + k)
                v.scalar_tensor_tensor(nb[:, :], mv[:, :, 0], -1.0, rs[:, :], ALU.mult, ALU.mult).then_inc(vd.sem, 1)

            def aggregated(s, n):
                dve.wait_ge(agg.sem, agg.at(s, n, "t0"))
                dve.wait_ge(carry.sem, carry.at(s, n, "t0"))

            A4ps = PS[:, 0:4, 0:D]
            for s, kind in STAGES:
                if kind in hself.order:
                    with dve.Fori(0, QUADS) as n:
                        Q4 = n * (-4) + 4 * LAST
                        for j in (3, 2, 1, 0):
                            dve.wait_ge(gat[j].sem, gat[j].at(s, n, "rows"))
                            v.tensor_copy(G[:, ds(Q4 + j, 1), :], M[:, j:j + 1, :]).then_inc(m_free.sem, 1)
                    attention_middle(dve, v, link, s)

                with dve.Fori(0, QUADS) as n:
                    Q4 = n * (-4) + 4 * LAST
                    if kind == "X":
                        for j in (3, 2, 1, 0):
                            dve.wait_ge(gat[j].sem, gat[j].at(s, n, "rows"))
                        dve.wait_ge(st_x.sem, st_x.at(s, n))
                        dve.wait_ge(ad.sem, ad.at(s, n))
                        chain(s, n, v.tensor_copy(U[:, :, :], M[:, :, 0:D]), "copy")
                        sums(s, n, U)
                        coef(s, n)
                    elif kind in ("C1", "C2"):
                        selectors(s, n, wgcn)
                        dve.wait_ge(own.sem, own.at(s, n, "rows"))
                        if kind == "C1":
                            dve.wait_ge(pd.sem, pd.at(s, n))
                        else:
                            dve.wait_ge(st_x.sem, st_x.at(s, n))
                            dve.wait_ge(ad.sem, ad.at(s, n))
                        chain(s, n, v.tensor_tensor(U[:, :, :], OWN[:, :, 0:D], wide(dis2[:, ds(Q4, 4)], D),
                                                    ALU.mult), "own")
                        aggregated(s, n)
                        chain(s, n, v.tensor_tensor(U[:, :, :], A4ps, U[:, :, :], ALU.add), "comb")
                        if kind == "C1":
                            dve.wait_ge(pd.sem, pd.at(s, n, "h1b"))
                            v.tensor_scalar(H1T[:, 1, :], PS[:, 6, :], b1[:, 1:2], 0.0, ALU.add,
                                            ALU.max).then_inc(vd.sem, 1)
                        else:
                            chain(s, n, v.tensor_tensor(U[:, :, :], U[:, :, :], on4(b2_r[:, :]), ALU.add), "bias")
                            dve.wait_ge(xin.sem, xin.at(s, n, "rows"))
                            chain(s, n, v.tensor_tensor(U[:, :, :], U[:, :, :], XIN[:, :, :], ALU.add), "x")
                            sums(s, n, U)
                            coef(s, n)
                    elif kind == "S1":
                        selectors(s, n, winv)
                        dve.wait_ge(pd.sem, pd.at(s, n))
                        aggregated(s, n)
                        chain(s, n, v.tensor_copy(U[:, :, :], A4ps), "comb")
                    elif kind == "S2":
                        selectors(s, n, winv)
                        dve.wait_ge(own.sem, own.at(s, n, "rows"))
                        dve.wait_ge(st_x.sem, st_x.at(s, n))
                        dve.wait_ge(ad.sem, ad.at(s, n))
                        aggregated(s, n)
                        chain(s, n, v.tensor_tensor(U[:, :, :], A4ps, OWN[:, :, 0:D], ALU.add), "comb")
                        chain(s, n, v.tensor_tensor(U[:, :, :], U[:, :, :], on4(b2l_r[:, :]), ALU.add), "bias")
                        dve.wait_ge(xin.sem, xin.at(s, n, "rows"))
                        chain(s, n, v.scalar_tensor_tensor(U[:, :, :], U[:, :, :], 0.0, XIN[:, :, :], ALU.max,
                                                           ALU.add), "x")
                        sums(s, n, U)
                        coef(s, n)
                    elif kind in ("LA", "LB"):
                        l = s - 5
                        selectors(s, n, None)
                        dve.wait_ge(pd.sem, pd.at(s, n, "em"))
                        for j in (3, 2, 1, 0):
                            i = ds(Q4 + j, 1)
                            dve.wait_ge(gat[j].sem, gat[j].at(s, n, "rows"))
                            v.scalar_tensor_tensor(MP[:, j, 0:D], M[:, j, 0:D], wl2[:, i], bank(5)[:, j, :],
                                                   ALU.mult, ALU.add).then_inc(mprod.sem, 1)
                        dve.wait_ge(ad.sem, ad.at(s, n))
                        if kind == "LB":
                            dve.wait_ge(st_x.sem, st_x.at(s, n))
                        aggregated(s, n)
                        chain(s, n, v.tensor_tensor(U[:, :, :], A4ps, on4(bias_r[:, l, :]), ALU.add), "comb")
                        sums(s, n, U)
                        coef(s, n)
                        if kind == "LB":
                            dve.wait_ge(ad.sem, ad.at(s, n, "n"))
                            chain(s, n, v.tensor_tensor(U[:, :, :], GN[:, :, :], on4(lnw_r[:, :]), ALU.mult), "lnw")
                            chain(s, n, v.tensor_tensor(U[:, :, :], U[:, :, :], on4(lnb_r[:, :]), ALU.add), "lnb")
                            dve.wait_ge(xin.sem, xin.at(s, n, "rows"))
                            chain(s, n, v.scalar_tensor_tensor(U[:, :, :], U[:, :, :], 0.0, XIN[:, :, :], ALU.max,
                                                               ALU.add), "x")
                            sums(s, n, U, "2")
                            coef(s, n, "2")
                    else:
                        selectors(s, n, None)
                        aggregated(s, n)
                        ps = PT[:, 2:4, ds(Q4, 4)].rearrange("p h j -> p j h")
                        chain(s, n, v.tensor_tensor(den[:, :, :], PS[:, 0:4, D:GW], ps, ALU.add), "den")
                        chain(s, n, v.tensor_scalar_add(den[:, :, :], den[:, :, :], 1e-16), "dene")
                        chain(s, n, v.reciprocal(den[:, :, :], den[:, :, :]), "rden")
                        dve.wait_ge(hself.sem, hself.at(s, n, "own"))
                        chain(s, n, v.tensor_tensor(U[:, :, :], A4ps, U[:, :, :], ALU.add), "comb")
                        for h in (0, 1):
                            uh = U[:, :, 64 * h:64 * h + 64]
                            i = v.tensor_tensor(uh, uh, wide(den[:, :, h], 64), ALU.mult)
                        chain(s, n, i, "norm")
                        if kind == "GZ":
                            chain(s, n, v.tensor_tensor(U[:, :, :], U[:, :, :], on4(gout_r[:, :]), ALU.add), "bias")
                            dve.wait_ge(xin.sem, xin.at(s, n, "rows"))
                            v.tensor_tensor(U[:, :, :], U[:, :, :], XIN[:, :, :], ALU.add).then_inc(vd.sem, 1)

        @block.tensor
        def _(pe):
            def turn(o, i):
                k = i.shape[0]
                return nc.tensor.transpose(o, i, ident[0:k, 0:k])

            def mm(o, l, r, start=True, stop=True):
                return nc.tensor.matmul(o, l, r, start=start, stop=stop)

            pe.wait_ge(c_pool, 5)
            pe.wait_ge(p_v, 1)
            for c, (lo, hi) in enumerate(((0, 1), (1, 2), (2, 6), (6, 8), (8, 9))):
                for b in (0, 1):
                    i = turn(PS[0:hi - lo, c, HALF * b:HALF * b + HALF], ends[:, b, lo:hi])
            i.then_inc(p_p, 1)
            pe.wait_ge(p_v, 2)
            for b in (0, 1):
                turn(PS[0:HALF, 5, b:b + 1], crow[0:1, HALF * b:HALF * b + HALF])
                i = turn(PS[0:HALF, 6, b:b + 1], brow[0:1, HALF * b + 1:HALF * b + HALF + 1])
            i.then_inc(p_p, 1)
            pe.wait_ge(p_v, 3)
            for c, t in enumerate((V[:, 1], V[:, 2], FI4[:, 0], V[:, 3], V[:, 4])):
                for b in (0, 1):
                    turn(PS[:, c, HALF * b:HALF * b + HALF], t[:, b, :])
            for b in (0, 1):
                i = turn(PS[0:1, 5, HALF * b:HALF * b + HALF], V[:, 2, b, P - 1:P])
            i.then_inc(p_p, 1)
            def ea_turn(n, rows):
                for j in range(4):
                    i = turn(PS[0:ED, 7, P * j:P * j + P], rows[:, j, :])
                i.then_inc(e_tr, 1)

            with pe.Fori(0, LAST) as n:
                pe.wait_ge(e_ld, n * 16 + 16)
                pe.wait_ge(e_cp, n)
                ea_turn(n, ea_in)
            pe.wait_ge(e_ld, 16 * QUADS)
            pe.wait_ge(e_cp, LAST)
            ea_turn(LAST, ea_last)

            pe.wait_ge(c_load, LOADED)
            pe.wait_ge(p_ready, 1)

            def turn4(o, rows):
                for j in range(4):
                    i = turn(o[:, P * j:P * j + P], rows[:, j, :])
                return i

            def rows4(o, hT, w):
                for j in range(4):
                    i = mm(o[:, j, :], hT[:, P * j:P * j + P], w)
                return i

            def plain(m):
                for b in (0, 1):
                    pe.wait_ge(q_v[b].sem, q_v[b].at(0, m))
                    pe.wait_ge(q_a[b].sem, q_a[b].at(0, m, "g1"))
                    turn4(PS[:, 4 * b], PGN[b]).then_inc(q_p[b].sem, 1)
                for b in (0, 1):
                    pe.wait_ge(q_a[b].sem, q_a[b].at(0, m, "gT1"))
                    mm(PS[:, 4 * b + 1], w1[:, 0:P], PTT[b]).then_inc(q_p[b].sem, 1)
                    mm(PS[:, 4 * b + 2], w1[:, P:2 * P], PTT[b]).then_inc(q_p[b].sem, 1)
                for b in (0, 1):
                    pe.wait_ge(q_a[b].sem, q_a[b].at(0, m, "h1a"))
                    pe.wait_ge(q_v[b].sem, q_v[b].at(0, m, "h1b"))
                    for j in range(4):
                        for k in (0, 1):
                            i = mm(bank(4 * b + 3)[:, j, :], PHT[b][:, k, P * j:P * j + P], w2[:, k, :], k == 0, k == 1)
                    i.then_inc(q_p[b].sem, 1)
                for b in (0, 1):
                    pe.wait_ge(q_a[b].sem, q_a[b].at(0, m, "g2"))
                    turn4(PS[:, 4 * b], PGN[b]).then_inc(q_p[b].sem, 1)
                for b in (0, 1):
                    pe.wait_ge(q_a[b].sem, q_a[b].at(0, m, "gT2"))
                    mm(PS[:, 4 * b + 1], w1r[:, :], PTT[b]).then_inc(q_p[b].sem, 1)
                for b in (0, 1):
                    pe.wait_ge(q_a[b].sem, q_a[b].at(0, m, "h2"))
                    rows4(bank(4 * b + 2), PHT[b][:, 0, :], w2l[:, :]).then_inc(q_p[b].sem, 1)
                    rows4(bank(4 * b + 3), PHT[b][:, 0, :], w2r[:, :]).then_inc(q_p[b].sem, 1)
                for b in (0, 1):
                    pe.wait_ge(q_a[b].sem, q_a[b].at(0, m, "g3"))
                    turn4(PS[:, 4 * b], PGN[b]).then_inc(q_p[b].sem, 1)
                for l, hT, at in ((0, lambda b: PTT[b], "gT3"), (1, lambda b: PHT[b][:, 0, :], "h8"),
                                  (2, lambda b: PHT[b][:, 1, :], "h9"), (3, lambda b: PHT[b][:, 0, :], "h10")):
                    for b in (0, 1):
                        pe.wait_ge(q_a[b].sem, q_a[b].at(0, m, at))
                        if l < 3:
                            mm(PS[:, 4 * b + 1], WX[:, l, 0:D], hT(b)).then_inc(q_p[b].sem, 1)
                        if l:
                            pe.wait_ge(q_v[b].sem, q_v[b].at(0, m, f"r{7 + l}"))
                        rows4(pair(4 * b + 2), hT(b), WX[:, l, 0:GW]).then_inc(q_p[b].sem, 1)

            with pe.Fori(0, PLAIN_TURNS - 1) as m:
                plain(m)
            plain(PLAIN_TURNS - 1)
            for b in (0, 1):
                pe.wait_ge(q_v[b].sem, q_v[b].at(0, PLAIN_TURNS - 1, "xf"))

            def aggregate(s, n, kind):
                w = GW if kind in hself.order else D
                if kind in hself.order:
                    pe.wait_ge(mprod.sem, mprod.at(s, n, "quad"))
                pe.wait_ge(vd.sem, vd.last(s, n, "comb"))
                for j in (3, 2, 1, 0):
                    A = PS[:, j, 0:w]
                    pe.wait_ge(sel.sem, sel.at(s, n, f"t{j}"))
                    if kind in hself.order:
                        mm(A, S[:, j, :], MP[:, j, :], True, False)
                    elif kind in ("LA", "LB"):
                        pe.wait_ge(mprod.sem, mprod.at(s, n, f"t{j}"))
                        mm(A, S[:, j, :], MP[:, j, 0:D], True, False)
                    else:
                        pe.wait_ge(gat[j].sem, gat[j].at(s, n, "rows"))
                        mm(A, S[:, j, :], M[:, j, 0:D], True, False).then_inc(m_free.sem, 1)
                    before = carry.at(s, n) + (3 - j)
                    pe.wait_ge(carry.sem, before)
                    mm(A, LO[:, j, :], C[:, 0:w], False, True).then_inc(agg.sem, 1)

            for s, kind in STAGES:
                if kind == "X":
                    continue
                pe.wait_ge(vd.sem, vd.at(s, 0))
                pe.wait_ge(ad.sem, ad.at(s, 0))
                if kind in hself.order:
                    attention_turns(pe, turn, s)
                with pe.Fori(0, QUADS) as n:
                    if kind in ("LA", "LB"):
                        l = s - 5
                        pe.wait_ge(eas.sem, eas.at(s, n, "attr"))
                        mm(PS[:, 4, :], ew1[:, l, :], eat[:, :]).then_inc(pd.sem, 1)
                        pe.wait_ge(ad.sem, ad.at(s, n, "rT"))
                        pe.wait_ge(mprod.sem, mprod.at(s, n))
                        mm(PS[:, 5, :], ones_row[:, :], eb2[0:1, l, :, :].rearrange("p j c -> p (j c)"), True, False)
                        for j in range(4):
                            i = mm(bank(5)[:, j, :], H1T[:, 0, P * j:P * j + P], ew2[:, l, :], False, j == 3)
                        i.then_inc(pd.sem, 1)
                    aggregate(s, n, kind)
                    if kind == "C1":
                        pe.wait_ge(vd.sem, vd.at(s, n, "comb"))
                        turn4(PS[:, 4], U).then_inc(pd.sem, 1)
                        pe.wait_ge(ad.sem, ad.at(s, n, "uT"))
                        mm(PS[:, 5, :], w1[:, 0:P], UT[:, :]).then_inc(pd.sem, 1)
                        mm(PS[:, 6, :], w1[:, P:2 * P], UT[:, :]).then_inc(pd.sem, 1)
                        pe.wait_ge(ad.sem, ad.at(s, n, "h1a"))
                        pe.wait_ge(vd.sem, vd.at(s, n, "h1b"))
                        for j in range(4):
                            for k in (0, 1):
                                i = mm(bank(7)[:, j, :], H1T[:, k, P * j:P * j + P], w2[:, k, :], k == 0, k == 1)
                        i.then_inc(pd.sem, 1)
                    elif kind == "S1":
                        pe.wait_ge(vd.sem, vd.at(s, n, "comb"))
                        turn4(PS[:, 4], U).then_inc(pd.sem, 1)
                        pe.wait_ge(own.sem, own.at(s, n, "rows"))
                        turn4(PS[:, 5], OWN[:, :, 0:D]).then_inc(pd.sem, 1)
                        pe.wait_ge(ad.sem, ad.at(s, n, "oT"))
                        mm(PS[:, 6, :], w1l[:, :], UT[:, :], True, False)
                        mm(PS[:, 6, :], w1r[:, :], OT[:, :], False, True).then_inc(pd.sem, 1)
                        pe.wait_ge(ad.sem, ad.at(s, n, "hT"))
                        rows4(bank(7), H1T[:, 0, :], w2l[:, :]).then_inc(pd.sem, 1)
                        rows4(bank(4), H1T[:, 0, :], w2r[:, :]).then_inc(pd.sem, 1)
                    elif kind == "S2":
                        pe.wait_ge(ad.sem, ad.at(s, n, "g"))
                        turn4(PS[:, 4], GN).then_inc(pd.sem, 1)
                        pe.wait_ge(ad.sem, ad.at(s, n, "gT"))
                        rows4(bank(7), OT[:, :], linw[:, 0, :]).then_inc(pd.sem, 1)
                    elif kind == "LA":
                        pe.wait_ge(ad.sem, ad.at(s, n, "n"))
                        turn4(PS[:, 6], GN).then_inc(pd.sem, 1)
                        pe.wait_ge(ad.sem, ad.at(s, n, "nT"))
                        rows4(bank(7), OT[:, :], linw[:, s - 4, :]).then_inc(pd.sem, 1)
                    elif kind == "LB":
                        pe.wait_ge(ad.sem, ad.at(s, n, "g"))
                        turn4(PS[:, 4], GN).then_inc(pd.sem, 1)
                        pe.wait_ge(ad.sem, ad.at(s, n, "gT"))
                        rows4(pair(6, GW + 2), OT[:, :], WX[:, 0, :]).then_inc(pd.sem, 1)
                    elif kind == "GA":
                        pe.wait_ge(vd.sem, vd.at(s, n, "norm"))
                        turn4(PS[:, 4], U).then_inc(pd.sem, 1)
                        pe.wait_ge(ad.sem, ad.at(s, n, "uT"))
                        rows4(pair(6, GW + 2), OT[:, :], WX[:, s - 7, :]).then_inc(pd.sem, 1)

        @block.scalar
        def _(act):
            def f(o, i, fn, **kw):
                return nc.scalar.activation(o, i, fn, **kw)

            nc.scalar.preload_act_table(ACT.Sqrt)
            act.wait_ge(c_pool, 5)
            with act.Fori(0, QUADS) as n:
                act.wait_ge(e_tr, n + 1)
                act.wait_ge(e_st, n * 16)
                f(eat[:, :].rearrange("c (p j) -> c j p", j=4),
                  PS[0:ED, 7, :].rearrange("c (j p) -> c j p", j=4), ACT.Copy).then_inc(e_cp, 1)
            act.wait_ge(p_va, 1)
            f(sd[:, 0:1], te4[:, 0:1], ACT.Sqrt, bias=eps[:, :]).then_inc(p_a, 1)
            act.wait_ge(c_load, LOADED)

            def norm(m, b, k, before):
                act.wait_ge(q_v[b].sem, q_v[b].at(0, m, f"aggr{k}"))
                f(PSD[b], PMV[b][:, :, 1], ACT.Sqrt, bias=eps[:, :]).then_inc(q_a[b].sem, 1)

            def apply(m, b, k, st):
                act.wait_ge(q_v[b].sem, q_v[b].at(0, m, f"nb{k}"))
                act.wait_ge(*st)
                for j in range(4):
                    i = f(PGN[b][:, j, :], PXT[b][:, j, :], ACT.Relu, scale=PRS[b][:, j:j + 1], bias=PNB[b][:, j:j + 1])
                i.then_inc(q_a[b].sem, 1)

            def plain(m):
                for k in (1, 2, 3):
                    for b in (0, 1):
                        norm(m, b, k, None)
                    for b in (0, 1):
                        st = q_st["t1" if k == 2 else "t3"][b]
                        apply(m, b, k, (st.sem, st.at(0, m, st.order["P"][0]) if k > 1 else st.at(0, m)))
                    for b in (0, 1):
                        act.wait_ge(q_p[b].sem, q_p[b].at(0, m, f"gT{k}"))
                        f(PTT[b], PS[:, 4 * b, :], ACT.Copy).then_inc(q_a[b].sem, 1)
                    if k == 1:
                        for b in (0, 1):
                            act.wait_ge(q_p[b].sem, q_p[b].at(0, m, "h1a"))
                            f(PHT[b][:, 0, :], PS[:, 4 * b + 1, :], ACT.Relu, bias=b1[:, 0:1]).then_inc(q_a[b].sem, 1)
                        for b in (0, 1):
                            act.wait_ge(q_p[b].sem, q_p[b].at(0, m, "t1"))
                            st = q_st["t10"][b]
                            act.wait_ge(st.sem, st.at(0, m))
                            f(PRO[b][0][:, :, 0:D], bank(4 * b + 3), ACT.Copy).then_inc(q_a[b].sem, 1)
                    elif k == 2:
                        for b in (0, 1):
                            act.wait_ge(q_p[b].sem, q_p[b].at(0, m, "h2"))
                            f(PHT[b][:, 0, :], PS[:, 4 * b + 1, :], ACT.Relu, bias=b1l[:, 0:1]).then_inc(q_a[b].sem, 1)
                        for b in (0, 1):
                            act.wait_ge(q_p[b].sem, q_p[b].at(0, m, "rA"))
                            st = q_st["t11"][b]
                            act.wait_ge(st.sem, st.at(0, m))
                            act.wait_ge(q_v[b].sem, q_v[b].at(0, m))
                            f(PRO[b][1][:, :, 0:D], bank(4 * b + 2), ACT.Copy).then_inc(q_a[b].sem, 1)
                    else:
                        for l, name in ((0, "h8"), (1, "h9"), (2, "h10")):
                            for b in (0, 1):
                                act.wait_ge(q_p[b].sem, q_p[b].at(0, m, name))
                                f(PHT[b][:, l % 2, :], PS[:, 4 * b + 1, :], ACT.Relu,
                                  bias=gb_c[:, l:l + 1]).then_inc(q_a[b].sem, 1)

            with act.Fori(0, PLAIN_TURNS - 1) as m:
                plain(m)
            plain(PLAIN_TURNS - 1)
            act.wait_ge(p_va, 2)
            f(te3[:, :], te3[:, :], ACT.Sqrt)
            f(te4[:, :], te4[:, :], ACT.Sqrt).then_inc(p_a, 1)

            def sqrts(s, n, k=""):
                act.wait_ge(vd.sem, vd.at(s, n, "aggr" + k))
                f(sd[:, :], mv[:, :, 1], ACT.Sqrt, bias=eps[:, :]).then_inc(ad.sem, 1)

            def scaled(s, n, fn, k=""):
                act.wait_ge(vd.sem, vd.at(s, n, "nb" + k))
                for j in range(4):
                    i = f(GN[:, j, :], U[:, j, :], fn, scale=rs[:, j:j + 1], bias=nb[:, j:j + 1])
                i.then_inc(ad.sem, 1)

            for s, kind in STAGES:
                if kind in hself.order:
                    attention_exp(act, f, s)
                with act.Fori(0, QUADS) as n:
                    Q4 = n * (-4) + 4 * LAST
                    if kind in ("LA", "LB"):
                        act.wait_ge(pd.sem, pd.at(s, n, "rT"))
                        f(H1T[:, 0, :], PS[:, 4, :], ACT.Relu, bias=eb1[:, s - 5:s - 4]).then_inc(ad.sem, 1)
                    if kind in AGG:
                        w = GW if kind in hself.order else D
                        for j in (3, 2, 1, 0):
                            act.wait_ge(agg.sem, agg.at(s, n, f"t{j}"))
                            f(C[:, 0:w], PS[0:1, j, 0:w], ACT.Copy).then_inc(carry.sem, 1)
                    if kind in st_t.order:
                        act.wait_ge(st_t.sem, st_t.at(s, n))
                    if kind in ("X", "C2"):
                        sqrts(s, n)
                        scaled(s, n, ACT.Relu)
                    elif kind == "C1":
                        act.wait_ge(pd.sem, pd.at(s, n, "uT"))
                        f(UT[:, :], PS[:, 4, :], ACT.Copy).then_inc(ad.sem, 1)
                        act.wait_ge(pd.sem, pd.at(s, n, "h1a"))
                        f(H1T[:, 0, :], PS[:, 5, :], ACT.Relu, bias=b1[:, 0:1]).then_inc(ad.sem, 1)
                        act.wait_ge(pd.sem, pd.at(s, n, "rows"))
                        f(RO[:, :, 0:D], bank(7), ACT.Copy).then_inc(ad.sem, 1)
                    elif kind == "S1":
                        act.wait_ge(pd.sem, pd.at(s, n, "uT"))
                        f(UT[:, :], PS[:, 4, :], ACT.Copy).then_inc(ad.sem, 1)
                        act.wait_ge(pd.sem, pd.at(s, n, "oT"))
                        f(OT[:, :], PS[:, 5, :], ACT.Copy).then_inc(ad.sem, 1)
                        act.wait_ge(pd.sem, pd.at(s, n, "hT"))
                        f(H1T[:, 0, :], PS[:, 6, :], ACT.Relu, bias=b1l[:, 0:1]).then_inc(ad.sem, 1)
                        act.wait_ge(pd.sem, pd.at(s, n, "rA"))
                        f(RO[:, :, 0:D], bank(7), ACT.Copy).then_inc(ad.sem, 1)
                        act.wait_ge(st_x.sem, st_x.at(s, n))
                        act.wait_ge(pd.sem, pd.at(s, n, "rB"))
                        f(RB[:, :, :], bank(4), ACT.Copy).then_inc(ad.sem, 1)
                    elif kind == "S2":
                        sqrts(s, n)
                        scaled(s, n, ACT.Relu)
                        act.wait_ge(pd.sem, pd.at(s, n, "gT"))
                        f(OT[:, :], PS[:, 4, :], ACT.Copy).then_inc(ad.sem, 1)
                        act.wait_ge(pd.sem, pd.at(s, n, "rows"))
                        f(RO[:, :, 0:D], bank(7), ACT.Copy).then_inc(ad.sem, 1)
                    elif kind == "LA":
                        l = s - 5
                        sqrts(s, n)
                        scaled(s, n, ACT.Identity)
                        act.wait_ge(pd.sem, pd.at(s, n, "nT"))
                        f(OT[:, :], PS[:, 6, :], ACT.Relu, scale=lnw_c[:, l:l + 1], bias=lnb_c[:, l:l + 1]).then_inc(ad.sem, 1)
                        act.wait_ge(pd.sem, pd.at(s, n, "rows"))
                        f(RO[:, :, 0:D], bank(7), ACT.Copy).then_inc(ad.sem, 1)
                    elif kind == "LB":
                        sqrts(s, n)
                        scaled(s, n, ACT.Identity)
                        sqrts(s, n, "2")
                        scaled(s, n, ACT.Relu, "2")
                        act.wait_ge(pd.sem, pd.at(s, n, "gT"))
                        f(OT[:, :], PS[:, 4, :], ACT.Copy).then_inc(ad.sem, 1)
                    elif kind == "GA":
                        act.wait_ge(pd.sem, pd.at(s, n, "uT"))
                        f(OT[:, :], PS[:, 4, :], ACT.Relu, bias=gb_c[:, s - 8:s - 7]).then_inc(ad.sem, 1)
                    if kind in ("LB", "GA"):
                        act.wait_ge(pd.sem, pd.at(s, n, "rows"))
                        f(RO[:, :, :], pair(6), ACT.Copy).then_inc(ad.sem, 1)
                        f(NV[:, :, ds(Q4, 4)].rearrange("p k j -> p j k"), pair(6, GW + 2)[:, :, D:GW + 2],
                          ACT.Copy).then_inc(ad.sem, 1)


_INS = ["x", "src", "dst", "edge_attr_16", "L0_gnn_W1", "L0_gnn_b1", "L0_gnn_W2", "L0_gnn_b2",
        "L1_gnn_w1l", "L1_gnn_b1l", "L1_gnn_w1r", "L1_gnn_w2l", "L1_gnn_b2l", "L1_gnn_w2r",
        "L2_gnn_lin_w", "L2_gnn_edge_w1", "L2_gnn_edge_b1", "L2_gnn_edge_w2", "L2_gnn_edge_b2",
        "L2_gnn_bias", "L2_gnn_ln_w", "L2_gnn_ln_b", "L3_gnn_W_in", "L3_gnn_a_src_in", "L3_gnn_a_dst_in",
        "L3_gnn_b_in", "L3_gnn_W_h", "L3_gnn_a_src_h", "L3_gnn_a_dst_h", "L3_gnn_b_h", "L3_gnn_W_out",
        "L3_gnn_a_src_out", "L3_gnn_a_dst_out", "L3_gnn_b_out"]


def kernel(**inputs):
    import numpy as _np
    import concourse.bacc as _bacc
    from concourse.bass_utils import run_bass_kernel_spmd as _run

    nc = _bacc.Bacc("TRN2", target_bir_lowering=False, num_devices=1)
    arrays, aps = {}, {}
    for name in _INS:
        arr = _np.ascontiguousarray(inputs[name])
        arrays[f"in_{name}"] = arr
        aps[name] = nc.dram_tensor(f"in_{name}", arr.shape, mybir.dt.from_np(arr.dtype), kind="ExternalInput").ap()
    out = nc.dram_tensor("out_x", (N, D), mybir.dt.float32, kind="ExternalOutput").ap()
    gnn_program(nc, aps, out)
    r = _run(nc, [arrays], core_ids=[0])
    return r.results[0]["out_x"]
```

```python
import concourse.bass as bass
from concourse import mybir
from contextlib import ExitStack

P = 128
N = 50000
E = 25000
D = 128
ED = 16
T = -(-E // P)
EP = T * P
QUADS = T // 4
QR = 4 * P
HALF = T // 2
NROW = EP + N
GW = D + 2
BIG = 1.0e30
FAR = 1.0e6
LN_EPS = 1e-5
PLAIN_QUADS = -(-N // QR)
PLAIN_TURNS = PLAIN_QUADS // 2

KINDS = ["X", "C1", "C2", "S1", "S2", "LA", "LA", "LB", "GA", "GA", "GA", "GZ"]


class Steps:

    def __init__(self, sem, order, by=1, start=0, stages=KINDS, turns=QUADS):
        self.sem, self.order, self.by, self.start, self.stages, self.turns = sem, order, by, start, stages, turns

    def at(self, stage, turn, step=None):
        names = self.order.get(self.stages[stage], ())
        before = self.turns * sum(len(self.order.get(k, ())) for k in self.stages[:stage])
        k = 0 if step is None else names.index(step) + 1
        return turn * (self.by * len(names)) + (self.start + self.by * (before + k))

    def last(self, stage, turn, step):
        return self.at(stage, turn, step) - self.by * len(self.order[self.stages[stage]])


def gnn_program(nc, a, out):
    f32, i32 = mybir.dt.float32, mybir.dt.int32
    ALU, ACT, AX = mybir.AluOpType, mybir.ActivationFunctionType, mybir.AxisListType
    ds = bass.ds
    ctx = ExitStack()
    with ctx:
        def sb(name, shape, dt=f32):
            return ctx.enter_context(nc.sbuf_tensor(name, shape, dt))

        def sem(name):
            return ctx.enter_context(nc.semaphore(name))

        def dram(name, shape, dt=f32):
            return nc.dram_tensor(name, shape, dt, kind="Internal").ap()

        TAB = {s: dram(f"table{s}", (NROW, D)) for s in (1, 2, 3, 4)}
        TAB.update({s: dram(f"table{s}", (EP, D)) for s in (5, 6, 7)})
        TAB.update({s: dram(f"table{s}", (NROW, GW)) for s in (8, 9, 10, 11)})
        XR = {s: dram(f"xrows{s}", (EP, D)) for s in (0, 2, 4, 7)}
        SELF = dram("sage_self", (EP, D))
        NODE = dram("node_info", (N, 2))
        EAT = dram("edge_attr_t", (ED, EP))

        ident = sb("ident", [P, P])
        iota_row = sb("iota_row", [P, P])
        eps = sb("eps", [P, 1])
        ones_row = sb("ones_row", [1, P])
        w1 = sb("w1", [P, 256])
        w2 = sb("w2", [P, 2, D])
        b1 = sb("b1", [P, 2])
        w1l, w1r, w2l, w2r = (sb(n, [P, D]) for n in ("w1l", "w1r", "w2l", "w2r"))
        b1l = sb("b1l", [P, 1])
        linw = sb("linw", [P, 3, D])
        ew1 = sb("ew1", [ED, 3, D])
        ew2 = sb("ew2", [P, 3, D])
        eb1 = sb("eb1", [P, 3])
        eb2 = sb("eb2", [1, 3, 4, D])
        lnw_c = sb("lnw_c", [P, 3])
        lnb_c = sb("lnb_c", [P, 3])
        WX = sb("WX", [P, 4, GW + 2])
        gb_c = sb("gb_c", [P, 4])
        b2_r, b2l_r, lnw_r, lnb_r, gout_r, c2_r = (
            sb(n, [P, D]) for n in ("b2_r", "b2l_r", "lnw_r", "lnb_r", "gout_r", "c2_r"))
        bias_r = sb("bias_r", [P, 3, D])

        rel, deg, wgcn, winv, wl2, dis2, te1, te2, te3, te4 = (
            sb(n, [P, T]) for n in ("rel", "deg", "wgcn", "winv", "wl2", "dis2", "te1", "te2", "te3", "te4"))
        idx_all, idx_l2, idx_dst, idx_x, idx_src = (
            sb(n, [P, T], i32) for n in ("idx_all", "idx_l2", "idx_dst", "idx_x", "idx_src"))
        node_val = sb("node_val", [P, T, 2])
        node_src = sb("node_src", [P, T, 2])
        relL = sb("relL", [1, T])
        cont = sb("cont", [1, T])

        A4 = sb("A4", [HALF, 4, 2, P])
        FI4 = sb("FI4", [HALF, 4, 2, P])
        CM = sb("CM", [HALF, 2, P])
        LMB = sb("LMB", [HALF, 2, P])
        R2 = sb("R2", [HALF, 2, 2, P])
        V = sb("V", [HALF, 6, 2, P])
        W4 = sb("W4", [HALF, 4, 2, P])
        HS = sb("HS", [HALF, 4, 2, P])
        ends = sb("ends", [HALF, 2, 12])
        rfa = sb("rfa", [4, T])
        rb = sb("rb", [2, T])
        crow = sb("crow", [4, T + 1])
        brow = sb("brow", [2, T + 1])
        cb = sb("cb", [HALF, 2, 4])

        G = sb("G", [P, T, GW])
        NV = sb("NV", [P, 4, T])
        ES = sb("ES", [P, 2, T])
        PT = sb("PT", [P, 4, T])

        M = sb("M", [P, 4, GW])
        idx_slot = sb("idx_slot", [P, 8], i32)
        node_slot = sb("node_slot", [P, 4, 2])
        MP = sb("MP", [P, 4, GW])
        S = sb("S", [P, 4, P])
        LO = sb("LO", [1, 4, P])
        C = sb("C", [1, GW])
        OWN = sb("OWN", [P, 4, GW])
        XIN = sb("XIN", [P, 4, D])
        U = sb("U", [P, 4, D])
        GN = sb("GN", [P, 4, D])
        UT = sb("UT", [P, QR])
        OT = sb("OT", [P, QR])
        H1T = sb("H1T", [P, 2, QR])
        RO = sb("RO", [P, 4, GW])
        RB = sb("RB", [P, 4, D])
        stat = sb("stat", [P, 4, 6])
        mv = sb("mv", [P, 4, 2])
        sd, rs, nb = (sb(n, [P, 4]) for n in ("sd", "rs", "nb"))
        den = sb("den", [P, 4, 2])
        ea_in = sb("ea_in", [P, 4, ED])
        ea_last = sb("ea_last", [P, 4, ED])
        eat = sb("eat", [ED, QR])

        Gf = G[:, :, :].rearrange("p t c -> p (t c)")

        def lend(at, *shape):
            size = 1
            for n in shape:
                size *= n
            v = Gf[:, at:at + size]
            return v if len(shape) == 1 else v.rearrange("p (x y) -> p x y", x=shape[0])

        ROOM = 6144
        PXT = [lend(b * ROOM, 4, D) for b in (0, 1)]
        PGN = [lend(b * ROOM + 512, 4, D) for b in (0, 1)]
        PTT = [lend(b * ROOM + 1024, QR) for b in (0, 1)]
        PHT = [lend(b * ROOM + 1536, 2, QR) for b in (0, 1)]
        PRO = [[lend(b * ROOM + 2560 + r * 520, 4, GW) for r in (0, 1)] for b in (0, 1)]
        PYT = [lend(b * ROOM + 3600, 4, D) for b in (0, 1)]
        PST = [lend(b * ROOM + 4112, 4, 6) for b in (0, 1)]
        PMV = [lend(b * ROOM + 4136, 4, 2) for b in (0, 1)]
        PSD = [lend(b * ROOM + 4144, 4) for b in (0, 1)]
        PRS = [lend(b * ROOM + 4148, 4) for b in (0, 1)]
        PNB = [lend(b * ROOM + 4152, 4) for b in (0, 1)]
        av = [lend(2 * ROOM + v * D, D) for v in range(8)]
        avt = lend(2 * ROOM + 8 * D, D)
        FILL = lend(2 * ROOM + 9 * D, 1000)
        raw2 = lend(2 * ROOM + 3000, 2, P + 2)[0:HALF].bitcast(i32)
        srcraw = lend(2 * ROOM + 4000, 2, P)[0:HALF].bitcast(i32)
        x2f = lend(2 * ROOM + 5000, 2, P + 2)[0:HALF]

        PS = ctx.enter_context(nc.psum_tensor("PS", [P, 8, 512], f32))

        def bank(b, w=D, k=4):
            return PS[:, b, 0:k * w].rearrange("p (j c) -> p j c", j=k)

        def pair(b, w=GW):
            return PS[:, b:b + 2, :].rearrange("p b (j c) -> p (b j) c", j=2)[:, :, 0:w]

        def wide(v, n):
            return v.unsqueeze(2).to_broadcast([v.shape[0], v.shape[1], n])

        def on4(v):
            return v.unsqueeze(1).to_broadcast([P, 4, D])

        c_load = sem("c_load")
        c_pool = sem("c_pool")
        p_set = sem("p_set")
        p_raw = sem("p_raw")
        p_fill = sem("p_fill")
        p_dve = sem("p_dve")
        p_v = sem("p_v")
        p_p = sem("p_p")
        p_va = sem("p_va")
        p_a = sem("p_a")
        p_ready = sem("p_ready")
        e_ld = sem("e_ld")
        e_tr = sem("e_tr")
        e_cp = sem("e_cp")
        e_st = sem("e_st")
        n_idx = sem("n_idx")
        n_val = sem("n_val")
        n_sc = [sem(f"n_sc{j}") for j in range(4)]
        n_g = [sem(f"n_g{j}") for j in range(4)]
        n_cp = sem("n_cp")

        def psteps(name, order, by=1):
            return [Steps(sem(f"{name}{b}"), {"P": order}, by, 0, ["P"], PLAIN_TURNS) for b in (0, 1)]

        q_ld = psteps("q_ld", ("x",), 16)
        q_v = psteps("q_v", ("stats1", "aggr1", "rs1", "nb1", "h1b", "xb", "x1", "stats2", "aggr2", "rs2", "nb2",
                             "y", "yx", "x3", "stats3", "aggr3", "rs3", "nb3", "r8", "r9", "r10", "r11", "xo", "xf"))
        q_p = psteps("q_p", ("gT1", "h1a", "h1b", "t1", "gT2", "h2", "rA", "rB", "gT3", "h8", "r8", "h9", "r9",
                             "h10", "r10", "r11"))
        q_a = psteps("q_a", ("sd1", "g1", "gT1", "h1a", "t1", "sd2", "g2", "gT2", "h2", "rA", "sd3", "g3", "gT3",
                             "h8", "h9", "h10"))
        q_st = {t: psteps(f"q_st{t}_", (t,), 16) for t in ("t1", "t2", "t3", "t4", "t8", "t9", "t10", "t11", "out")}

        AGG = ("C1", "C2", "S1", "S2", "LA", "LB", "GA", "GZ")
        four = ("t3", "t2", "t1", "t0")

        def steps(name, order, by=1, start=0):
            return Steps(sem(name), order, by, start)

        idxed = steps("idxed", {k: ("slots",) for k in KINDS})
        gat = [steps(f"gat{j}", {k: ("rows",) for k in KINDS}, 16) for j in range(4)]
        m_free = steps("m_free", {k: four for k in ("C1", "C2", "S1", "S2", "GA", "GZ")}, 1, 4)
        sel = steps("sel", {k: four for k in AGG})
        agg = steps("agg", {k: four for k in AGG}, 1, 4)
        carry = steps("carry", {k: four for k in AGG})
        mprod = steps("mprod", {"LA": four, "LB": four, "GA": ("quad",), "GZ": ("quad",)}, 1, 4)
        own = steps("own", {k: ("rows",) for k in ("C1", "C2", "S1", "S2", "GA", "GZ")}, 16)
        xin = steps("xin", {k: ("rows",) for k in ("C2", "S2", "LB", "GZ")}, 16)
        eas = steps("eas", {k: ("attr",) for k in ("LA", "LB")}, 16)
        st_t = steps("st_t", {k: ("table",) for k in KINDS if k != "GZ"}, 16)
        st_x = steps("st_x", {k: ("rows",) for k in ("X", "C2", "S1", "S2", "LB")}, 16)
        st_o = [steps(f"st_o{j}", {"GZ": ("rows",)}, 16) for j in range(4)]
        vd = steps("vd", {
            "X": ("copy", "stats", "aggr", "rs", "nb"),
            "C1": ("own", "comb", "h1b"),
            "C2": ("own", "comb", "bias", "x", "stats", "aggr", "rs", "nb"),
            "S1": ("comb", "rB"),
            "S2": ("comb", "x", "stats", "aggr", "rs", "nb"),
            "LA": ("comb", "stats", "aggr", "rs", "nb"),
            "LB": ("comb", "stats", "aggr", "rs", "nb", "lnw", "lnb", "x", "stats2", "aggr2", "rs2", "nb2"),
            "GA": ("den", "comb", "dene", "rden", "norm"),
            "GZ": ("den", "comb", "dene", "rden", "norm", "bias", "x")})
        pd = steps("pd", {
            "C1": ("uT", "h1a", "h1b", "rows"), "S1": ("oT", "uT", "hT", "rA", "rB"), "S2": ("gT", "rows"),
            "LA": ("nT", "rows"), "LB": ("gT", "rows"), "GA": ("uT", "rows")}, 1, 4)
        ad = steps("ad", {
            "X": ("sd", "g"), "C1": ("uT", "h1a", "rows"), "C2": ("sd", "g"),
            "S1": ("oT", "uT", "hT", "rA"), "S2": ("sd", "g", "gT", "rows"),
            "LA": ("sd", "n", "nT", "rows"), "LB": ("sd", "n", "sd2", "g", "gT", "rows", "nv"),
            "GA": ("uT", "rows", "nv")})
        pd_e = steps("pd_e", {k: ("rT", "em") for k in ("LA", "LB")})
        ad_e = steps("ad_e", {k: ("rT",) for k in ("LA", "LB")})
        hself = steps("hself", {"GA": ("own",), "GZ": ("own",)})
        m_p = Steps(sem("m_p"), {"mid": ("scan", "rowmax", "getmax", "rowown", "getown", "tile")}, 1, 0, ["mid"], 0)
        m_v = Steps(sem("m_v"), {"mid": ("es", "max", "maxes", "own", "owns", "power", "weights")}, 1, 0, ["mid"], 0)
        m_a = Steps(sem("m_a"), {"mid": ("exp",)}, 1, 0, ["mid"], 0)
        m_idx = sem("m_idx")
        ATTENTION = [s for s, k in enumerate(KINDS) if k in ("GA", "GZ")]

        OWN_SRC = {1: TAB[1], 2: TAB[2], 3: TAB[3], 4: SELF, 8: TAB[8], 9: TAB[9], 10: TAB[10], 11: TAB[11]}
        X_SRC = {2: XR[0], 4: XR[2], 7: XR[4], 11: XR[7]}
        X_DST = {0: XR[0], 2: XR[2], 3: SELF, 4: XR[4], 7: XR[7]}
        STAGES = list(enumerate(KINDS))
        LAST = QUADS - 1

        def quad_rows(t, Q):
            return t[ds(Q * QR, QR), :].rearrange("(j p) c -> p j c", p=P)

        def plain_rows(t, base):
            return t[ds(base, QR), :].rearrange("(p j) c -> p j c", j=4)

        def stage_stored(eng, s):
            for st in (st_t, st_x):
                if KINDS[s] in st.order:
                    eng.wait_ge(st.sem, st.at(s, LAST, st.order[KINDS[s]][-1]))

        def alone(eng, *waits):
            for _, value in waits:
                eng.compute_val(value)
            eng.wait_ge(c_pool, 13)
            for sm, value in waits:
                eng.wait_ge(sm, value)

        loads = [(w1[:, :], a["L0_gnn_W1"]), (w2[:, :, :], a["L0_gnn_W2"].rearrange("(b p) c -> p b c", p=P)),
                 (b1[:, :], a["L0_gnn_b1"].rearrange("(b p) -> p b", p=P)),
                 (w1l[:, :], a["L1_gnn_w1l"]), (w1r[:, :], a["L1_gnn_w1r"]),
                 (w2l[:, :], a["L1_gnn_w2l"]), (w2r[:, :], a["L1_gnn_w2r"]),
                 (b1l[:, :], a["L1_gnn_b1l"].rearrange("(p o) -> p o", o=1)),
                 (linw[:, :, :], a["L2_gnn_lin_w"].rearrange("l p c -> p l c")),
                 (ew1[:, :, :], a["L2_gnn_edge_w1"].rearrange("l p c -> p l c")),
                 (ew2[:, :, :], a["L2_gnn_edge_w2"].rearrange("l p c -> p l c")),
                 (eb1[:, :], a["L2_gnn_edge_b1"].rearrange("l p -> p l")),
                 (lnw_c[:, :], a["L2_gnn_ln_w"].rearrange("l p -> p l")),
                 (lnb_c[:, :], a["L2_gnn_ln_b"].rearrange("l p -> p l")),
                 (WX[:, 0, 0:D], a["L3_gnn_W_in"]), (WX[:, 1, 0:D], a["L3_gnn_W_h"][0]),
                 (WX[:, 2, 0:D], a["L3_gnn_W_h"][1]), (WX[:, 3, 0:D], a["L3_gnn_W_out"]),
                 (gb_c[:, 0:1], a["L3_gnn_b_in"].rearrange("(p o) -> p o", o=1)),
                 (gb_c[:, 1:3], a["L3_gnn_b_h"].rearrange("l p -> p l")),
                 (b2_r[:, :], a["L0_gnn_b2"].partition_broadcast(P)),
                 (b2l_r[:, :], a["L1_gnn_b2l"].partition_broadcast(P)),
                 (lnw_r[:, :], a["L2_gnn_ln_w"][2].partition_broadcast(P)),
                 (lnb_r[:, :], a["L2_gnn_ln_b"][2].partition_broadcast(P)),
                 (gout_r[:, :], a["L3_gnn_b_out"].partition_broadcast(P))]
        loads += [(bias_r[:, l, :], a["L2_gnn_bias"][l].partition_broadcast(P)) for l in range(3)]
        loads += [(eb2[0:1, l, j, :], a["L2_gnn_edge_b2"][l:l + 1, :]) for l in range(3) for j in range(4)]
        attn = [a["L3_gnn_a_src_in"], a["L3_gnn_a_dst_in"], a["L3_gnn_a_src_h"][0], a["L3_gnn_a_dst_h"][0],
                a["L3_gnn_a_src_h"][1], a["L3_gnn_a_dst_h"][1], a["L3_gnn_a_src_out"], a["L3_gnn_a_dst_out"]]
        loads += [(av[v], attn[v].rearrange("h c -> (h c)").partition_broadcast(P)) for v in range(8)]
        LOADED = 16 * len(loads)

        x, src, dst, ea = a["x"], a["src"], a["dst"], a["edge_attr_16"]
        BLOCK1 = HALF * P
        TAIL = (T - 1) * P

        def span(t, start, rows, step, cols):
            return bass.AP(tensor=t.tensor, offset=start, ap=[[step, rows], [1, cols]])


        def attention_middle(dve, v, link, s):
            mid = ATTENTION.index(s)

            def flat(t):
                return t.rearrange("q k b p -> q (k b p)")

            def leaky(t):
                link(v.scalar_tensor_tensor(t, t, 0.2, t, ALU.mult, ALU.max))

            dve.wait_ge(m_free.sem, m_free.at(s, LAST, "t0"))
            v.tensor_copy(ES[:, :, :], G[:, :, D:GW].rearrange("p t h -> p h t")).then_inc(m_v.sem, 1)
            dve.wait_ge(m_p.sem, m_p.at(0, mid, "scan"))
            link(v.tensor_copy(V[:, :, :, :].rearrange("q k b p -> q (k b p)"),
                               PS[0:HALF, 4:7, :].rearrange("q x c -> q (x c)")))
            v.tensor_tensor_scan(flat(HS[:, 0:2])[:, ::-1], flat(R2[:, :])[:, ::-1], flat(V[:, 0:2])[:, ::-1], -BIG,
                                 ALU.add, ALU.max).then_inc(m_v.sem, 1)
            dve.wait_ge(m_p.sem, m_p.at(0, mid, "rowmax"))
            v.tensor_tensor_scan(brow[:, 0:T][:, ::-1], rb[:, :][:, ::-1], PS[0:2, 7, 0:T][:, ::-1], -BIG,
                                 ALU.add, ALU.max).then_inc(m_v.sem, 1)
            dve.wait_ge(m_p.sem, m_p.at(0, mid, "getmax"))
            for b in (0, 1):
                link(v.tensor_copy(cb[:, b, 0:2], PS[0:HALF, 4, 4 * b:4 * b + 2]))
            for k in (0, 1):
                for b in (0, 1):
                    i = v.scalar_tensor_tensor(HS[:, k, b], LMB[:, b, :], cb[:, b, k:k + 1], HS[:, k, b],
                                               ALU.add, ALU.max)
            link(i)
            top, own_ = W4[:, 0:2], V[:, 2:4]
            link(v.tensor_tensor(top, HS[:, 0:2], own_, ALU.max))
            v.tensor_copy(W4[:, 2:4], V[:, 4:6])
            link(v.tensor_tensor(top, top, V[:, 4:6], ALU.add))
            leaky(flat(top))
            link(v.tensor_tensor(own_, own_, V[:, 4:6], ALU.add))
            leaky(flat(own_))
            link(v.tensor_tensor(own_, own_, top, ALU.subtract))
            link(v.tensor_tensor(flat(W4[:, :]), flat(W4[:, :]), flat(FI4[:, :]), ALU.mult))
            v.tensor_tensor_scan(flat(HS[:, :]), flat(A4[:, :]), flat(W4[:, :]), 0.0, ALU.mult,
                                 ALU.add).then_inc(m_v.sem, 1)
            dve.wait_ge(m_p.sem, m_p.at(0, mid, "rowown"))
            v.tensor_tensor_scan(crow[:, 1:T + 1], rfa[:, :], PS[0:4, 7, 0:T], 0.0, ALU.mult,
                                 ALU.add).then_inc(m_v.sem, 1)
            dve.wait_ge(m_p.sem, m_p.at(0, mid, "getown"))
            for b in (0, 1):
                link(v.tensor_copy(cb[:, b, :], PS[0:HALF, 4, 4 * b:4 * b + 4]))
            for k in range(4):
                for b in (0, 1):
                    i = v.scalar_tensor_tensor(HS[:, k, b], CM[:, b, :], cb[:, b, k:k + 1], HS[:, k, b],
                                               ALU.mult, ALU.add)
            link(i)
            es = V[:, 0:2]
            link(v.tensor_tensor(es, es, HS[:, 2:4], ALU.add))
            leaky(flat(es))
            v.tensor_tensor(es, es, HS[:, 0:2], ALU.subtract).then_inc(m_v.sem, 1)
            dve.wait_ge(m_p.sem, m_p.at(0, mid, "tile"))
            v.tensor_copy(PT[:, 0:2, :].rearrange("p k t -> p (k t)"), PS[:, 4, 0:2 * T])
            v.tensor_copy(PT[:, 2:4, :].rearrange("p k t -> p (k t)"), PS[:, 5, 0:2 * T]).then_inc(m_v.sem, 1)

        def attention_turns(pe, turn, s):
            mid = ATTENTION.index(s)
            pe.wait_ge(m_v.sem, m_v.at(0, mid, "es"))
            for k in range(6):
                for b in (0, 1):
                    c = 2 * k + b
                    row = (ES[:, k, :] if k < 2 else NV[:, k - 2, :])[:, HALF * b:HALF * b + HALF]
                    i = turn(PS[0:HALF, 4 + c // 4, P * (c % 4):P * (c % 4) + P], row)
            i.then_inc(m_p.sem, 1)
            pe.wait_ge(m_v.sem, m_v.at(0, mid, "max"))
            for b in (0, 1):
                i = turn(PS[0:2, 7, HALF * b:HALF * b + HALF], HS[:, 0:2, b, 0])
            i.then_inc(m_p.sem, 1)
            pe.wait_ge(m_v.sem, m_v.at(0, mid, "maxes"))
            for b in (0, 1):
                i = turn(PS[0:HALF, 4, 4 * b:4 * b + 2], brow[:, HALF * b + 1:HALF * b + HALF + 1])
            i.then_inc(m_p.sem, 1)
            pe.wait_ge(m_v.sem, m_v.at(0, mid, "own"))
            for b in (0, 1):
                i = turn(PS[0:4, 7, HALF * b:HALF * b + HALF], HS[:, :, b, P - 1])
            i.then_inc(m_p.sem, 1)
            pe.wait_ge(m_v.sem, m_v.at(0, mid, "owns"))
            for b in (0, 1):
                i = turn(PS[0:HALF, 4, 4 * b:4 * b + 4], crow[:, HALF * b:HALF * b + HALF])
            i.then_inc(m_p.sem, 1)
            pe.wait_ge(m_a.sem, m_a.at(0, mid, "exp"))
            for k in range(4):
                for b in (0, 1):
                    at = T * (k % 2) + HALF * b
                    i = turn(PS[:, 4 + k // 2, at:at + HALF], W4[:, k, b])
            i.then_inc(m_p.sem, 1)
            pe.wait_ge(m_v.sem, m_v.at(0, mid, "weights"))

        def attention_exp(act, f, s):
            mid = ATTENTION.index(s)
            act.wait_ge(m_v.sem, m_v.at(0, mid, "power"))
            f(W4[:, :, :, :].rearrange("q k b p -> q (k b p)"), V[:, 0:4].rearrange("q k b p -> q (k b p)"),
              ACT.Exp).then_inc(m_a.sem, 1)

        block = ctx.enter_context(nc.Block())

        @block.sync
        def _(sp):
            for o, i in loads:
                sp.dma_start(o, i, allow_slow_non_contiguous=True).then_inc(c_load, 16)
            sp.wait_ge(p_set, 3)
            sp.dma_start(raw2[0:1, 0, 1:P + 2], span(dst, 0, 1, 1, P + 1)).then_inc(p_raw, 16)
            sp.dma_start(raw2[1:HALF, 0, :], span(dst, P - 1, HALF - 1, P, P + 2)).then_inc(p_raw, 16)
            sp.dma_start(raw2[0:HALF - 1, 1, :], span(dst, BLOCK1 - 1, HALF - 1, P, P + 2)).then_inc(p_raw, 16)
            sp.dma_start(raw2[HALF - 1:HALF, 1, 0:E - TAIL + 1],
                         span(dst, TAIL - 1, 1, 1, E - TAIL + 1)).then_inc(p_raw, 16)
            sp.dma_start(srcraw[:, 0, :], span(src, 0, HALF, P, P)).then_inc(p_raw, 16)
            sp.dma_start(srcraw[0:HALF - 1, 1, :], span(src, BLOCK1, HALF - 1, P, P)).then_inc(p_raw, 16)
            sp.dma_start(srcraw[HALF - 1:HALF, 1, 0:E - TAIL], span(src, TAIL, 1, 1, E - TAIL)).then_inc(p_raw, 16)
            sp.wait_ge(c_pool, 11)
            sp.dma_start(NODE.rearrange("(p a) c -> p (a c)", p=100), FILL[0:100, :]).then_inc(p_fill, 16)

            with sp.Fori(0, LAST) as n:
                sp.wait_ge(e_tr, n)
                sp.dma_start(ea_in[:, :, :], ea[ds(n * QR, QR), :].rearrange("(p j) c -> p j c", j=4)).then_inc(e_ld, 16)
                alone(sp, (e_cp, n + 1))
                sp.dma_start(EAT[:, ds(n * QR, QR)], eat[:, :]).then_inc(e_st, 16)
            sp.dma_start(ea_last[0:(E - LAST * QR) // 4, :, :],
                         ea[LAST * QR:E, :].rearrange("(p j) c -> p j c", j=4)).then_inc(e_ld, 16)
            sp.wait_ge(e_cp, QUADS)
            sp.dma_start(EAT[:, LAST * QR:EP], eat[:, :]).then_inc(e_st, 16)
            sp.wait_ge(e_st, 16 * QUADS)

            def plain(m, bases):
                for b in (0, 1):
                    alone(sp, (q_v[b].sem, q_v[b].at(0, m)), (q_st["out"][b].sem, q_st["out"][b].at(0, m)))
                    sp.dma_start(PXT[b], plain_rows(x, bases[b])).then_inc(q_ld[b].sem, 16)

                def keep(name, tab, b, ready, rows, shift=EP):
                    sp.wait_ge(*ready)
                    if b and isinstance(m, int):
                        sp.wait_ge(q_st[name][0].sem, q_st[name][0].at(0, m, name))
                    sp.dma_start(plain_rows(tab, bases[b] + shift), rows).then_inc(q_st[name][b].sem, 16)

                for b in (0, 1):
                    keep("t1", TAB[1], b, (q_a[b].sem, q_a[b].at(0, m, "g1")), PGN[b])
                for b in (0, 1):
                    keep("t2", TAB[2], b, (q_a[b].sem, q_a[b].at(0, m, "t1")), PRO[b][0][:, :, 0:D])
                for b in (0, 1):
                    keep("t3", TAB[3], b, (q_a[b].sem, q_a[b].at(0, m, "g2")), PGN[b])
                for b in (0, 1):
                    keep("t4", TAB[4], b, (q_a[b].sem, q_a[b].at(0, m, "rA")), PRO[b][1][:, :, 0:D])
                for t, r in ((8, 0), (9, 1), (10, 0), (11, 1)):
                    for b in (0, 1):
                        keep(f"t{t}", TAB[t], b, (q_v[b].sem, q_v[b].at(0, m, f"r{t}")), PRO[b][r])
                for b in (0, 1):
                    keep("out", out, b, (q_v[b].sem, q_v[b].at(0, m, "xf")), PXT[b], 0)

            with sp.Fori(0, PLAIN_TURNS - 1) as m:
                plain(m, (m * (2 * QR), m * (2 * QR) + QR))
            for t in q_st.values():
                for b in (0, 1):
                    sp.wait_ge(t[b].sem, 16 * (PLAIN_TURNS - 1))
            plain(PLAIN_TURNS - 1, ((PLAIN_QUADS - 2) * QR, N - QR))

            for s, kind in STAGES:
                if s:
                    stage_stored(sp, s - 1)

                def quad(n):
                    return LAST - n if isinstance(n, int) else n * (-1) + LAST

                def load_attr(n):
                    alone(sp, (pd_e.sem, pd_e.at(s, n) if isinstance(n, int) and n == 0 else pd_e.last(s, n, "rT")))
                    sp.dma_start(eat[:, :], EAT[:, ds(quad(n) * QR, QR)]).then_inc(eas.sem, 16)

                def load(n):
                    first = isinstance(n, int) and n == 0
                    if kind in own.order:
                        used, step = {"C1": (vd, "own"), "C2": (vd, "own"), "S1": (pd, "oT")}.get(kind, (vd, "comb"))
                        sp.wait_ge(used.sem, used.at(s, n) if first else used.last(s, n, step))
                        w = GW if kind in hself.order else D
                        sp.dma_start(OWN[:, :, 0:w], quad_rows(OWN_SRC[s], quad(n))).then_inc(own.sem, 16)
                    if kind in xin.order:
                        sp.wait_ge(vd.sem, vd.at(s, n) if first else vd.last(s, n, "x"))
                        sp.dma_start(XIN[:, :, :], quad_rows(X_SRC[s], quad(n))).then_inc(xin.sem, 16)

                def store(n):
                    xstep = {"X": "copy", "C2": "x", "S2": "x", "LB": "x"}.get(kind)
                    if xstep:
                        sp.wait_ge(vd.sem, vd.at(s, n, xstep))
                        sp.dma_start(quad_rows(X_DST[s], quad(n)), U[:, :, :]).then_inc(st_x.sem, 16)
                    astep, rows = {"X": ("g", GN[:, :, :]), "C2": ("g", GN[:, :, :]), "C1": ("rows", RO[:, :, 0:D]),
                                   "S1": ("rA", RO[:, :, 0:D]), "S2": ("rows", RO[:, :, 0:D]),
                                   "LA": ("rows", RO[:, :, 0:D]), "LB": ("rows", RO[:, :, :]),
                                   "GA": ("rows", RO[:, :, :])}[kind]
                    sp.wait_ge(ad.sem, ad.at(s, n, astep))
                    sp.dma_start(quad_rows(TAB[s + 1], quad(n)), rows).then_inc(st_t.sem, 16)
                    if kind == "S1":
                        sp.wait_ge(vd.sem, vd.at(s, n, "rB"))
                        sp.dma_start(quad_rows(X_DST[s], quad(n)), RB[:, :, :]).then_inc(st_x.sem, 16)

                if kind == "X":
                    with sp.Fori(0, QUADS) as n:
                        store(n)
                elif kind == "GZ":
                    load(0)
                    with sp.Fori(0, LAST) as n:
                        load(n + 1)
                elif kind in eas.order:
                    load_attr(0)
                    load_attr(1)
                    load(0)
                    with sp.Fori(0, LAST - 1) as n:
                        load_attr(n + 2)
                        load(n + 1)
                        store(n)
                    load(LAST)
                    store(LAST - 1)
                    store(LAST)
                else:
                    load(0)
                    with sp.Fori(0, LAST) as n:
                        load(n + 1)
                        store(n)
                    store(LAST)

        @block.gpsimd
        def _(pool):
            g = nc.gpsimd
            g.memset(ident[:, :], 0.0).then_inc(c_pool, 1)
            g.iota(iota_row[:, :], [[1, P]], base=0, channel_multiplier=0,
                   allow_small_or_imprecise_dtypes=True).then_inc(c_pool, 1)
            g.memset(eps[:, :], LN_EPS).then_inc(c_pool, 1)
            g.memset(ones_row[:, :], 1.0).then_inc(c_pool, 1)
            pool.wait_ge(c_pool, 4)
            g.affine_select(out=ident[:, :], in_=ident[:, :], compare_op=ALU.not_equal, fill=1.0, base=0,
                            pattern=[[-1, P]], channel_multiplier=1).then_inc(c_pool, 1)
            g.memset(raw2[:, :, :], 60000).then_inc(p_set, 1)
            g.memset(srcraw[:, :, :], 0).then_inc(p_set, 1)
            pool.wait_ge(p_set, 2)
            g.memset(raw2[:, 1, P + 1:P + 2], 70000).then_inc(p_set, 1)
            g.iota(W4[:, 0, :, :], [[BLOCK1, 2], [1, P]], base=0, channel_multiplier=P,
                   allow_small_or_imprecise_dtypes=True).then_inc(c_pool, 1)
            g.iota(W4[:, 1, :, :], [[BLOCK1, 2], [0, P]], base=0, channel_multiplier=P,
                   allow_small_or_imprecise_dtypes=True).then_inc(c_pool, 1)
            g.iota(te1[:, :], [[P, T]], base=0, channel_multiplier=1,
                   allow_small_or_imprecise_dtypes=True).then_inc(c_pool, 1)
            g.memset(ea_last[:, :, :], 0.0).then_inc(c_pool, 1)
            fill2 = FILL[0:100, :].rearrange("p (a c) -> p a c", c=2)
            g.memset(fill2[:, :, 0:1], -1.0).then_inc(c_pool, 1)
            g.memset(fill2[:, :, 1:2], 0.0).then_inc(c_pool, 1)
            g.memset(crow[:, :], 0.0).then_inc(c_pool, 1)
            g.memset(brow[:, :], -BIG).then_inc(c_pool, 1)
            g.memset(C[:, :], 0.0).then_inc(m_free.sem, 4)
            g.memset(M[:, :, :], 0.0).then_inc(agg.sem, 4)
            g.memset(den[:, :, :], 0.0).then_inc(mprod.sem, 4)
            g.memset(GN[:, :, :], 0.0).then_inc(pd.sem, 4)

            pool.wait_ge(p_ready, 1)
            pool.wait_ge(p_fill, 16)
            with pool.Fori(0, QUADS) as n:
                for j in range(4):
                    pool.wait_ge(n_sc[j], n * 16)
                g.tensor_copy(idx_slot[:, 0:4], idx_dst[:, ds(n * 4, 4)]).then_inc(n_idx, 1)
                g.tensor_copy(node_slot[:, :, :], node_val[:, ds(n * 4, 4), :]).then_inc(n_val, 1)
                alone(pool, (n_idx, n + 1), (n_val, n + 1))
                for j in range(4):
                    g.indirect_dma_start(NODE, bass.IndirectOffsetOnAxis(ap=idx_slot[:, j:j + 1], axis=0),
                                         node_slot[:, j, :], None, bounds_check=N - 1,
                                         oob_is_err=False).then_inc(n_sc[j], 16)
            for j in range(4):
                pool.wait_ge(n_sc[j], 16 * QUADS)
            with pool.Fori(0, QUADS) as n:
                g.tensor_copy(idx_slot[:, 0:4], idx_src[:, ds(n * 4, 4)]).then_inc(n_idx, 1)
                alone(pool, (n_idx, n + (QUADS + 1)))
                for j in range(4):
                    g.indirect_dma_start(node_slot[:, j, :], None, NODE,
                                         bass.IndirectOffsetOnAxis(ap=idx_slot[:, j:j + 1], axis=0)).then_inc(n_g[j], 16)
                for j in range(4):
                    pool.wait_ge(n_g[j], n * 16 + 16)
                g.tensor_copy(node_src[:, ds(n * 4, 4), :], node_slot[:, :, :]).then_inc(n_cp, 1)
                pool.wait_ge(n_cp, n + 1)

            def gather_quad(s, table, idx, w, n, half):
                Q4 = n * (-4) + 4 * LAST
                if not isinstance(n, int) or n > 1:
                    for j in range(4):
                        pool.wait_ge(gat[j].sem, gat[j].at(s, n) - (16 if s else 0))
                at = 4 * half
                g.tensor_copy(idx_slot[:, at:at + 4], idx[:, ds(Q4, 4)]).then_inc(idxed.sem, 1)
                for j in (3, 2, 1, 0):
                    if KINDS[s] == "X":
                        used = (vd.sem, vd.at(s, n))
                    else:
                        free = mprod if KINDS[s] in ("LA", "LB") else m_free
                        used = (free.sem, free.last(s, n, f"t{j}"))
                    alone(pool, used, *([(idxed.sem, idxed.at(s, n, "slots"))] if j == 3 else []))
                    g.indirect_dma_start(M[:, j, 0:w], None, table,
                                         bass.IndirectOffsetOnAxis(ap=idx_slot[:, at + j:at + j + 1], axis=0)
                                         ).then_inc(gat[j].sem, 16)

            def gathers(s, table, idx, w):
                with pool.Fori(0, QUADS // 2) as m:
                    gather_quad(s, table, idx, w, m * 2, 0)
                    gather_quad(s, table, idx, w, m * 2 + 1, 1)
                gather_quad(s, table, idx, w, LAST, 0)

            gathers(0, x, idx_x, D)
            pool.wait_ge(p_ready, 2)
            for t in q_st.values():
                for b in (0, 1):
                    pool.wait_ge(t[b].sem, 16 * PLAIN_TURNS)
            for s, kind in STAGES[1:]:
                stage_stored(pool, s - 1)
                if kind not in hself.order:
                    gathers(s, TAB[s], idx_l2 if kind in ("LA", "LB") else idx_all, D)
                    continue
                gathers(s, TAB[s], idx_all, GW)
                pool.wait_ge(m_v.sem, m_v.at(0, ATTENTION.index(s), "weights"))

                def messages(n):
                    Q4 = n * (-4) + 4 * LAST
                    for h in (0, 1):
                        gh = G[:, ds(Q4, 4), 64 * h:64 * h + 64]
                        g.tensor_tensor(gh, gh, wide(PT[:, h, ds(Q4, 4)], 64), ALU.mult)
                    g.tensor_copy(G[:, ds(Q4, 4), D:GW],
                                  PT[:, 0:2, ds(Q4, 4)].rearrange("p h j -> p j h")).then_inc(mprod.sem, 1)

                def own_rows(n):
                    Q4 = n * (-4) + 4 * LAST
                    pool.wait_ge(own.sem, own.at(s, n, "rows"))
                    for h in (0, 1):
                        oh = OWN[:, :, 64 * h:64 * h + 64]
                        last = g.tensor_tensor(oh, oh, wide(PT[:, 2 + h, ds(Q4, 4)], 64), ALU.mult)
                    last.then_inc(hself.sem, 1)
                    if kind == "GZ":
                        for j in range(4):
                            pool.wait_ge(st_o[j].sem, st_o[j].at(s, n))
                        g.tensor_copy(idx_slot[:, 0:4], idx_dst[:, ds(Q4, 4)]).then_inc(m_idx, 1)
                        alone(pool, (m_idx, n + 1), (vd.sem, vd.at(s, n, "x")))
                        for j in range(4):
                            g.indirect_dma_start(out, bass.IndirectOffsetOnAxis(ap=idx_slot[:, j:j + 1], axis=0),
                                                 RO[:, j, 0:D], None, bounds_check=N - 1,
                                                 oob_is_err=False).then_inc(st_o[j].sem, 16)

                messages(0)
                with pool.Fori(0, LAST) as n:
                    messages(n + 1)
                    own_rows(n)
                own_rows(LAST)
            for j in range(4):
                pool.wait_ge(st_o[j].sem, 16 * QUADS)

        @block.vector
        def _(dve):
            v = nc.vector
            count = [0]

            def link(ins):
                count[0] += 1
                ins.then_inc(p_dve, 1)
                dve.wait_ge(p_dve, count[0])

            def two(t):
                return t.rearrange("q b p -> q (b p)")

            dve.wait_ge(p_raw, 7 * 16)
            dve.wait_ge(c_pool, 13)
            link(v.tensor_copy(x2f[:, :, :], raw2[:, :, :]))
            dst2 = x2f[:, :, 1:P + 1]
            FI, A, last, cm0, lm1, lm0, lm = FI4[:, 0], A4[:, 0], V[:, 0], V[:, 1], V[:, 2], V[:, 3], V[:, 4]
            v.tensor_tensor(FI, dst2, x2f[:, :, 0:P], ALU.not_equal)
            v.tensor_tensor(last, dst2, x2f[:, :, 2:P + 2], ALU.not_equal)
            v.memset(cm0, 0.0)
            link(v.memset(lm0, 0.0))
            v.tensor_scalar(A, FI, -1.0, 1.0, ALU.mult, ALU.add)
            v.tensor_scalar(lm1, last, -1.0, 1.0, ALU.mult, ALU.add)
            v.tensor_scalar(R2[:, 0], last, -BIG, None, ALU.mult)
            link(v.tensor_tensor(W4[:, 2], FI, W4[:, 0], ALU.mult))
            v.tensor_copy(cm0[:, :, 0:1], A[:, :, 0:1])
            link(v.tensor_copy(lm0[:, :, P - 1:P], lm1[:, :, P - 1:P]))
            v.memset(A[:, :, 0:1], 0.0)
            v.memset(lm1[:, :, P - 1:P], 0.0)
            link(v.memset(R2[:, 0, :, P - 1:P], -BIG))
            v.tensor_tensor_scan(two(CM[:, :, :]), two(A), two(cm0), 0.0, ALU.mult, ALU.add)
            v.tensor_tensor_scan(two(lm)[:, ::-1], two(lm1)[:, ::-1], two(lm0)[:, ::-1], 0.0, ALU.mult, ALU.add)
            v.tensor_tensor_scan(two(HS[:, 0]), two(A), two(W4[:, 2]), 0.0, ALU.mult, ALU.add)
            v.tensor_tensor_scan(two(HS[:, 1])[:, ::-1], two(R2[:, 0])[:, ::-1], two(W4[:, 0])[:, ::-1], -BIG,
                                 ALU.add, ALU.max)
            for k in (1, 2, 3):
                v.tensor_copy(FI4[:, k], FI)
                v.tensor_copy(A4[:, k], A)
            link(v.tensor_copy(R2[:, 1], R2[:, 0]))
            link(v.tensor_scalar(LMB[:, :, :], lm, BIG, -BIG, ALU.mult, ALU.add))
            v.tensor_copy(ends[:, :, 0:1], HS[:, 0, :, P - 1:P])
            v.tensor_copy(ends[:, :, 1:2], HS[:, 1, :, 0:1])
            v.tensor_copy(ends[:, :, 2:6], CM[:, :, P - 1:P].to_broadcast([HALF, 2, 4]))
            v.tensor_copy(ends[:, :, 6:8], LMB[:, :, 0:1].to_broadcast([HALF, 2, 2]))
            v.tensor_copy(ends[:, :, 8:9], lm[:, :, P - 1:P]).then_inc(p_v, 1)
            dve.wait_ge(p_p, 1)
            v.tensor_copy(rfa[:, :], PS[0:4, 2, 0:T])
            v.tensor_copy(rb[:, :], PS[0:2, 3, 0:T])
            link(v.tensor_copy(cont[:, :], PS[0:1, 4, 0:T]))
            v.tensor_tensor_scan(crow[0:1, 1:T + 1], rfa[0:1, :], PS[0:1, 0, 0:T], 0.0, ALU.mult, ALU.add)
            v.tensor_tensor_scan(brow[0:1, 0:T][:, ::-1], rb[0:1, :][:, ::-1], PS[0:1, 1, 0:T][:, ::-1], -BIG,
                                 ALU.add, ALU.max).then_inc(p_v, 1)
            dve.wait_ge(p_p, 2)
            link(v.tensor_copy(cb[:, 0, 0:2], PS[0:HALF, 5, 0:2]))
            link(v.tensor_copy(cb[:, 1, 0:2], PS[0:HALF, 6, 0:2]))
            for b in (0, 1):
                v.scalar_tensor_tensor(W4[:, 2, b], CM[:, b, :], cb[:, 0, b:b + 1], HS[:, 0, b], ALU.mult, ALU.add)
                last_ = v.scalar_tensor_tensor(W4[:, 3, b], LMB[:, b, :], cb[:, 1, b:b + 1], HS[:, 1, b],
                                               ALU.add, ALU.max)
            link(last_)
            v.scalar_tensor_tensor(V[:, 1], W4[:, 3], 1.0, W4[:, 2], ALU.add, ALU.subtract)
            link(v.tensor_tensor(V[:, 0], W4[:, 2], W4[:, 1], ALU.subtract))
            v.tensor_scalar_max(V[:, 2], V[:, 0], 0.0)
            v.tensor_copy(V[:, 3], dst2)
            v.tensor_copy(V[:, 4], srcraw[:, :, :]).then_inc(p_v, 1)

            dve.wait_ge(c_load, LOADED)
            for l in range(4):
                for k in (0, 1):
                    link(v.tensor_tensor(avt, WX[:, l, 0:D], av[2 * l + k], ALU.mult))
                    link(v.tensor_reduce(WX[:, l, D + 2 * k:D + 2 * k + 2], avt.rearrange("p (h c) -> p h c", h=2),
                                         AX.X, ALU.add))
            link(v.bn_stats(stat[:, 0, :], bias_r[:, 2, :]))
            link(v.bn_aggr(mv[:, 0, :], stat[:, 0, :]))
            v.tensor_copy(te4[:, 0:1], mv[:, 0, 1:2]).then_inc(p_va, 1)
            dve.wait_ge(p_a, 1)
            link(v.reciprocal(rs[:, 0:1], sd[:, 0:1]))
            link(v.tensor_scalar(c2_r[:, :], bias_r[:, 2, :], mv[:, 0, 0:1], rs[:, 0:1], ALU.subtract, ALU.mult))
            link(v.tensor_tensor(c2_r[:, :], c2_r[:, :], lnw_r[:, :], ALU.mult))
            link(v.tensor_tensor(c2_r[:, :], c2_r[:, :], lnb_r[:, :], ALU.add))
            link(v.tensor_scalar_max(c2_r[:, :], c2_r[:, :], 0.0))

            dve.wait_ge(p_p, 3)
            v.tensor_copy(deg[:, :], PS[:, 0, 0:T])
            v.tensor_copy(rel[:, :], PS[:, 1, 0:T])
            v.tensor_copy(te3[:, :], PS[:, 3, 0:T])
            v.tensor_copy(idx_src[:, :], PS[:, 4, 0:T])
            v.tensor_copy(relL[:, :], PS[0:1, 5, 0:T])
            link(v.tensor_scalar(te2[:, :], PS[:, 2, 0:T], -FAR, FAR, ALU.mult, ALU.add))
            link(v.scalar_tensor_tensor(relL[:, :], relL[:, :], 1.0, cont[:, :], ALU.add, ALU.mult))
            link(v.tensor_scalar_add(relL[:, :], relL[:, :], -1.0))
            v.tensor_tensor(idx_dst[:, :], te2[:, :], te3[:, :], ALU.add)
            v.tensor_scalar_min(idx_x[:, :], te3[:, :], float(N - 1))
            v.tensor_copy(node_val[:, :, 0], te1[:, :])
            v.tensor_copy(node_val[:, :, 1], deg[:, :]).then_inc(p_ready, 1)

            def norm_sums(q, m, b, x_, k):
                for j in range(4):
                    i = v.bn_stats(PST[b][:, j, :], x_[:, j, :])
                i.then_inc(q.sem, 1)
                alone(dve, (q.sem, q.at(0, m, f"stats{k}")))
                for j in range(4):
                    i = v.bn_aggr(PMV[b][:, j, :], PST[b][:, j, :])
                i.then_inc(q.sem, 1)

            def norm_coef(q, m, b, k):
                dve.wait_ge(q_a[b].sem, q_a[b].at(0, m, f"sd{k}"))
                v.reciprocal(PRS[b], PSD[b]).then_inc(q.sem, 1)
                dve.wait_ge(q.sem, q.at(0, m, f"rs{k}"))
                v.scalar_tensor_tensor(PNB[b], PMV[b][:, :, 0], -1.0, PRS[b], ALU.mult, ALU.mult).then_inc(q.sem, 1)

            def plain(m):
                for b in (0, 1):
                    dve.wait_ge(q_ld[b].sem, q_ld[b].at(0, m, "x"))
                    norm_sums(q_v[b], m, b, PXT[b], 1)
                for b in (0, 1):
                    norm_coef(q_v[b], m, b, 1)
                for b in (0, 1):
                    q = q_v[b]
                    dve.wait_ge(q_p[b].sem, q_p[b].at(0, m, "h1b"))
                    v.tensor_scalar(PHT[b][:, 1, :], PS[:, 4 * b + 2, :], b1[:, 1:2], 0.0, ALU.add,
                                    ALU.max).then_inc(q.sem, 1)
                for b in (0, 1):
                    q = q_v[b]
                    dve.wait_ge(q_a[b].sem, q_a[b].at(0, m, "g1"))
                    v.tensor_tensor(PXT[b], PXT[b], on4(b2_r[:, :]), ALU.add).then_inc(q.sem, 1)
                    dve.wait_ge(q.sem, q.at(0, m, "xb"))
                    dve.wait_ge(q_a[b].sem, q_a[b].at(0, m, "t1"))
                    v.tensor_tensor(PXT[b], PXT[b], PRO[b][0][:, :, 0:D], ALU.add).then_inc(q.sem, 1)
                    dve.wait_ge(q.sem, q.at(0, m, "x1"))
                    norm_sums(q, m, b, PXT[b], 2)
                for b in (0, 1):
                    norm_coef(q_v[b], m, b, 2)
                for b in (0, 1):
                    q = q_v[b]
                    dve.wait_ge(q_p[b].sem, q_p[b].at(0, m, "rB"))
                    v.tensor_tensor(PYT[b], bank(4 * b + 3), on4(b2l_r[:, :]), ALU.add).then_inc(q.sem, 1)
                    dve.wait_ge(q.sem, q.at(0, m, "y"))
                    dve.wait_ge(q_a[b].sem, q_a[b].at(0, m, "g2"))
                    v.scalar_tensor_tensor(PXT[b], PYT[b], 0.0, PXT[b], ALU.max, ALU.add).then_inc(q.sem, 1)
                    dve.wait_ge(q.sem, q.at(0, m, "yx"))
                    v.tensor_tensor(PXT[b], PXT[b], on4(c2_r[:, :]), ALU.add).then_inc(q.sem, 1)
                    dve.wait_ge(q.sem, q.at(0, m, "x3"))
                    norm_sums(q, m, b, PXT[b], 3)
                for b in (0, 1):
                    norm_coef(q_v[b], m, b, 3)
                for t, r, before in ((8, 0, "t2"), (9, 1, "t4"), (10, 0, "t8"), (11, 1, "t9")):
                    for b in (0, 1):
                        q = q_v[b]
                        st = q_st[before][b]
                        dve.wait_ge(st.sem, st.at(0, m, before))
                        dve.wait_ge(q_p[b].sem, q_p[b].at(0, m, f"r{t}"))
                        v.tensor_copy(PRO[b][r], pair(4 * b + 2)).then_inc(q.sem, 1)
                for b in (0, 1):
                    q = q_v[b]
                    dve.wait_ge(q_a[b].sem, q_a[b].at(0, m, "g3"))
                    v.tensor_tensor(PXT[b], PXT[b], on4(gout_r[:, :]), ALU.add).then_inc(q.sem, 1)
                    dve.wait_ge(q.sem, q.at(0, m, "xo"))
                    v.tensor_tensor(PXT[b], PXT[b], PRO[b][1][:, :, 0:D], ALU.add).then_inc(q.sem, 1)

            with dve.Fori(0, PLAIN_TURNS - 1) as m:
                plain(m)
            plain(PLAIN_TURNS - 1)

            dve.wait_ge(n_cp, QUADS)
            pos, degs = node_src[:, :, 0], node_src[:, :, 1]
            v.tensor_copy(te4[:, :], idx_src[:, :])
            link(v.tensor_scalar(te2[:, :], pos, 0.0, None, ALU.is_lt))
            link(v.scalar_tensor_tensor(te3[:, :], te4[:, :], float(EP + 1), te2[:, :], ALU.add, ALU.mult))
            link(v.tensor_tensor(idx_all[:, :], pos, te3[:, :], ALU.add))
            link(v.scalar_tensor_tensor(te3[:, :], te1[:, :], 1.0, te2[:, :], ALU.add, ALU.mult))
            link(v.tensor_tensor(idx_l2[:, :], pos, te3[:, :], ALU.add))
            link(v.tensor_scalar_add(dis2[:, :], deg[:, :], 1.0))
            link(v.scalar_tensor_tensor(te3[:, :], degs, 1.0, dis2[:, :], ALU.add, ALU.mult))
            link(v.scalar_tensor_tensor(te4[:, :], degs, 1.0, deg[:, :], ALU.max, ALU.mult))
            v.tensor_scalar(te2[:, :], te2[:, :], -1.0, 1.0, ALU.mult, ALU.add).then_inc(p_va, 1)
            dve.wait_ge(p_a, 2)
            link(v.reciprocal(wgcn[:, :], te3[:, :]))
            link(v.reciprocal(te4[:, :], te4[:, :]))
            link(v.tensor_tensor(wl2[:, :], te4[:, :], te2[:, :], ALU.mult))
            link(v.reciprocal(winv[:, :], deg[:, :]))
            link(v.reciprocal(dis2[:, :], dis2[:, :]))
            v.memset(te4[:, 0:1], 0.0).then_inc(p_ready, 1)

            def select(s, n, j):
                Q4 = n * (-4) + 4 * LAST
                weight = {"C": wgcn, "S": winv}.get(KINDS[s][0])
                dve.wait_ge(agg.sem, agg.last(s, n, f"t{0 if j == 3 else j}"))
                if j == 3:
                    v.tensor_tensor(LO[:, :, :], iota_row[0:1, :].unsqueeze(1).to_broadcast([1, 4, P]),
                                    wide(relL[:, ds(Q4, 4)], P), ALU.is_equal)
                if weight is None:
                    i = v.tensor_scalar(S[:, j, :], iota_row[:, :], rel[:, ds(Q4 + j, 1)], None, ALU.is_equal)
                else:
                    i = v.tensor_scalar(S[:, j, :], iota_row[:, :], rel[:, ds(Q4 + j, 1)], weight[:, ds(Q4 + j, 1)],
                                        ALU.is_equal, ALU.mult)
                i.then_inc(sel.sem, 1)

            def message(s, n, j):
                if j == 3:
                    dve.wait_ge(pd_e.sem, pd_e.at(s, n, "em"))
                dve.wait_ge(gat[j].sem, gat[j].at(s, n, "rows"))
                v.scalar_tensor_tensor(MP[:, j, 0:D], M[:, j, 0:D], wl2[:, ds(n * (-4) + (4 * LAST + j), 1)],
                                       bank(5)[:, j, :], ALU.mult, ALU.add).then_inc(mprod.sem, 1)

            def step(s, n, ins, name, *meanwhile):
                ins.then_inc(vd.sem, 1)
                for work in meanwhile:
                    work()
                alone(dve, (vd.sem, vd.at(s, n, name)))

            def sums(s, n, x_, k="", w1_=(), w2_=()):
                for j in range(4):
                    i = v.bn_stats(stat[:, j, :], x_[:, j, :])
                step(s, n, i, "stats" + k, *w1_)
                for j in range(4):
                    i = v.bn_aggr(mv[:, j, :], stat[:, j, :])
                i.then_inc(vd.sem, 1)
                for work in w2_:
                    work()

            def coef(s, n, k="", w1_=()):
                dve.wait_ge(ad.sem, ad.at(s, n, "sd" + k))
                step(s, n, v.reciprocal(rs[:, :], sd[:, :]), "rs" + k, *w1_)
                v.scalar_tensor_tensor(nb[:, :], mv[:, :, 0], -1.0, rs[:, :], ALU.mult, ALU.mult).then_inc(vd.sem, 1)

            def aggregated(s, n):
                dve.wait_ge(agg.sem, agg.at(s, n, "t0"))
                dve.wait_ge(carry.sem, carry.at(s, n, "t0"))

            A4ps = PS[:, 0:4, 0:D]

            def finish(s, kind, n, ahead):
                Q4 = n * (-4) + 4 * LAST
                s3, s2, s1, s0 = ahead
                if kind in ("C1", "C2"):
                    dve.wait_ge(own.sem, own.at(s, n, "rows"))
                    if kind == "C1":
                        dve.wait_ge(pd.sem, pd.last(s, n, "uT"))
                    else:
                        dve.wait_ge(st_x.sem, st_x.at(s, n))
                        dve.wait_ge(ad.sem, ad.at(s, n))
                    step(s, n, v.tensor_tensor(U[:, :, :], OWN[:, :, 0:D], wide(dis2[:, ds(Q4, 4)], D), ALU.mult),
                         "own")
                    aggregated(s, n)
                if kind == "C1":
                    v.tensor_tensor(U[:, :, :], A4ps, U[:, :, :], ALU.add).then_inc(vd.sem, 1)
                    for work in (s3, s2, s1, s0):
                        work()
                    dve.wait_ge(pd.sem, pd.at(s, n, "h1b"))
                    v.tensor_scalar(H1T[:, 1, :], PS[:, 6, :], b1[:, 1:2], 0.0, ALU.add, ALU.max).then_inc(vd.sem, 1)
                elif kind == "C2":
                    step(s, n, v.tensor_tensor(U[:, :, :], A4ps, U[:, :, :], ALU.add), "comb", s3)
                    step(s, n, v.tensor_tensor(U[:, :, :], U[:, :, :], on4(b2_r[:, :]), ALU.add), "bias", s2)
                    dve.wait_ge(xin.sem, xin.at(s, n, "rows"))
                    step(s, n, v.tensor_tensor(U[:, :, :], U[:, :, :], XIN[:, :, :], ALU.add), "x", s1)
                    sums(s, n, U, "", (s0,))
                    coef(s, n)
                elif kind == "S1":
                    dve.wait_ge(pd.sem, pd.last(s, n, "uT"))
                    aggregated(s, n)
                    v.tensor_copy(U[:, :, :], A4ps).then_inc(vd.sem, 1)
                    for work in (s3, s2, s1, s0):
                        work()
                    dve.wait_ge(pd.sem, pd.at(s, n, "rB"))
                    dve.wait_ge(st_x.sem, st_x.at(s, n))
                    v.tensor_tensor(RB[:, :, :], bank(4), on4(b2l_r[:, :]), ALU.add).then_inc(vd.sem, 1)
                elif kind == "S2":
                    dve.wait_ge(own.sem, own.at(s, n, "rows"))
                    dve.wait_ge(st_x.sem, st_x.at(s, n))
                    dve.wait_ge(ad.sem, ad.last(s, n, "g"))
                    aggregated(s, n)
                    step(s, n, v.tensor_tensor(U[:, :, :], A4ps, OWN[:, :, 0:D], ALU.add), "comb", s3)
                    dve.wait_ge(xin.sem, xin.at(s, n, "rows"))
                    step(s, n, v.scalar_tensor_tensor(U[:, :, :], U[:, :, :], 0.0, XIN[:, :, :], ALU.max, ALU.add),
                         "x", s2)
                    sums(s, n, U, "", (s1,), (s0,))
                    coef(s, n)
                elif kind in ("LA", "LB"):
                    dve.wait_ge(ad.sem, ad.last(s, n, "n" if kind == "LA" else "g"))
                    if kind == "LB":
                        dve.wait_ge(st_x.sem, st_x.at(s, n))
                    aggregated(s, n)
                    step(s, n, v.tensor_tensor(U[:, :, :], A4ps, on4(bias_r[:, s - 5, :]), ALU.add), "comb", s3)
                    sums(s, n, U, "", (s2,), (s1,))
                    coef(s, n, "", (s0,))
                else:
                    aggregated(s, n)
                    ps = PT[:, 2:4, ds(Q4, 4)].rearrange("p h j -> p j h")
                    v.tensor_tensor(den[:, :, :], PS[:, 0:4, D:GW], ps, ALU.add).then_inc(vd.sem, 1)
                    dve.wait_ge(hself.sem, hself.at(s, n, "own"))
                    if kind == "GA":
                        dve.wait_ge(pd.sem, pd.last(s, n, "uT"))
                    step(s, n, v.tensor_tensor(U[:, :, :], A4ps, OWN[:, :, 0:D], ALU.add), "comb", s3)
                    step(s, n, v.tensor_scalar_add(den[:, :, :], den[:, :, :], 1e-16), "dene", s2)
                    step(s, n, v.reciprocal(den[:, :, :], den[:, :, :]), "rden", s1)
                    for h in (0, 1):
                        uh = U[:, :, 64 * h:64 * h + 64]
                        i = v.tensor_tensor(uh, uh, wide(den[:, :, h], 64), ALU.mult)
                    if kind == "GA":
                        i.then_inc(vd.sem, 1)
                        s0()
                    else:
                        step(s, n, i, "norm", s0)
                        step(s, n, v.tensor_tensor(U[:, :, :], U[:, :, :], on4(gout_r[:, :]), ALU.add), "bias")
                        dve.wait_ge(xin.sem, xin.at(s, n, "rows"))
                        for j in range(4):
                            dve.wait_ge(st_o[j].sem, st_o[j].at(s, n))
                        v.tensor_tensor(RO[:, :, 0:D], U[:, :, :], XIN[:, :, :], ALU.add).then_inc(vd.sem, 1)

            def finish_lb(s, n):
                dve.wait_ge(ad.sem, ad.at(s, n, "n"))
                step(s, n, v.tensor_tensor(U[:, :, :], GN[:, :, :], on4(lnw_r[:, :]), ALU.mult), "lnw")
                step(s, n, v.tensor_tensor(U[:, :, :], U[:, :, :], on4(lnb_r[:, :]), ALU.add), "lnb")
                dve.wait_ge(xin.sem, xin.at(s, n, "rows"))
                step(s, n, v.scalar_tensor_tensor(U[:, :, :], U[:, :, :], 0.0, XIN[:, :, :], ALU.max, ALU.add), "x")
                sums(s, n, U, "2")
                coef(s, n, "2")

            for s, kind in STAGES:
                if kind == "X":
                    with dve.Fori(0, QUADS) as n:
                        for j in (3, 2, 1, 0):
                            dve.wait_ge(gat[j].sem, gat[j].at(s, n, "rows"))
                        dve.wait_ge(st_x.sem, st_x.at(s, n))
                        dve.wait_ge(ad.sem, ad.at(s, n))
                        step(s, n, v.tensor_copy(U[:, :, :], M[:, :, 0:D]), "copy")
                        sums(s, n, U)
                        coef(s, n)
                    continue
                if kind in hself.order:
                    with dve.Fori(0, QUADS) as n:
                        Q4 = n * (-4) + 4 * LAST
                        for j in (3, 2, 1, 0):
                            dve.wait_ge(gat[j].sem, gat[j].at(s, n, "rows"))
                            v.tensor_copy(G[:, ds(Q4 + j, 1), :], M[:, j:j + 1, :]).then_inc(m_free.sem, 1)
                    attention_middle(dve, v, link, s)

                def quad(n, more, s=s, kind=kind):
                    finish(s, kind, n, [(lambda j=j: select(s, n + 1, j)) if more else (lambda: None)
                                        for j in (3, 2, 1, 0)])
                    if more and kind in ("LA", "LB"):
                        for j in (3, 2, 1, 0):
                            message(s, n + 1, j)
                    if kind == "LB":
                        finish_lb(s, n)

                for j in (3, 2, 1, 0):
                    select(s, 0, j)
                if kind in ("LA", "LB"):
                    for j in (3, 2, 1, 0):
                        message(s, 0, j)
                with dve.Fori(0, LAST) as n:
                    quad(n, True)
                quad(LAST, False)

        @block.tensor
        def _(pe):
            def turn(o, i):
                k = i.shape[0]
                return nc.tensor.transpose(o, i, ident[0:k, 0:k])

            def mm(o, l, r, start=True, stop=True):
                return nc.tensor.matmul(o, l, r, start=start, stop=stop)

            pe.wait_ge(c_pool, 5)
            pe.wait_ge(p_v, 1)
            for c, (lo, hi) in enumerate(((0, 1), (1, 2), (2, 6), (6, 8), (8, 9))):
                for b in (0, 1):
                    i = turn(PS[0:hi - lo, c, HALF * b:HALF * b + HALF], ends[:, b, lo:hi])
            i.then_inc(p_p, 1)
            pe.wait_ge(p_v, 2)
            for b in (0, 1):
                turn(PS[0:HALF, 5, b:b + 1], crow[0:1, HALF * b:HALF * b + HALF])
                i = turn(PS[0:HALF, 6, b:b + 1], brow[0:1, HALF * b + 1:HALF * b + HALF + 1])
            i.then_inc(p_p, 1)
            pe.wait_ge(p_v, 3)
            for c, t in enumerate((V[:, 1], V[:, 2], FI4[:, 0], V[:, 3], V[:, 4])):
                for b in (0, 1):
                    turn(PS[:, c, HALF * b:HALF * b + HALF], t[:, b, :])
            for b in (0, 1):
                i = turn(PS[0:1, 5, HALF * b:HALF * b + HALF], V[:, 2, b, P - 1:P])
            i.then_inc(p_p, 1)
            def ea_turn(n, rows):
                for j in range(4):
                    i = turn(PS[0:ED, 7, P * j:P * j + P], rows[:, j, :])
                i.then_inc(e_tr, 1)

            with pe.Fori(0, LAST) as n:
                pe.wait_ge(e_ld, n * 16 + 16)
                pe.wait_ge(e_cp, n)
                ea_turn(n, ea_in)
            pe.wait_ge(e_ld, 16 * QUADS)
            pe.wait_ge(e_cp, LAST)
            ea_turn(LAST, ea_last)

            pe.wait_ge(c_load, LOADED)
            pe.wait_ge(p_ready, 1)

            def turn4(o, rows):
                for j in range(4):
                    i = turn(o[:, P * j:P * j + P], rows[:, j, :])
                return i

            def rows4(o, hT, w):
                for j in range(4):
                    i = mm(o[:, j, :], hT[:, P * j:P * j + P], w)
                return i

            def plain(m):
                for b in (0, 1):
                    pe.wait_ge(q_v[b].sem, q_v[b].at(0, m))
                    pe.wait_ge(q_a[b].sem, q_a[b].at(0, m, "g1"))
                    turn4(PS[:, 4 * b], PGN[b]).then_inc(q_p[b].sem, 1)
                for b in (0, 1):
                    pe.wait_ge(q_a[b].sem, q_a[b].at(0, m, "gT1"))
                    mm(PS[:, 4 * b + 1], w1[:, 0:P], PTT[b]).then_inc(q_p[b].sem, 1)
                    mm(PS[:, 4 * b + 2], w1[:, P:2 * P], PTT[b]).then_inc(q_p[b].sem, 1)
                for b in (0, 1):
                    pe.wait_ge(q_a[b].sem, q_a[b].at(0, m, "h1a"))
                    pe.wait_ge(q_v[b].sem, q_v[b].at(0, m, "h1b"))
                    for j in range(4):
                        for k in (0, 1):
                            i = mm(bank(4 * b + 3)[:, j, :], PHT[b][:, k, P * j:P * j + P], w2[:, k, :], k == 0, k == 1)
                    i.then_inc(q_p[b].sem, 1)
                for b in (0, 1):
                    pe.wait_ge(q_a[b].sem, q_a[b].at(0, m, "g2"))
                    turn4(PS[:, 4 * b], PGN[b]).then_inc(q_p[b].sem, 1)
                for b in (0, 1):
                    pe.wait_ge(q_a[b].sem, q_a[b].at(0, m, "gT2"))
                    mm(PS[:, 4 * b + 1], w1r[:, :], PTT[b]).then_inc(q_p[b].sem, 1)
                for b in (0, 1):
                    pe.wait_ge(q_a[b].sem, q_a[b].at(0, m, "h2"))
                    rows4(bank(4 * b + 2), PHT[b][:, 0, :], w2l[:, :]).then_inc(q_p[b].sem, 1)
                    rows4(bank(4 * b + 3), PHT[b][:, 0, :], w2r[:, :]).then_inc(q_p[b].sem, 1)
                for b in (0, 1):
                    pe.wait_ge(q_a[b].sem, q_a[b].at(0, m, "g3"))
                    turn4(PS[:, 4 * b], PGN[b]).then_inc(q_p[b].sem, 1)
                for l, hT, at in ((0, lambda b: PTT[b], "gT3"), (1, lambda b: PHT[b][:, 0, :], "h8"),
                                  (2, lambda b: PHT[b][:, 1, :], "h9"), (3, lambda b: PHT[b][:, 0, :], "h10")):
                    for b in (0, 1):
                        pe.wait_ge(q_a[b].sem, q_a[b].at(0, m, at))
                        if l < 3:
                            mm(PS[:, 4 * b + 1], WX[:, l, 0:D], hT(b)).then_inc(q_p[b].sem, 1)
                        if l:
                            pe.wait_ge(q_v[b].sem, q_v[b].at(0, m, f"r{7 + l}"))
                        rows4(pair(4 * b + 2), hT(b), WX[:, l, 0:GW]).then_inc(q_p[b].sem, 1)

            with pe.Fori(0, PLAIN_TURNS - 1) as m:
                plain(m)
            plain(PLAIN_TURNS - 1)
            for b in (0, 1):
                pe.wait_ge(q_v[b].sem, q_v[b].at(0, PLAIN_TURNS - 1, "xf"))

            def edge_terms(s, n):
                l = s - 5
                pe.wait_ge(eas.sem, eas.at(s, n, "attr"))
                mm(PS[:, 4, :], ew1[:, l, :], eat[:, :]).then_inc(pd_e.sem, 1)
                pe.wait_ge(ad_e.sem, ad_e.at(s, n, "rT"))
                pe.wait_ge(mprod.sem, mprod.at(s, n))
                mm(PS[:, 5, :], ones_row[:, :], eb2[0:1, l, :, :].rearrange("p j c -> p (j c)"), True, False)
                for j in range(4):
                    i = mm(bank(5)[:, j, :], H1T[:, 0, P * j:P * j + P], ew2[:, l, :], False, j == 3)
                i.then_inc(pd_e.sem, 1)

            def tile(s, n, j):
                kind = KINDS[s]
                w = GW if kind in hself.order else D
                if j == 3:
                    if kind in hself.order:
                        pe.wait_ge(mprod.sem, mprod.at(s, n, "quad"))
                    pe.wait_ge(vd.sem, vd.last(s, n, "comb"))
                A = PS[:, j, 0:w]
                pe.wait_ge(sel.sem, sel.at(s, n, f"t{j}"))
                if kind in hself.order:
                    mm(A, S[:, j, :], G[:, ds(n * (-4) + (4 * LAST + j), 1), :].rearrange("p t c -> p (t c)"), True, False)
                elif kind in ("LA", "LB"):
                    pe.wait_ge(mprod.sem, mprod.at(s, n, f"t{j}"))
                    mm(A, S[:, j, :], MP[:, j, 0:D], True, False)
                else:
                    pe.wait_ge(gat[j].sem, gat[j].at(s, n, "rows"))
                    mm(A, S[:, j, :], M[:, j, 0:D], True, False).then_inc(m_free.sem, 1)
                pe.wait_ge(carry.sem, carry.at(s, n) + (3 - j))
                mm(A, LO[:, j, :], C[:, 0:w], False, True).then_inc(agg.sem, 1)

            def finish(s, kind, n, ahead):
                t3, t2, t1, t0 = ahead

                def half_rows(o, hT, w, js):
                    for j in js:
                        i = mm(o[:, j, :], hT[:, P * j:P * j + P], w)
                    return i

                if kind == "C1":
                    pe.wait_ge(vd.sem, vd.at(s, n, "comb"))
                    turn4(PS[:, 4], U).then_inc(pd.sem, 1)
                    t3()
                    pe.wait_ge(ad.sem, ad.at(s, n, "uT"))
                    mm(PS[:, 5, :], w1[:, 0:P], UT[:, :]).then_inc(pd.sem, 1)
                    mm(PS[:, 6, :], w1[:, P:2 * P], UT[:, :]).then_inc(pd.sem, 1)
                    t2()
                    pe.wait_ge(ad.sem, ad.at(s, n, "h1a"))
                    pe.wait_ge(vd.sem, vd.at(s, n, "h1b"))
                    for j in range(4):
                        for k in (0, 1):
                            i = mm(bank(7)[:, j, :], H1T[:, k, P * j:P * j + P], w2[:, k, :], k == 0, k == 1)
                        if j == 1:
                            t1()
                    i.then_inc(pd.sem, 1)
                    t0()
                elif kind == "C2":
                    for t in ahead:
                        t()
                elif kind == "S1":
                    pe.wait_ge(own.sem, own.at(s, n, "rows"))
                    turn4(PS[:, 5], OWN[:, :, 0:D]).then_inc(pd.sem, 1)
                    pe.wait_ge(vd.sem, vd.at(s, n, "comb"))
                    turn4(PS[:, 4], U).then_inc(pd.sem, 1)
                    t3()
                    pe.wait_ge(ad.sem, ad.at(s, n, "uT"))
                    mm(PS[:, 6, :], w1l[:, :], UT[:, :], True, False)
                    mm(PS[:, 6, :], w1r[:, :], OT[:, :], False, True).then_inc(pd.sem, 1)
                    t2()
                    pe.wait_ge(ad.sem, ad.at(s, n, "hT"))
                    rows4(bank(7), H1T[:, 0, :], w2l[:, :]).then_inc(pd.sem, 1)
                    t1()
                    rows4(bank(4), H1T[:, 0, :], w2r[:, :]).then_inc(pd.sem, 1)
                    t0()
                elif kind == "S2":
                    for t in ahead:
                        t()
                    pe.wait_ge(ad.sem, ad.at(s, n, "g"))
                    turn4(PS[:, 4], GN).then_inc(pd.sem, 1)
                    pe.wait_ge(ad.sem, ad.at(s, n, "gT"))
                    rows4(bank(7), OT[:, :], linw[:, 0, :]).then_inc(pd.sem, 1)
                elif kind == "LA":
                    t3()
                    t2()
                    pe.wait_ge(ad.sem, ad.at(s, n, "n"))
                    turn4(PS[:, 6], GN).then_inc(pd.sem, 1)
                    t1()
                    pe.wait_ge(ad.sem, ad.at(s, n, "nT"))
                    half_rows(bank(7), OT[:, :], linw[:, s - 4, :], (0, 1))
                    t0()
                    half_rows(bank(7), OT[:, :], linw[:, s - 4, :], (2, 3)).then_inc(pd.sem, 1)
                elif kind == "LB":
                    for t in ahead:
                        t()
                    pe.wait_ge(ad.sem, ad.at(s, n, "g"))
                    turn4(PS[:, 4], GN).then_inc(pd.sem, 1)
                    pe.wait_ge(ad.sem, ad.at(s, n, "gT"))
                    rows4(pair(6, GW + 2), OT[:, :], WX[:, 0, :]).then_inc(pd.sem, 1)
                elif kind == "GA":
                    t3()
                    t2()
                    pe.wait_ge(vd.sem, vd.at(s, n, "norm"))
                    turn4(PS[:, 4], U).then_inc(pd.sem, 1)
                    t1()
                    pe.wait_ge(ad.sem, ad.at(s, n, "uT"))
                    half_rows(pair(6, GW + 2), OT[:, :], WX[:, s - 7, :], (0, 1))
                    t0()
                    half_rows(pair(6, GW + 2), OT[:, :], WX[:, s - 7, :], (2, 3)).then_inc(pd.sem, 1)
                else:
                    for t in ahead:
                        t()

            for s, kind in STAGES:
                if kind == "X":
                    continue
                pe.wait_ge(vd.sem, vd.at(s, 0))
                pe.wait_ge(ad.sem, ad.at(s, 0))
                if kind in hself.order:
                    attention_turns(pe, turn, s)

                def quad(n, more, s=s, kind=kind):
                    if more and kind in ("LA", "LB"):
                        edge_terms(s, n + 1)
                    finish(s, kind, n, [(lambda j=j: tile(s, n + 1, j)) if more else (lambda: None)
                                        for j in (3, 2, 1, 0)])

                if kind in ("LA", "LB"):
                    edge_terms(s, 0)
                for j in (3, 2, 1, 0):
                    tile(s, 0, j)
                with pe.Fori(0, LAST) as n:
                    quad(n, True)
                quad(LAST, False)

        @block.scalar
        def _(act):
            def f(o, i, fn, **kw):
                return nc.scalar.activation(o, i, fn, **kw)

            nc.scalar.preload_act_table(ACT.Sqrt)
            act.wait_ge(c_pool, 5)
            with act.Fori(0, QUADS) as n:
                act.wait_ge(e_tr, n + 1)
                act.wait_ge(e_st, n * 16)
                f(eat[:, :].rearrange("c (p j) -> c j p", j=4),
                  PS[0:ED, 7, :].rearrange("c (j p) -> c j p", j=4), ACT.Copy).then_inc(e_cp, 1)
            act.wait_ge(p_va, 1)
            f(sd[:, 0:1], te4[:, 0:1], ACT.Sqrt, bias=eps[:, :]).then_inc(p_a, 1)
            act.wait_ge(c_load, LOADED)

            def norm(m, b, k, before):
                act.wait_ge(q_v[b].sem, q_v[b].at(0, m, f"aggr{k}"))
                f(PSD[b], PMV[b][:, :, 1], ACT.Sqrt, bias=eps[:, :]).then_inc(q_a[b].sem, 1)

            def apply(m, b, k, st):
                act.wait_ge(q_v[b].sem, q_v[b].at(0, m, f"nb{k}"))
                act.wait_ge(*st)
                for j in range(4):
                    i = f(PGN[b][:, j, :], PXT[b][:, j, :], ACT.Relu, scale=PRS[b][:, j:j + 1], bias=PNB[b][:, j:j + 1])
                i.then_inc(q_a[b].sem, 1)

            def plain(m):
                for k in (1, 2, 3):
                    for b in (0, 1):
                        norm(m, b, k, None)
                    for b in (0, 1):
                        st = q_st["t1" if k == 2 else "t3"][b]
                        apply(m, b, k, (st.sem, st.at(0, m, st.order["P"][0]) if k > 1 else st.at(0, m)))
                    for b in (0, 1):
                        act.wait_ge(q_p[b].sem, q_p[b].at(0, m, f"gT{k}"))
                        f(PTT[b], PS[:, 4 * b, :], ACT.Copy).then_inc(q_a[b].sem, 1)
                    if k == 1:
                        for b in (0, 1):
                            act.wait_ge(q_p[b].sem, q_p[b].at(0, m, "h1a"))
                            f(PHT[b][:, 0, :], PS[:, 4 * b + 1, :], ACT.Relu, bias=b1[:, 0:1]).then_inc(q_a[b].sem, 1)
                        for b in (0, 1):
                            act.wait_ge(q_p[b].sem, q_p[b].at(0, m, "t1"))
                            st = q_st["t10"][b]
                            act.wait_ge(st.sem, st.at(0, m))
                            f(PRO[b][0][:, :, 0:D], bank(4 * b + 3), ACT.Copy).then_inc(q_a[b].sem, 1)
                    elif k == 2:
                        for b in (0, 1):
                            act.wait_ge(q_p[b].sem, q_p[b].at(0, m, "h2"))
                            f(PHT[b][:, 0, :], PS[:, 4 * b + 1, :], ACT.Relu, bias=b1l[:, 0:1]).then_inc(q_a[b].sem, 1)
                        for b in (0, 1):
                            act.wait_ge(q_p[b].sem, q_p[b].at(0, m, "rA"))
                            st = q_st["t11"][b]
                            act.wait_ge(st.sem, st.at(0, m))
                            act.wait_ge(q_v[b].sem, q_v[b].at(0, m))
                            f(PRO[b][1][:, :, 0:D], bank(4 * b + 2), ACT.Copy).then_inc(q_a[b].sem, 1)
                    else:
                        for l, name in ((0, "h8"), (1, "h9"), (2, "h10")):
                            for b in (0, 1):
                                act.wait_ge(q_p[b].sem, q_p[b].at(0, m, name))
                                f(PHT[b][:, l % 2, :], PS[:, 4 * b + 1, :], ACT.Relu,
                                  bias=gb_c[:, l:l + 1]).then_inc(q_a[b].sem, 1)

            with act.Fori(0, PLAIN_TURNS - 1) as m:
                plain(m)
            plain(PLAIN_TURNS - 1)
            act.wait_ge(p_va, 2)
            f(te3[:, :], te3[:, :], ACT.Sqrt)
            f(te4[:, :], te4[:, :], ACT.Sqrt).then_inc(p_a, 1)

            def sqrts(s, n, k=""):
                act.wait_ge(vd.sem, vd.at(s, n, "aggr" + k))
                f(sd[:, :], mv[:, :, 1], ACT.Sqrt, bias=eps[:, :]).then_inc(ad.sem, 1)

            def scaled(s, n, fn, k=""):
                act.wait_ge(vd.sem, vd.at(s, n, "nb" + k))
                for j in range(4):
                    i = f(GN[:, j, :], U[:, j, :], fn, scale=rs[:, j:j + 1], bias=nb[:, j:j + 1])
                i.then_inc(ad.sem, 1)

            def edge_relu(s, n):
                act.wait_ge(pd_e.sem, pd_e.at(s, n, "rT"))
                f(H1T[:, 0, :], PS[:, 4, :], ACT.Relu, bias=eb1[:, s - 5:s - 4]).then_inc(ad_e.sem, 1)

            def carried(s, n, *tiles):
                w = GW if KINDS[s] in hself.order else D
                for j in tiles:
                    act.wait_ge(agg.sem, agg.at(s, n, f"t{j}"))
                    f(C[:, 0:w], PS[0:1, j, 0:w], ACT.Copy).then_inc(carry.sem, 1)

            def finish(s, kind, n, ahead):
                Q4 = n * (-4) + 4 * LAST

                def out_rows():
                    act.wait_ge(st_t.sem, st_t.at(s, n))
                    act.wait_ge(pd.sem, pd.at(s, n, "rA" if kind == "S1" else "rows"))
                    f(RO[:, :, 0:D], bank(7), ACT.Copy).then_inc(ad.sem, 1)

                if kind == "C2":
                    ahead(3, 2, 1, 0)
                    sqrts(s, n)
                    act.wait_ge(st_t.sem, st_t.at(s, n))
                    scaled(s, n, ACT.Relu)
                elif kind == "C1":
                    act.wait_ge(pd.sem, pd.at(s, n, "uT"))
                    f(UT[:, :], PS[:, 4, :], ACT.Copy).then_inc(ad.sem, 1)
                    ahead(3)
                    act.wait_ge(pd.sem, pd.at(s, n, "h1a"))
                    f(H1T[:, 0, :], PS[:, 5, :], ACT.Relu, bias=b1[:, 0:1]).then_inc(ad.sem, 1)
                    ahead(2, 1, 0)
                    out_rows()
                elif kind == "S1":
                    act.wait_ge(pd.sem, pd.at(s, n, "oT"))
                    f(OT[:, :], PS[:, 5, :], ACT.Copy).then_inc(ad.sem, 1)
                    act.wait_ge(pd.sem, pd.at(s, n, "uT"))
                    f(UT[:, :], PS[:, 4, :], ACT.Copy).then_inc(ad.sem, 1)
                    ahead(3)
                    act.wait_ge(pd.sem, pd.at(s, n, "hT"))
                    f(H1T[:, 0, :], PS[:, 6, :], ACT.Relu, bias=b1l[:, 0:1]).then_inc(ad.sem, 1)
                    ahead(2, 1, 0)
                    out_rows()
                elif kind == "S2":
                    ahead(3, 2, 1, 0)
                    sqrts(s, n)
                    scaled(s, n, ACT.Relu)
                    act.wait_ge(pd.sem, pd.at(s, n, "gT"))
                    f(OT[:, :], PS[:, 4, :], ACT.Copy).then_inc(ad.sem, 1)
                    out_rows()
                elif kind == "LA":
                    l = s - 5
                    sqrts(s, n)
                    scaled(s, n, ACT.Identity)
                    ahead(3, 2)
                    act.wait_ge(pd.sem, pd.at(s, n, "nT"))
                    f(OT[:, :], PS[:, 6, :], ACT.Relu, scale=lnw_c[:, l:l + 1],
                      bias=lnb_c[:, l:l + 1]).then_inc(ad.sem, 1)
                    ahead(1, 0)
                    out_rows()
                elif kind == "LB":
                    sqrts(s, n)
                    scaled(s, n, ACT.Identity)
                    ahead(3, 2, 1, 0)
                    sqrts(s, n, "2")
                    scaled(s, n, ACT.Relu, "2")
                    act.wait_ge(pd.sem, pd.at(s, n, "gT"))
                    f(OT[:, :], PS[:, 4, :], ACT.Copy).then_inc(ad.sem, 1)
                elif kind == "GA":
                    ahead(3, 2)
                    act.wait_ge(pd.sem, pd.at(s, n, "uT"))
                    f(OT[:, :], PS[:, 4, :], ACT.Relu, bias=gb_c[:, s - 8:s - 7]).then_inc(ad.sem, 1)
                    ahead(1, 0)
                else:
                    ahead(3, 2, 1, 0)
                if kind in ("LB", "GA"):
                    act.wait_ge(st_t.sem, st_t.at(s, n))
                    act.wait_ge(pd.sem, pd.at(s, n, "rows"))
                    f(RO[:, :, :], pair(6), ACT.Copy).then_inc(ad.sem, 1)
                    f(NV[:, :, ds(Q4, 4)].rearrange("p k j -> p j k"), pair(6, GW + 2)[:, :, D:GW + 2],
                      ACT.Copy).then_inc(ad.sem, 1)

            for s, kind in STAGES:
                if kind == "X":
                    with act.Fori(0, QUADS) as n:
                        sqrts(s, n)
                        act.wait_ge(st_t.sem, st_t.at(s, n))
                        scaled(s, n, ACT.Relu)
                    continue
                if kind in hself.order:
                    attention_exp(act, f, s)

                def quad(n, more, s=s, kind=kind):
                    if more and kind in ("LA", "LB"):
                        edge_relu(s, n + 1)
                    finish(s, kind, n, (lambda *tiles: carried(s, n + 1, *tiles)) if more else (lambda *tiles: None))

                if kind in ("LA", "LB"):
                    edge_relu(s, 0)
                carried(s, 0, 3, 2, 1, 0)
                with act.Fori(0, LAST) as n:
                    quad(n, True)
                quad(LAST, False)


_INS = ["x", "src", "dst", "edge_attr_16", "L0_gnn_W1", "L0_gnn_b1", "L0_gnn_W2", "L0_gnn_b2",
        "L1_gnn_w1l", "L1_gnn_b1l", "L1_gnn_w1r", "L1_gnn_w2l", "L1_gnn_b2l", "L1_gnn_w2r",
        "L2_gnn_lin_w", "L2_gnn_edge_w1", "L2_gnn_edge_b1", "L2_gnn_edge_w2", "L2_gnn_edge_b2",
        "L2_gnn_bias", "L2_gnn_ln_w", "L2_gnn_ln_b", "L3_gnn_W_in", "L3_gnn_a_src_in", "L3_gnn_a_dst_in",
        "L3_gnn_b_in", "L3_gnn_W_h", "L3_gnn_a_src_h", "L3_gnn_a_dst_h", "L3_gnn_b_h", "L3_gnn_W_out",
        "L3_gnn_a_src_out", "L3_gnn_a_dst_out", "L3_gnn_b_out"]


def kernel(**inputs):
    import numpy as _np
    import concourse.bacc as _bacc
    from concourse.bass_utils import run_bass_kernel_spmd as _run

    nc = _bacc.Bacc("TRN2", target_bir_lowering=False, num_devices=1)
    arrays, aps = {}, {}
    for name in _INS:
        arr = _np.ascontiguousarray(inputs[name])
        arrays[f"in_{name}"] = arr
        aps[name] = nc.dram_tensor(f"in_{name}", arr.shape, mybir.dt.from_np(arr.dtype), kind="ExternalInput").ap()
    out = nc.dram_tensor("out_x", (N, D), mybir.dt.float32, kind="ExternalOutput").ap()
    gnn_program(nc, aps, out)
    r = _run(nc, [arrays], core_ids=[0])
    return r.results[0]["out_x"]
```

```python
import concourse.bass as bass
from concourse import mybir
from contextlib import ExitStack

P = 128
N = 50000
E = 25000
D = 128
ED = 16
T = -(-E // P)
EP = T * P
QUADS = T // 4
QR = 4 * P
HALF = T // 2
NROW = EP + N
GW = D + 2
BIG = 1.0e30
FAR = 1.0e6
LN_EPS = 1e-5
PLAIN_QUADS = -(-N // QR)
PLAIN_TURNS = PLAIN_QUADS // 2

PARTS = [(w, e) for w in range(3) for e in range(3)][:8]

KINDS = ["X", "C1", "C2", "S1", "S2", "LA", "LA", "LB", "GA", "GA", "GA", "GZ"]


class Steps:

    def __init__(self, sem, order, by=1, start=0, stages=KINDS, turns=QUADS):
        self.sem, self.order, self.by, self.start, self.stages, self.turns = sem, order, by, start, stages, turns

    def at(self, stage, turn, step=None):
        names = self.order.get(self.stages[stage], ())
        before = self.turns * sum(len(self.order.get(k, ())) for k in self.stages[:stage])
        k = 0 if step is None else names.index(step) + 1
        return turn * (self.by * len(names)) + (self.start + self.by * (before + k))

    def last(self, stage, turn, step):
        return self.at(stage, turn, step) - self.by * len(self.order[self.stages[stage]])


def gnn_program(nc, a, out):
    f32, i32, bf16 = mybir.dt.float32, mybir.dt.int32, mybir.dt.bfloat16
    ALU, ACT, AX = mybir.AluOpType, mybir.ActivationFunctionType, mybir.AxisListType
    ds = bass.ds
    ctx = ExitStack()
    with ctx:
        def sb(name, shape, dt=f32):
            return ctx.enter_context(nc.sbuf_tensor(name, shape, dt))

        def sem(name):
            return ctx.enter_context(nc.semaphore(name))

        def dram(name, shape, dt=f32):
            return nc.dram_tensor(name, shape, dt, kind="Internal").ap()

        TAB = {s: dram(f"table{s}", (NROW, D)) for s in (1, 2, 3, 4)}
        TAB.update({s: dram(f"table{s}", (EP, D)) for s in (5, 6, 7)})
        TAB.update({s: dram(f"table{s}", (NROW, GW)) for s in (8, 9, 10, 11)})
        XR = {s: dram(f"xrows{s}", (EP, D)) for s in (0, 2, 4, 7)}
        SELF = dram("sage_self", (EP, D))
        NODE = dram("node_info", (N, 2))
        EAT = dram("edge_attr_t", (8 * ED, EP), bf16)

        ident = sb("ident", [P, P])
        iota_row = sb("iota_row", [P, P])
        eps = sb("eps", [P, 1])
        ones_row = sb("ones_row", [3, P], bf16)
        w1 = sb("w1", [P, 256])
        w2 = sb("w2", [P, 2, D])
        b1 = sb("b1", [P, 2])
        w1l, w1r, w2l, w2r = (sb(n, [P, D]) for n in ("w1l", "w1r", "w2l", "w2r"))
        b1l = sb("b1l", [P, 1])
        linw = sb("linw", [P, 3, D])
        ew1 = sb("ew1", [8 * ED, 3, D], bf16)
        ew2 = sb("ew2", [P, 3, D])
        eb1 = sb("eb1", [P, 3])
        eb2 = sb("eb2", [3, 3, 4, D], bf16)
        lnw_c = sb("lnw_c", [P, 3])
        lnb_c = sb("lnb_c", [P, 3])
        WX = sb("WX", [P, 4, GW + 2])
        gb_c = sb("gb_c", [P, 4])
        b2_r, b2l_r, lnw_r, lnb_r, gout_r, c2_r = (
            sb(n, [P, D]) for n in ("b2_r", "b2l_r", "lnw_r", "lnb_r", "gout_r", "c2_r"))
        bias_r = sb("bias_r", [P, 3, D])

        rel, deg, wgcn, winv, wl2, dis2, te1, te2, te3, te4 = (
            sb(n, [P, T]) for n in ("rel", "deg", "wgcn", "winv", "wl2", "dis2", "te1", "te2", "te3", "te4"))
        idx_all, idx_l2, idx_dst, idx_x, idx_src = (
            sb(n, [P, T], i32) for n in ("idx_all", "idx_l2", "idx_dst", "idx_x", "idx_src"))
        relL = sb("relL", [1, T])
        cont = sb("cont", [1, T])

        A4 = sb("A4", [HALF, 4, 2, P])
        FI4 = sb("FI4", [HALF, 4, 2, P])
        CM = sb("CM", [HALF, 2, P])
        LMB = sb("LMB", [HALF, 2, P])
        R2 = sb("R2", [HALF, 2, 2, P])
        V = sb("V", [HALF, 6, 2, P])
        W4 = sb("W4", [HALF, 4, 2, P])
        HS = sb("HS", [HALF, 4, 2, P])
        ends = sb("ends", [HALF, 2, 12])
        rfa = sb("rfa", [4, T])
        rb = sb("rb", [2, T])
        crow = sb("crow", [4, T + 1])
        brow = sb("brow", [2, T + 1])
        cb = sb("cb", [HALF, 2, 4])

        G = sb("G", [P, T, GW])
        NV = sb("NV", [P, 4, T])
        ES = sb("ES", [P, 2, T])
        PT = sb("PT", [P, 4, T])

        M = sb("M", [P, 4, GW])
        idx_slot = sb("idx_slot", [P, 8], i32)
        node_slot = sb("node_slot", [P, 4, 2])
        S = sb("S", [P, 8, P])
        LO = sb("LO", [1, 8, P])
        C = sb("C", [1, GW])
        OWN = sb("OWN", [P, 4, GW])
        XIN = sb("XIN", [P, 4, D])
        U = sb("U", [P, 4, D])
        GN = sb("GN", [P, 4, D])
        UT = sb("UT", [P, QR])
        OT = sb("OT", [P, QR])
        H1T = sb("H1T", [P, 2, QR])
        RO = sb("RO", [P, 4, GW])
        RB = sb("RB", [P, 4, D])
        stat = sb("stat", [P, 4, 6])
        mv = sb("mv", [P, 4, 2])
        sd, rs, nb = (sb(n, [P, 4]) for n in ("sd", "rs", "nb"))
        den = sb("den", [P, 4, 2])
        ea_in = sb("ea_in", [P, 4, ED])
        ea_last = sb("ea_last", [P, 4, ED])
        eat = sb("eat", [8 * ED, QR], bf16)
        ea_parts = sb("ea_parts", [P, 2, 4, ED], bf16)

        Gf = G[:, :, :].rearrange("p t c -> p (t c)")

        def lend(at, *shape):
            size = 1
            for n in shape:
                size *= n
            v = Gf[:, at:at + size]
            return v if len(shape) == 1 else v.rearrange("p (x y) -> p x y", x=shape[0])

        ROOM = 6144
        PXT = [lend(b * ROOM, 4, D) for b in (0, 1)]
        PGN = [lend(b * ROOM + 512, 4, D) for b in (0, 1)]
        PTT = [lend(b * ROOM + 1024, QR) for b in (0, 1)]
        PHT = [lend(b * ROOM + 1536, 2, QR) for b in (0, 1)]
        PRO = [[lend(b * ROOM + 2560 + r * 520, 4, GW) for r in range(4)] for b in (0, 1)]
        PYT = [lend(b * ROOM + 4640, 4, D) for b in (0, 1)]
        PST = [lend(b * ROOM + 5152, 4, 6) for b in (0, 1)]
        PMV = [lend(b * ROOM + 5176, 4, 2) for b in (0, 1)]
        PSD = [lend(b * ROOM + 5184, 4) for b in (0, 1)]
        PRS = [lend(b * ROOM + 5188, 4) for b in (0, 1)]
        PNB = [lend(b * ROOM + 5192, 4) for b in (0, 1)]
        av = [lend(2 * ROOM + v * D, D) for v in range(8)]
        avt = lend(2 * ROOM + 8 * D, D)
        FILL = lend(2 * ROOM + 9 * D, 1000)
        raw2 = lend(2 * ROOM + 3000, 2, P + 2)[0:HALF].bitcast(i32)
        srcraw = lend(2 * ROOM + 4000, 2, P)[0:HALF].bitcast(i32)
        x2f = lend(2 * ROOM + 5000, 2, P + 2)[0:HALF]
        w_in, w_rest, w_sum = (lend(2 * ROOM + 6000 + k * 384, 3, D) for k in range(3))
        w_high, w_mid = (lend(2 * ROOM + 7200 + k * 192, 3, 64).bitcast(bf16) for k in (0, 1))
        b_in, b_rest, b_sum = (lend(2 * ROOM + 7600 + k * 384, 3, D)[0:3] for k in range(3))
        b_high, b_mid = (lend(2 * ROOM + 8800 + k * 192, 3, 64)[0:3].bitcast(bf16) for k in (0, 1))
        is_part = lend(2 * ROOM + 9200, 3)
        E8 = lend(2 * ROOM + 9300, 4, 8 * ED)
        node_val, node_src = (lend(2 * ROOM + 10000 + k * 2 * T, T, 2) for k in (0, 1))
        MP = lend(2 * ROOM + 11000, 8, D)
        e_rest = lend(2 * ROOM + 9300 + 512, 2, 4 * ED)

        PS = ctx.enter_context(nc.psum_tensor("PS", [P, 8, 512], f32))

        def bank(b, w=D, k=4):
            return PS[:, b, 0:k * w].rearrange("p (j c) -> p j c", j=k)

        def sums_of(h, j, w, rows=P):
            return PS[0:rows, 2 * h + j % 2, (j // 2) * GW:(j // 2) * GW + w]

        def all_sums(h, lo=0, hi=D):
            return PS[:, 2 * h:2 * h + 2, 0:2 * GW].rearrange("p b (k c) -> p k b c", k=2)[:, :, :, lo:hi]

        def by_bank(v):
            return v.rearrange("p (k b) c -> p k b c", b=2)

        def pair(b, w=GW):
            return PS[:, b:b + 2, :].rearrange("p b (j c) -> p (b j) c", j=2)[:, :, 0:w]

        def wide(v, n):
            return v.unsqueeze(2).to_broadcast([v.shape[0], v.shape[1], n])

        def on4(v):
            return v.unsqueeze(1).to_broadcast([P, 4, D])

        c_load = sem("c_load")
        c_pool = sem("c_pool")
        p_set = sem("p_set")
        p_raw = sem("p_raw")
        p_fill = sem("p_fill")
        p_dve = sem("p_dve")
        p_v = sem("p_v")
        p_p = sem("p_p")
        p_va = sem("p_va")
        p_a = sem("p_a")
        p_ready = sem("p_ready")
        e_ld = sem("e_ld")
        e_split = Steps(sem("e_split"), {"E": ("high", "rest1", "mid", "rest2", "placed")}, 1, 0, ["E"], QUADS)
        e_tr = sem("e_tr")
        e_cp = sem("e_cp")
        e_st = sem("e_st")
        n_idx = sem("n_idx")
        n_val = sem("n_val")
        n_sc = [sem(f"n_sc{j}") for j in range(4)]
        n_g = [sem(f"n_g{j}") for j in range(4)]
        n_cp = sem("n_cp")

        def psteps(name, order, by=1):
            return [Steps(sem(f"{name}{b}"), {"P": order}, by, 0, ["P"], PLAIN_TURNS) for b in (0, 1)]

        q_ld = psteps("q_ld", ("x",), 16)
        q_v = psteps("q_v", ("stats1", "aggr1", "rs1", "nb1", "h1b", "xb", "x1", "stats2", "aggr2", "rs2", "nb2",
                             "xc", "y", "yx", "stats3", "aggr3", "rs3", "nb3", "xo", "r8", "r9", "r10", "r11", "xf"))
        q_p = psteps("q_p", ("gT1", "h1a", "h1b", "t1", "gT2", "h2", "rA", "rB", "gT3", "h8", "r8", "h9", "r9",
                             "h10", "r10", "r11"))
        q_a = psteps("q_a", ("sd1", "half1", "g1", "gT1", "h1a", "t1", "sd2", "half2", "g2", "gT2", "h2", "rA", "sd3", "half3", "g3", "gT3",
                             "h8", "h9", "h10"))
        q_st = {t: psteps(f"q_st{t}_", (t,), 16) for t in ("t1", "t2", "t3", "t4", "t8", "t9", "t10", "t11", "out")}

        AGG = ("C1", "C2", "S1", "S2", "LA", "LB", "GA", "GZ")
        four = ("t3", "t2", "t1", "t0")

        def steps(name, order, by=1, start=0):
            return Steps(sem(name), order, by, start)

        idxed = steps("idxed", {k: ("slots",) for k in KINDS})
        gat = [steps(f"gat{j}", {k: ("rows",) for k in KINDS}, 16) for j in range(4)]
        m_free = steps("m_free", {k: four for k in ("C1", "C2", "S1", "S2", "GA", "GZ")}, 1, 4)
        sel = steps("sel", {k: four for k in AGG})
        agg = steps("agg", {k: four for k in AGG}, 1, 8)
        carry = steps("carry", {k: four for k in AGG})
        mprod = steps("mprod", {"LA": four, "LB": four, "GA": ("quad",), "GZ": ("quad",)}, 1, 4)
        own = steps("own", {k: ("rows",) for k in ("C1", "C2", "S1", "S2", "GA", "GZ")}, 16)
        xin = steps("xin", {k: ("rows",) for k in ("C2", "S2", "LB", "GZ")}, 16)
        eas = steps("eas", {k: ("attr",) for k in ("LA", "LB")}, 16)
        st_t = steps("st_t", {k: ("table",) for k in KINDS if k != "GZ"}, 16)
        st_x = steps("st_x", {k: ("rows",) for k in ("X", "C2", "S1", "S2", "LB")}, 16)
        st_o = [steps(f"st_o{j}", {"GZ": ("rows",)}, 16) for j in range(4)]
        vd = steps("vd", {
            "X": ("stats", "aggr", "rs", "nb"),
            "C1": ("own", "comb", "h1b"),
            "C2": ("own", "bias", "comb", "x", "stats", "aggr", "rs", "nb"),
            "S1": ("comb", "rB"),
            "S2": ("comb", "x", "stats", "aggr", "rs", "nb"),
            "LA": ("comb", "stats", "aggr", "rs", "nb"),
            "LB": ("comb", "stats", "aggr", "rs", "nb", "lnw", "lnb", "x", "stats2", "aggr2", "rs2", "nb2"),
            "GA": ("den", "comb", "dene", "rden", "norm"),
            "GZ": ("den", "comb", "dene", "rden", "norm", "bias", "x")})
        pd = steps("pd", {
            "C1": ("uT", "h1a", "h1b", "rows"), "S1": ("oT", "uT", "hT", "rA", "rB"), "S2": ("gT", "rows"),
            "LA": ("nT", "rows"), "LB": ("gT", "rows"), "GA": ("uT", "rows")}, 1, 4)
        ad = steps("ad", {
            "X": ("sd", "g"), "C1": ("uT", "h1a", "rows"), "C2": ("sd", "g"),
            "S1": ("oT", "uT", "hT", "rA"), "S2": ("sd", "g"),
            "LA": ("sd", "n"), "LB": ("sd", "n", "sd2", "g"),
            "GA": ("uT", "rows", "nv")})
        ad_t = steps("ad_t", {"S2": ("gT", "rows"), "LB": ("gT", "rows", "nv"), "LA": ("nT", "rows")})
        BEHIND = ("S2", "LB")
        LATE = ("LA", "GA")
        pd_e = steps("pd_e", {k: ("rT", "em") for k in ("LA", "LB")})
        ad_e = steps("ad_e", {k: ("rT",) for k in ("LA", "LB")})
        hself = steps("hself", {"GA": ("own",), "GZ": ("own",)})
        m_p = Steps(sem("m_p"), {"mid": ("scan", "rowmax", "getmax", "rowown", "getown", "tile")}, 1, 0, ["mid"], 0)
        m_v = Steps(sem("m_v"), {"mid": ("es", "max", "maxes", "own", "owns", "power", "weights")}, 1, 0, ["mid"], 0)
        m_a = Steps(sem("m_a"), {"mid": ("exp",)}, 1, 0, ["mid"], 0)
        m_idx = sem("m_idx")
        ATTENTION = [s for s, k in enumerate(KINDS) if k in ("GA", "GZ")]

        OWN_SRC = {1: TAB[1], 2: TAB[2], 3: TAB[3], 4: SELF, 8: TAB[8], 9: TAB[9], 10: TAB[10], 11: TAB[11]}
        X_SRC = {2: XR[0], 4: XR[2], 7: XR[4], 11: XR[7]}
        X_DST = {0: XR[0], 2: XR[2], 3: SELF, 4: XR[4], 7: XR[7]}
        STAGES = list(enumerate(KINDS))
        LAST = QUADS - 1

        def quad_rows(t, Q):
            return t[ds(Q * QR, QR), :].rearrange("(j p) c -> p j c", p=P)

        def plain_rows(t, base):
            return t[ds(base, QR), :].rearrange("(p j) c -> p j c", j=4)

        def stage_stored(eng, s):
            for st in (st_t, st_x):
                if KINDS[s] in st.order:
                    eng.wait_ge(st.sem, st.at(s, LAST, st.order[KINDS[s]][-1]))

        def alone(eng, *waits):
            for _, value in waits:
                eng.compute_val(value)
            eng.wait_ge(c_pool, 13)
            for sm, value in waits:
                eng.wait_ge(sm, value)

        loads = [(w1[:, :], a["L0_gnn_W1"]), (w2[:, :, :], a["L0_gnn_W2"].rearrange("(b p) c -> p b c", p=P)),
                 (b1[:, :], a["L0_gnn_b1"].rearrange("(b p) -> p b", p=P)),
                 (w1l[:, :], a["L1_gnn_w1l"]), (w1r[:, :], a["L1_gnn_w1r"]),
                 (w2l[:, :], a["L1_gnn_w2l"]), (w2r[:, :], a["L1_gnn_w2r"]),
                 (b1l[:, :], a["L1_gnn_b1l"].rearrange("(p o) -> p o", o=1)),
                 (linw[:, :, :], a["L2_gnn_lin_w"].rearrange("l p c -> p l c")),
                 (ew2[:, :, :], a["L2_gnn_edge_w2"].rearrange("l p c -> p l c")),
                 (eb1[:, :], a["L2_gnn_edge_b1"].rearrange("l p -> p l")),
                 (lnw_c[:, :], a["L2_gnn_ln_w"].rearrange("l p -> p l")),
                 (lnb_c[:, :], a["L2_gnn_ln_b"].rearrange("l p -> p l")),
                 (WX[:, 0, 0:D], a["L3_gnn_W_in"]), (WX[:, 1, 0:D], a["L3_gnn_W_h"][0]),
                 (WX[:, 2, 0:D], a["L3_gnn_W_h"][1]), (WX[:, 3, 0:D], a["L3_gnn_W_out"]),
                 (gb_c[:, 0:1], a["L3_gnn_b_in"].rearrange("(p o) -> p o", o=1)),
                 (gb_c[:, 1:3], a["L3_gnn_b_h"].rearrange("l p -> p l")),
                 (b2_r[:, :], a["L0_gnn_b2"].partition_broadcast(P)),
                 (b2l_r[:, :], a["L1_gnn_b2l"].partition_broadcast(P)),
                 (lnw_r[:, :], a["L2_gnn_ln_w"][2].partition_broadcast(P)),
                 (lnb_r[:, :], a["L2_gnn_ln_b"][2].partition_broadcast(P)),
                 (gout_r[:, :], a["L3_gnn_b_out"].partition_broadcast(P))]
        loads += [(bias_r[:, l, :], a["L2_gnn_bias"][l].partition_broadcast(P)) for l in range(3)]
        loads += [(w_in[ED * k:ED * k + ED, :, :], a["L2_gnn_edge_w1"].rearrange("l p c -> p l c")) for k in range(8)]
        loads += [(b_in[:, l, :], a["L2_gnn_edge_b2"][l].partition_broadcast(3)) for l in range(3)]
        attn = [a["L3_gnn_a_src_in"], a["L3_gnn_a_dst_in"], a["L3_gnn_a_src_h"][0], a["L3_gnn_a_dst_h"][0],
                a["L3_gnn_a_src_h"][1], a["L3_gnn_a_dst_h"][1], a["L3_gnn_a_src_out"], a["L3_gnn_a_dst_out"]]
        loads += [(av[v], attn[v].rearrange("h c -> (h c)").partition_broadcast(P)) for v in range(8)]
        LOADED = 16 * len(loads)

        x, src, dst, ea = a["x"], a["src"], a["dst"], a["edge_attr_16"]
        BLOCK1 = HALF * P
        TAIL = (T - 1) * P

        def span(t, start, rows, step, cols):
            return bass.AP(tensor=t.tensor, offset=start, ap=[[step, rows], [1, cols]])


        def attention_middle(dve, v, link, s):
            mid = ATTENTION.index(s)

            def flat(t):
                return t.rearrange("q k b p -> q (k b p)")

            def leaky(t):
                link(v.scalar_tensor_tensor(t, t, 0.2, t, ALU.mult, ALU.max))

            dve.wait_ge(m_free.sem, m_free.at(s, LAST, "t0"))
            v.tensor_copy(ES[:, :, :], G[:, :, D:GW].rearrange("p t h -> p h t")).then_inc(m_v.sem, 1)
            dve.wait_ge(m_p.sem, m_p.at(0, mid, "scan"))
            link(v.tensor_copy(V[:, :, :, :].rearrange("q k b p -> q (k b p)"),
                               PS[0:HALF, 4:7, :].rearrange("q x c -> q (x c)")))
            v.tensor_tensor_scan(flat(HS[:, 0:2])[:, ::-1], flat(R2[:, :])[:, ::-1], flat(V[:, 0:2])[:, ::-1], -BIG,
                                 ALU.add, ALU.max).then_inc(m_v.sem, 1)
            dve.wait_ge(m_p.sem, m_p.at(0, mid, "rowmax"))
            v.tensor_tensor_scan(brow[:, 0:T][:, ::-1], rb[:, :][:, ::-1], PS[0:2, 7, 0:T][:, ::-1], -BIG,
                                 ALU.add, ALU.max).then_inc(m_v.sem, 1)
            dve.wait_ge(m_p.sem, m_p.at(0, mid, "getmax"))
            for b in (0, 1):
                link(v.tensor_copy(cb[:, b, 0:2], PS[0:HALF, 4, 4 * b:4 * b + 2]))
            for k in (0, 1):
                for b in (0, 1):
                    i = v.scalar_tensor_tensor(HS[:, k, b], LMB[:, b, :], cb[:, b, k:k + 1], HS[:, k, b],
                                               ALU.add, ALU.max)
            link(i)
            top, own_ = W4[:, 0:2], V[:, 2:4]
            link(v.tensor_tensor(top, HS[:, 0:2], own_, ALU.max))
            v.tensor_copy(W4[:, 2:4], V[:, 4:6])
            link(v.tensor_tensor(top, top, V[:, 4:6], ALU.add))
            leaky(flat(top))
            link(v.tensor_tensor(own_, own_, V[:, 4:6], ALU.add))
            leaky(flat(own_))
            link(v.tensor_tensor(own_, own_, top, ALU.subtract))
            link(v.tensor_tensor(flat(W4[:, :]), flat(W4[:, :]), flat(FI4[:, :]), ALU.mult))
            v.tensor_tensor_scan(flat(HS[:, :]), flat(A4[:, :]), flat(W4[:, :]), 0.0, ALU.mult,
                                 ALU.add).then_inc(m_v.sem, 1)
            dve.wait_ge(m_p.sem, m_p.at(0, mid, "rowown"))
            v.tensor_tensor_scan(crow[:, 1:T + 1], rfa[:, :], PS[0:4, 7, 0:T], 0.0, ALU.mult,
                                 ALU.add).then_inc(m_v.sem, 1)
            dve.wait_ge(m_p.sem, m_p.at(0, mid, "getown"))
            for b in (0, 1):
                link(v.tensor_copy(cb[:, b, :], PS[0:HALF, 4, 4 * b:4 * b + 4]))
            for k in range(4):
                for b in (0, 1):
                    i = v.scalar_tensor_tensor(HS[:, k, b], CM[:, b, :], cb[:, b, k:k + 1], HS[:, k, b],
                                               ALU.mult, ALU.add)
            link(i)
            es = V[:, 0:2]
            link(v.tensor_tensor(es, es, HS[:, 2:4], ALU.add))
            leaky(flat(es))
            v.tensor_tensor(es, es, HS[:, 0:2], ALU.subtract).then_inc(m_v.sem, 1)
            dve.wait_ge(m_p.sem, m_p.at(0, mid, "tile"))
            v.tensor_copy(PT[:, 0:2, :].rearrange("p k t -> p (k t)"), PS[:, 4, 0:2 * T])
            v.tensor_copy(PT[:, 2:4, :].rearrange("p k t -> p (k t)"), PS[:, 5, 0:2 * T]).then_inc(m_v.sem, 1)

        def attention_turns(pe, turn, s):
            mid = ATTENTION.index(s)
            pe.wait_ge(m_v.sem, m_v.at(0, mid, "es"))
            for k in range(6):
                for b in (0, 1):
                    c = 2 * k + b
                    row = (ES[:, k, :] if k < 2 else NV[:, k - 2, :])[:, HALF * b:HALF * b + HALF]
                    i = turn(PS[0:HALF, 4 + c // 4, P * (c % 4):P * (c % 4) + P], row)
            i.then_inc(m_p.sem, 1)
            pe.wait_ge(m_v.sem, m_v.at(0, mid, "max"))
            for b in (0, 1):
                i = turn(PS[0:2, 7, HALF * b:HALF * b + HALF], HS[:, 0:2, b, 0])
            i.then_inc(m_p.sem, 1)
            pe.wait_ge(m_v.sem, m_v.at(0, mid, "maxes"))
            for b in (0, 1):
                i = turn(PS[0:HALF, 4, 4 * b:4 * b + 2], brow[:, HALF * b + 1:HALF * b + HALF + 1])
            i.then_inc(m_p.sem, 1)
            pe.wait_ge(m_v.sem, m_v.at(0, mid, "own"))
            for b in (0, 1):
                i = turn(PS[0:4, 7, HALF * b:HALF * b + HALF], HS[:, :, b, P - 1])
            i.then_inc(m_p.sem, 1)
            pe.wait_ge(m_v.sem, m_v.at(0, mid, "owns"))
            for b in (0, 1):
                i = turn(PS[0:HALF, 4, 4 * b:4 * b + 4], crow[:, HALF * b:HALF * b + HALF])
            i.then_inc(m_p.sem, 1)
            pe.wait_ge(m_a.sem, m_a.at(0, mid, "exp"))
            for k in range(4):
                for b in (0, 1):
                    at = T * (k % 2) + HALF * b
                    i = turn(PS[:, 4 + k // 2, at:at + HALF], W4[:, k, b])
            i.then_inc(m_p.sem, 1)
            pe.wait_ge(m_v.sem, m_v.at(0, mid, "weights"))

        def attention_exp(act, f, s):
            mid = ATTENTION.index(s)
            act.wait_ge(m_v.sem, m_v.at(0, mid, "power"))
            f(W4[:, :, :, :].rearrange("q k b p -> q (k b p)"), V[:, 0:4].rearrange("q k b p -> q (k b p)"),
              ACT.Exp).then_inc(m_a.sem, 1)

        block = ctx.enter_context(nc.Block())

        @block.sync
        def _(sp):
            for o, i in loads:
                sp.dma_start(o, i, allow_slow_non_contiguous=True).then_inc(c_load, 16)
            sp.wait_ge(p_set, 3)
            sp.dma_start(raw2[0:1, 0, 1:P + 2], span(dst, 0, 1, 1, P + 1)).then_inc(p_raw, 16)
            sp.dma_start(raw2[1:HALF, 0, :], span(dst, P - 1, HALF - 1, P, P + 2)).then_inc(p_raw, 16)
            sp.dma_start(raw2[0:HALF - 1, 1, :], span(dst, BLOCK1 - 1, HALF - 1, P, P + 2)).then_inc(p_raw, 16)
            sp.dma_start(raw2[HALF - 1:HALF, 1, 0:E - TAIL + 1],
                         span(dst, TAIL - 1, 1, 1, E - TAIL + 1)).then_inc(p_raw, 16)
            sp.dma_start(srcraw[:, 0, :], span(src, 0, HALF, P, P)).then_inc(p_raw, 16)
            sp.dma_start(srcraw[0:HALF - 1, 1, :], span(src, BLOCK1, HALF - 1, P, P)).then_inc(p_raw, 16)
            sp.dma_start(srcraw[HALF - 1:HALF, 1, 0:E - TAIL], span(src, TAIL, 1, 1, E - TAIL)).then_inc(p_raw, 16)
            sp.wait_ge(c_pool, 11)
            sp.dma_start(NODE.rearrange("(p a) c -> p (a c)", p=100), FILL[0:100, :]).then_inc(p_fill, 16)

            def base(m, b):
                return N - QR if b and isinstance(m, int) and m == PLAIN_TURNS - 1 else m * (2 * QR) + b * QR

            def load_x(m, b):
                if not isinstance(m, int) or m:
                    alone(sp, (q_v[b].sem, q_v[b].last(0, m, "xo")))
                sp.dma_start(PXT[b], plain_rows(x, base(m, b))).then_inc(q_ld[b].sem, 16)

            def keep(m, b, name, ready, rows, to=None):
                sp.wait_ge(*ready)
                if b and isinstance(m, int) and m == PLAIN_TURNS - 1:
                    sp.wait_ge(q_st[name][0].sem, q_st[name][0].at(0, m, name))
                tab, shift = (out, 0) if name == "out" else (TAB[int(name[1:])], EP)
                sp.dma_start(plain_rows(tab, base(m, b) + shift), rows).then_inc(q_st[name][b].sem, 16)

            def keep_attention(m, b, then=None):
                for t, r in ((8, 2), (9, 3), (10, 0), (11, 1)):
                    keep(m, b, f"t{t}", (q_v[b].sem, q_v[b].at(0, m, f"r{t}")), PRO[b][r])
                    if t == 8 and then:
                        then()
                keep(m, b, "out", (q_v[b].sem, q_v[b].at(0, m, "xf")), PYT[b])

            def keep_norm(m, b, k):
                keep(m, b, f"t{2 * k - 1}", (q_a[b].sem, q_a[b].at(0, m, f"g{k}")), PGN[b])

            def keep_rows(m, b, k):
                keep(m, b, f"t{2 * k}", (q_a[b].sem, q_a[b].at(0, m, ("t1", "rA")[k - 1])), PRO[b][k - 1][:, :, 0:D])

            def load_attributes(m):
                if isinstance(m, int) and m == LAST:
                    sp.dma_start(ea_last[0:(E - LAST * QR) // 4, :, :],
                                 ea[LAST * QR:E, :].rearrange("(p j) c -> p j c", j=4)).then_inc(e_ld, 16)
                else:
                    sp.dma_start(ea_in[:, :, :],
                                 ea[ds(m * QR, QR), :].rearrange("(p j) c -> p j c", j=4)).then_inc(e_ld, 16)

            def plain(m):
                at = m if isinstance(m, int) else 1
                if at:
                    load_x(m, 1)
                    keep_attention(m - 1, 1)
                keep_norm(m, 0, 1)
                keep_norm(m, 1, 1)
                keep_rows(m, 0, 1)
                if at < LAST:
                    alone(sp, (e_split.sem, e_split.at(0, m, "rest1")))
                    load_attributes(m + 1)
                keep_norm(m, 0, 2)
                keep_rows(m, 1, 1)
                for j in range(4):
                    sp.wait_ge(gat[j].sem, gat[j].at(0, m, "rows"))
                sp.dma_start(quad_rows(XR[0], m), M[:, :, 0:D]).then_inc(st_x.sem, 16)
                keep_norm(m, 1, 2)
                keep_rows(m, 0, 2)
                sp.wait_ge(ad.sem, ad.at(0, m, "g"))
                sp.dma_start(quad_rows(TAB[1], m), GN[:, :, :]).then_inc(st_t.sem, 16)
                alone(sp, (e_cp, m + 1))
                sp.dma_start(EAT[:, ds(m * QR, QR)], eat[:, :]).then_inc(e_st, 16)
                keep_rows(m, 1, 2)
                keep_attention(m, 0, (lambda: load_x(m + 1, 0)) if at < PLAIN_TURNS - 1 else None)

            load_attributes(0)
            for b in (0, 1):
                load_x(0, b)
            plain(0)
            with sp.Fori(1, PLAIN_TURNS - 2) as m:
                plain(m)
            plain(PLAIN_TURNS - 2)
            plain(PLAIN_TURNS - 1)
            keep_attention(PLAIN_TURNS - 1, 1)
            sp.wait_ge(e_st, 16 * QUADS)

            for s, kind in STAGES[1:]:
                stage_stored(sp, s - 1)

                def quad(n):
                    return LAST - n if isinstance(n, int) else n * (-1) + LAST

                def load_attr(n):
                    alone(sp, (pd_e.sem, pd_e.at(s, n) if isinstance(n, int) and n == 0 else pd_e.last(s, n, "rT")))
                    sp.dma_start(eat[:, :], EAT[:, ds(quad(n) * QR, QR)]).then_inc(eas.sem, 16)

                def load(n):
                    first = isinstance(n, int) and n == 0
                    if kind in own.order:
                        used, step = {"S1": (pd, "oT")}.get(kind, (vd, "comb"))
                        sp.wait_ge(used.sem, used.at(s, n) if first else used.last(s, n, step))
                        w = GW if kind in hself.order else D
                        sp.dma_start(OWN[:, :, 0:w], quad_rows(OWN_SRC[s], quad(n))).then_inc(own.sem, 16)
                    if kind in xin.order:
                        sp.wait_ge(vd.sem, vd.at(s, n) if first else vd.last(s, n, "x"))
                        sp.dma_start(XIN[:, :, :], quad_rows(X_SRC[s], quad(n))).then_inc(xin.sem, 16)

                def store_x(n):
                    xstep = {"C2": "x", "S2": "x", "LB": "x"}.get(kind)
                    if xstep:
                        sp.wait_ge(vd.sem, vd.at(s, n, xstep))
                        sp.dma_start(quad_rows(X_DST[s], quad(n)), RB[:, :, :]).then_inc(st_x.sem, 16)

                def store(n):
                    astep, rows = {"C2": ("g", GN[:, :, :]), "C1": ("rows", RO[:, :, 0:D]),
                                   "S1": ("rA", RO[:, :, 0:D]), "S2": ("rows", RO[:, :, 0:D]),
                                   "LA": ("rows", RO[:, :, 0:D]), "LB": ("rows", RO[:, :, :]),
                                   "GA": ("rows", RO[:, :, :])}[kind]
                    done = ad_t if kind in ad_t.order else ad
                    sp.wait_ge(done.sem, done.at(s, n, astep))
                    sp.dma_start(quad_rows(TAB[s + 1], quad(n)), rows).then_inc(st_t.sem, 16)
                    if kind == "S1":
                        sp.wait_ge(vd.sem, vd.at(s, n, "rB"))
                        sp.dma_start(quad_rows(X_DST[s], quad(n)), RB[:, :, :]).then_inc(st_x.sem, 16)

                if kind == "GZ":
                    load(0)
                    with sp.Fori(0, LAST) as n:
                        load(n + 1)
                else:
                    behind = kind in BEHIND + LATE

                    def turn(n):
                        at = n if isinstance(n, int) else 1
                        if kind in eas.order and at < LAST - 2:
                            load_attr(n + 3)
                        if at < LAST:
                            load(n + 1)
                        store_x(n)
                        if behind and at:
                            store(n - 1)
                        if not behind or at == LAST:
                            store(n)

                    if kind in eas.order:
                        for n in (0, 1, 2):
                            load_attr(n)
                    load(0)
                    turn(0)
                    with sp.Fori(1, LAST - 2) as n:
                        turn(n)
                    for n in (LAST - 2, LAST - 1, LAST):
                        turn(n)

        @block.gpsimd
        def _(pool):
            g = nc.gpsimd
            g.memset(ident[:, :], 0.0).then_inc(c_pool, 1)
            g.iota(iota_row[:, :], [[1, P]], base=0, channel_multiplier=0,
                   allow_small_or_imprecise_dtypes=True).then_inc(c_pool, 1)
            g.memset(eps[:, :], LN_EPS).then_inc(c_pool, 1)
            g.memset(ones_row[:, :], 1.0).then_inc(c_pool, 1)
            pool.wait_ge(c_pool, 4)
            g.affine_select(out=ident[:, :], in_=ident[:, :], compare_op=ALU.not_equal, fill=1.0, base=0,
                            pattern=[[-1, P]], channel_multiplier=1).then_inc(c_pool, 1)
            g.memset(raw2[:, :, :], 60000).then_inc(p_set, 1)
            g.memset(srcraw[:, :, :], 0).then_inc(p_set, 1)
            pool.wait_ge(p_set, 2)
            g.memset(raw2[:, 1, P + 1:P + 2], 70000).then_inc(p_set, 1)
            g.iota(W4[:, 0, :, :], [[BLOCK1, 2], [1, P]], base=0, channel_multiplier=P,
                   allow_small_or_imprecise_dtypes=True).then_inc(c_pool, 1)
            g.iota(W4[:, 1, :, :], [[BLOCK1, 2], [0, P]], base=0, channel_multiplier=P,
                   allow_small_or_imprecise_dtypes=True).then_inc(c_pool, 1)
            g.iota(te1[:, :], [[P, T]], base=0, channel_multiplier=1,
                   allow_small_or_imprecise_dtypes=True).then_inc(c_pool, 1)
            g.memset(ea_last[:, :, :], 0.0).then_inc(c_pool, 1)
            fill2 = FILL[0:100, :].rearrange("p (a c) -> p a c", c=2)
            g.memset(fill2[:, :, 0:1], -1.0).then_inc(c_pool, 1)
            g.memset(fill2[:, :, 1:2], 0.0).then_inc(c_pool, 1)
            g.memset(crow[:, :], 0.0).then_inc(c_pool, 1)
            g.memset(brow[:, :], -BIG).then_inc(c_pool, 1)
            g.memset(C[:, :], 0.0).then_inc(m_free.sem, 4)
            g.memset(M[:, :, :], 0.0).then_inc(agg.sem, 8)
            g.memset(den[:, :, :], 0.0).then_inc(mprod.sem, 4)
            g.memset(GN[:, :, :], 0.0).then_inc(pd.sem, 4)

            pool.wait_ge(p_ready, 1)
            pool.wait_ge(p_fill, 16)
            def node_scatter(n):
                for j in range(4):
                    if not isinstance(n, int) or n:
                        pool.wait_ge(n_sc[j], n * 16)
                g.tensor_copy(idx_slot[:, 0:4], idx_dst[:, ds(n * 4, 4)]).then_inc(n_idx, 1)
                g.tensor_copy(node_slot[:, :, :], node_val[:, ds(n * 4, 4), :]).then_inc(n_val, 1)
                alone(pool, (n_idx, n + 1), (n_val, n + 1))
                for j in range(4):
                    g.indirect_dma_start(NODE, bass.IndirectOffsetOnAxis(ap=idx_slot[:, j:j + 1], axis=0),
                                         node_slot[:, j, :], None, bounds_check=N - 1,
                                         oob_is_err=False).then_inc(n_sc[j], 16)

            def node_gather(n):
                g.tensor_copy(idx_slot[:, 0:4], idx_src[:, ds(n * 4, 4)]).then_inc(n_idx, 1)
                alone(pool, (n_idx, n + (QUADS + 1)))
                for j in range(4):
                    g.indirect_dma_start(node_slot[:, j, :], None, NODE,
                                         bass.IndirectOffsetOnAxis(ap=idx_slot[:, j:j + 1], axis=0)).then_inc(n_g[j], 16)
                for j in range(4):
                    pool.wait_ge(n_g[j], n * 16 + 16)
                g.tensor_copy(node_src[:, ds(n * 4, 4), :], node_slot[:, :, :]).then_inc(n_cp, 1)
                pool.wait_ge(n_cp, n + 1)

            def beside_plain(m):
                for j in range(4):
                    if not isinstance(m, int) or m:
                        pool.wait_ge(gat[j].sem, gat[j].at(0, m))
                g.tensor_copy(idx_slot[:, 4:8], idx_x[:, ds(m * 4, 4)]).then_inc(idxed.sem, 1)
                if isinstance(m, int) and m == 0:
                    pool.wait_ge(idxed.sem, 1)
                else:
                    alone(pool, (idxed.sem, idxed.at(0, m, "slots")), (st_x.sem, st_x.at(0, m)), (ad.sem, ad.at(0, m)))
                for j in range(4):
                    g.indirect_dma_start(M[:, j, 0:D], None, x,
                                         bass.IndirectOffsetOnAxis(ap=idx_slot[:, 4 + j:5 + j], axis=0)
                                         ).then_inc(gat[j].sem, 16)
                from_ = ea_last if isinstance(m, int) and m == LAST else ea_in
                rest = [e_rest[:, k, :].rearrange("p (j c) -> p j c", j=4) for k in (0, 1)]
                if not isinstance(m, int) or m:
                    pool.wait_ge(e_tr, m)

                def cutting(ins, name):
                    ins.then_inc(e_split.sem, 1)
                    alone(pool, (e_split.sem, e_split.at(0, m, name)))

                alone(pool, (e_ld, m * 16 + 16))
                cutting(g.tensor_copy(ea_parts[:, 0], from_[:, :, :]), "high")
                cutting(g.tensor_tensor(rest[0], from_[:, :, :], ea_parts[:, 0], ALU.subtract), "rest1")
                cutting(g.tensor_copy(ea_parts[:, 1], rest[0]), "mid")
                cutting(g.tensor_tensor(rest[1], rest[0], ea_parts[:, 1], ALU.subtract), "rest2")
                for k, (_, e) in enumerate(PARTS):
                    part = (ea_parts[:, 0], ea_parts[:, 1], rest[1])[e]
                    i = g.tensor_copy(E8[:, :, ED * k:ED * k + ED], part)
                i.then_inc(e_split.sem, 1)

            HALF_TURNS = QUADS // 2
            beside_plain(0)
            node_scatter(0)
            node_scatter(1)
            with pool.Fori(1, HALF_TURNS) as m:
                beside_plain(m)
                node_scatter(m * 2)
                node_scatter(m * 2 + 1)
            beside_plain(HALF_TURNS)
            node_scatter(QUADS - 1)
            for j in range(4):
                pool.wait_ge(n_sc[j], 16 * QUADS)
            with pool.Fori(0, HALF_TURNS - 1) as m:
                beside_plain(m + (HALF_TURNS + 1))
                node_gather(m * 2)
                node_gather(m * 2 + 1)
            beside_plain(LAST)
            for n in (LAST - 2, LAST - 1, LAST):
                node_gather(n)

            def gather_quad(s, table, idx, w, n, half):
                Q4 = n * (-4) + 4 * LAST
                for j in range(4):
                    pool.wait_ge(gat[j].sem, gat[j].at(s, n) - 16)
                at = 4 * half
                g.tensor_copy(idx_slot[:, at:at + 4], idx[:, ds(Q4, 4)]).then_inc(idxed.sem, 1)
                for j in (3, 2, 1, 0):
                    free = mprod if KINDS[s] in ("LA", "LB") else m_free
                    used = (free.sem, free.last(s, n, f"t{j}"))
                    alone(pool, used, *([(idxed.sem, idxed.at(s, n, "slots"))] if j == 3 else []))
                    g.indirect_dma_start(M[:, j, 0:w], None, table,
                                         bass.IndirectOffsetOnAxis(ap=idx_slot[:, at + j:at + j + 1], axis=0)
                                         ).then_inc(gat[j].sem, 16)

            def gathers(s, table, idx, w):
                with pool.Fori(0, QUADS // 2) as m:
                    gather_quad(s, table, idx, w, m * 2, 0)
                    gather_quad(s, table, idx, w, m * 2 + 1, 1)
                gather_quad(s, table, idx, w, LAST, 0)

            pool.wait_ge(p_ready, 2)
            for t in q_st.values():
                for b in (0, 1):
                    pool.wait_ge(t[b].sem, 16 * PLAIN_TURNS)
            for s, kind in STAGES[1:]:
                stage_stored(pool, s - 1)
                if kind not in hself.order:
                    gathers(s, TAB[s], idx_l2 if kind in ("LA", "LB") else idx_all, D)
                    continue
                gathers(s, TAB[s], idx_all, GW)
                pool.wait_ge(m_v.sem, m_v.at(0, ATTENTION.index(s), "weights"))

                def messages(n):
                    Q4 = n * (-4) + 4 * LAST
                    for h in (0, 1):
                        gh = G[:, ds(Q4, 4), 64 * h:64 * h + 64]
                        g.tensor_tensor(gh, gh, wide(PT[:, h, ds(Q4, 4)], 64), ALU.mult)
                    g.tensor_copy(G[:, ds(Q4, 4), D:GW],
                                  PT[:, 0:2, ds(Q4, 4)].rearrange("p h j -> p j h")).then_inc(mprod.sem, 1)

                def own_rows(n):
                    Q4 = n * (-4) + 4 * LAST
                    pool.wait_ge(own.sem, own.at(s, n, "rows"))
                    for h in (0, 1):
                        oh = OWN[:, :, 64 * h:64 * h + 64]
                        last = g.tensor_tensor(oh, oh, wide(PT[:, 2 + h, ds(Q4, 4)], 64), ALU.mult)
                    last.then_inc(hself.sem, 1)
                    if kind == "GZ":
                        for j in range(4):
                            pool.wait_ge(st_o[j].sem, st_o[j].at(s, n))
                        g.tensor_copy(idx_slot[:, 0:4], idx_dst[:, ds(Q4, 4)]).then_inc(m_idx, 1)
                        alone(pool, (m_idx, n + 1), (vd.sem, vd.at(s, n, "x")))
                        for j in range(4):
                            g.indirect_dma_start(out, bass.IndirectOffsetOnAxis(ap=idx_slot[:, j:j + 1], axis=0),
                                                 RO[:, j, 0:D], None, bounds_check=N - 1,
                                                 oob_is_err=False).then_inc(st_o[j].sem, 16)

                messages(0)
                messages(1)
                own_rows(0)
                with pool.Fori(1, LAST) as n:
                    messages(n + 1)
                    own_rows(n)
                own_rows(LAST)
            for j in range(4):
                pool.wait_ge(st_o[j].sem, 16 * QUADS)

        @block.vector
        def _(dve):
            v = nc.vector
            count = [0]

            def link(ins):
                count[0] += 1
                ins.then_inc(p_dve, 1)
                dve.wait_ge(p_dve, count[0])

            def two(t):
                return t.rearrange("q b p -> q (b p)")

            dve.wait_ge(p_raw, 7 * 16)
            dve.wait_ge(c_pool, 13)
            link(v.tensor_copy(x2f[:, :, :], raw2[:, :, :]))
            dst2 = x2f[:, :, 1:P + 1]
            FI, A, last, cm0, lm1, lm0, lm = FI4[:, 0], A4[:, 0], V[:, 0], V[:, 1], V[:, 2], V[:, 3], V[:, 4]
            v.tensor_tensor(FI, dst2, x2f[:, :, 0:P], ALU.not_equal)
            v.tensor_tensor(last, dst2, x2f[:, :, 2:P + 2], ALU.not_equal)
            v.memset(cm0, 0.0)
            link(v.memset(lm0, 0.0))
            v.tensor_scalar(A, FI, -1.0, 1.0, ALU.mult, ALU.add)
            v.tensor_scalar(lm1, last, -1.0, 1.0, ALU.mult, ALU.add)
            v.tensor_scalar(R2[:, 0], last, -BIG, None, ALU.mult)
            link(v.tensor_tensor(W4[:, 2], FI, W4[:, 0], ALU.mult))
            v.tensor_copy(cm0[:, :, 0:1], A[:, :, 0:1])
            link(v.tensor_copy(lm0[:, :, P - 1:P], lm1[:, :, P - 1:P]))
            v.memset(A[:, :, 0:1], 0.0)
            v.memset(lm1[:, :, P - 1:P], 0.0)
            link(v.memset(R2[:, 0, :, P - 1:P], -BIG))
            v.tensor_tensor_scan(two(CM[:, :, :]), two(A), two(cm0), 0.0, ALU.mult, ALU.add)
            v.tensor_tensor_scan(two(lm)[:, ::-1], two(lm1)[:, ::-1], two(lm0)[:, ::-1], 0.0, ALU.mult, ALU.add)
            v.tensor_tensor_scan(two(HS[:, 0]), two(A), two(W4[:, 2]), 0.0, ALU.mult, ALU.add)
            v.tensor_tensor_scan(two(HS[:, 1])[:, ::-1], two(R2[:, 0])[:, ::-1], two(W4[:, 0])[:, ::-1], -BIG,
                                 ALU.add, ALU.max)
            for k in (1, 2, 3):
                v.tensor_copy(FI4[:, k], FI)
                v.tensor_copy(A4[:, k], A)
            link(v.tensor_copy(R2[:, 1], R2[:, 0]))
            link(v.tensor_scalar(LMB[:, :, :], lm, BIG, -BIG, ALU.mult, ALU.add))
            v.tensor_copy(ends[:, :, 0:1], HS[:, 0, :, P - 1:P])
            v.tensor_copy(ends[:, :, 1:2], HS[:, 1, :, 0:1])
            v.tensor_copy(ends[:, :, 2:6], CM[:, :, P - 1:P].to_broadcast([HALF, 2, 4]))
            v.tensor_copy(ends[:, :, 6:8], LMB[:, :, 0:1].to_broadcast([HALF, 2, 2]))
            v.tensor_copy(ends[:, :, 8:9], lm[:, :, P - 1:P]).then_inc(p_v, 1)
            dve.wait_ge(p_p, 1)
            v.tensor_copy(rfa[:, :], PS[0:4, 2, 0:T])
            v.tensor_copy(rb[:, :], PS[0:2, 3, 0:T])
            link(v.tensor_copy(cont[:, :], PS[0:1, 4, 0:T]))
            v.tensor_tensor_scan(crow[0:1, 1:T + 1], rfa[0:1, :], PS[0:1, 0, 0:T], 0.0, ALU.mult, ALU.add)
            v.tensor_tensor_scan(brow[0:1, 0:T][:, ::-1], rb[0:1, :][:, ::-1], PS[0:1, 1, 0:T][:, ::-1], -BIG,
                                 ALU.add, ALU.max).then_inc(p_v, 1)
            dve.wait_ge(p_p, 2)
            link(v.tensor_copy(cb[:, 0, 0:2], PS[0:HALF, 5, 0:2]))
            link(v.tensor_copy(cb[:, 1, 0:2], PS[0:HALF, 6, 0:2]))
            for b in (0, 1):
                v.scalar_tensor_tensor(W4[:, 2, b], CM[:, b, :], cb[:, 0, b:b + 1], HS[:, 0, b], ALU.mult, ALU.add)
                last_ = v.scalar_tensor_tensor(W4[:, 3, b], LMB[:, b, :], cb[:, 1, b:b + 1], HS[:, 1, b],
                                               ALU.add, ALU.max)
            link(last_)
            v.scalar_tensor_tensor(V[:, 1], W4[:, 3], 1.0, W4[:, 2], ALU.add, ALU.subtract)
            link(v.tensor_tensor(V[:, 0], W4[:, 2], W4[:, 1], ALU.subtract))
            v.tensor_scalar_max(V[:, 2], V[:, 0], 0.0)
            v.tensor_copy(V[:, 3], dst2)
            v.tensor_copy(V[:, 4], srcraw[:, :, :]).then_inc(p_v, 1)

            dve.wait_ge(c_load, LOADED)
            for l in range(4):
                for k in (0, 1):
                    link(v.tensor_tensor(avt, WX[:, l, 0:D], av[2 * l + k], ALU.mult))
                    link(v.tensor_reduce(WX[:, l, D + 2 * k:D + 2 * k + 2], avt.rearrange("p (h c) -> p h c", h=2),
                                         AX.X, ALU.add))
            for w in range(3):
                lo, hi = (ED * k for k in (3 * w, min(3 * w + 3, 8)))
                link(v.tensor_reduce(is_part[:, w:w + 1], ident[:, lo:hi], AX.X, ALU.add))
            for in_, rest, sum_, high, mid, mask, to in (
                    (w_in, w_rest, w_sum, w_high, w_mid, is_part, ew1[:, :, :]),
                    (b_in, b_rest, b_sum, b_high, b_mid, ident[0:3, 0:3], None)):
                link(v.tensor_copy(high, in_))
                link(v.tensor_tensor(rest, in_, high, ALU.subtract))
                link(v.tensor_copy(mid, rest))
                link(v.tensor_tensor(rest, rest, mid, ALU.subtract))
                link(v.tensor_scalar(sum_, high, mask[:, 0:1], None, ALU.mult))
                link(v.scalar_tensor_tensor(sum_, mid, mask[:, 1:2], sum_, ALU.mult, ALU.add))
                link(v.scalar_tensor_tensor(sum_, rest, mask[:, 2:3], sum_, ALU.mult, ALU.add))
                if to is not None:
                    link(v.tensor_copy(to, sum_))
                else:
                    for j in range(4):
                        i = v.tensor_copy(eb2[:, :, j, :], sum_)
                    link(i)
            link(v.bn_stats(stat[:, 0, :], bias_r[:, 2, :]))
            link(v.bn_aggr(mv[:, 0, :], stat[:, 0, :]))
            v.tensor_copy(te4[:, 0:1], mv[:, 0, 1:2]).then_inc(p_va, 1)
            dve.wait_ge(p_a, 1)
            link(v.reciprocal(rs[:, 0:1], sd[:, 0:1]))
            link(v.tensor_scalar(c2_r[:, :], bias_r[:, 2, :], mv[:, 0, 0:1], rs[:, 0:1], ALU.subtract, ALU.mult))
            link(v.tensor_tensor(c2_r[:, :], c2_r[:, :], lnw_r[:, :], ALU.mult))
            link(v.tensor_tensor(c2_r[:, :], c2_r[:, :], lnb_r[:, :], ALU.add))
            link(v.tensor_scalar_max(c2_r[:, :], c2_r[:, :], 0.0))

            dve.wait_ge(p_p, 3)
            v.tensor_copy(deg[:, :], PS[:, 0, 0:T])
            v.tensor_copy(rel[:, :], PS[:, 1, 0:T])
            v.tensor_copy(te3[:, :], PS[:, 3, 0:T])
            v.tensor_copy(idx_src[:, :], PS[:, 4, 0:T])
            v.tensor_copy(relL[:, :], PS[0:1, 5, 0:T])
            link(v.tensor_scalar(te2[:, :], PS[:, 2, 0:T], -FAR, FAR, ALU.mult, ALU.add))
            link(v.scalar_tensor_tensor(relL[:, :], relL[:, :], 1.0, cont[:, :], ALU.add, ALU.mult))
            link(v.tensor_scalar_add(relL[:, :], relL[:, :], -1.0))
            v.tensor_tensor(idx_dst[:, :], te2[:, :], te3[:, :], ALU.add)
            v.tensor_scalar_min(idx_x[:, :], te3[:, :], float(N - 1))
            v.tensor_copy(node_val[:, :, 0], te1[:, :])
            v.tensor_copy(node_val[:, :, 1], deg[:, :]).then_inc(p_ready, 1)

            def norm_sums(q, m, b, x_, k):
                for j in range(4):
                    i = v.bn_stats(PST[b][:, j, :], x_[:, j, :])
                i.then_inc(q.sem, 1)
                alone(dve, (q.sem, q.at(0, m, f"stats{k}")))
                for j in range(4):
                    i = v.bn_aggr(PMV[b][:, j, :], PST[b][:, j, :])
                i.then_inc(q.sem, 1)

            def norm_coef(q, m, b, k):
                dve.wait_ge(q_a[b].sem, q_a[b].at(0, m, f"sd{k}"))
                v.reciprocal(PRS[b], PSD[b]).then_inc(q.sem, 1)
                dve.wait_ge(q.sem, q.at(0, m, f"rs{k}"))
                v.scalar_tensor_tensor(PNB[b], PMV[b][:, :, 0], -1.0, PRS[b], ALU.mult, ALU.mult).then_inc(q.sem, 1)

            def step_b(m, b, ins, name):
                ins.then_inc(q_v[b].sem, 1)
                dve.wait_ge(q_v[b].sem, q_v[b].at(0, m, name))

            def sums1(m, b):
                dve.wait_ge(q_ld[b].sem, q_ld[b].at(0, m, "x"))
                norm_sums(q_v[b], m, b, PXT[b], 1)

            def sums2(m, b):
                dve.wait_ge(q_p[b].sem, q_p[b].at(0, m, "t1"))
                step_b(m, b, v.tensor_tensor(PXT[b], PXT[b], bank(4 * b + 3), ALU.add), "x1")
                norm_sums(q_v[b], m, b, PXT[b], 2)

            def sums3(m, b):
                dve.wait_ge(q_p[b].sem, q_p[b].at(0, m, "rB"))
                st = q_st["out"][b]
                dve.wait_ge(st.sem, st.at(0, m))
                step_b(m, b, v.tensor_tensor(PYT[b], bank(4 * b + 3), on4(b2l_r[:, :]), ALU.add), "y")
                step_b(m, b, v.scalar_tensor_tensor(PXT[b], PYT[b], 0.0, PXT[b], ALU.max, ALU.add), "yx")
                norm_sums(q_v[b], m, b, PXT[b], 3)

            def convolution(m, b):
                dve.wait_ge(q_a[b].sem, q_a[b].at(0, m, "g1"))
                v.tensor_tensor(PXT[b], PXT[b], on4(b2_r[:, :]), ALU.add).then_inc(q_v[b].sem, 1)

            def hidden(m, b):
                dve.wait_ge(q_p[b].sem, q_p[b].at(0, m, "h1b"))
                v.tensor_scalar(PHT[b][:, 1, :], PS[:, 4 * b + 2, :], b1[:, 1:2], 0.0, ALU.add,
                                ALU.max).then_inc(q_v[b].sem, 1)

            def constant(m, b):
                dve.wait_ge(q_a[b].sem, q_a[b].at(0, m, "g2"))
                v.tensor_tensor(PXT[b], PXT[b], on4(c2_r[:, :]), ALU.add).then_inc(q_v[b].sem, 1)

            def out_bias(m, b):
                dve.wait_ge(q_a[b].sem, q_a[b].at(0, m, "g3"))
                v.tensor_tensor(PYT[b], PXT[b], on4(gout_r[:, :]), ALU.add).then_inc(q_v[b].sem, 1)

            def attention(m, b, *tables):
                for t in tables:
                    r = t - 10 if t > 9 else t - 6
                    before = {8: "t8", 9: "t9", 10: "t2", 11: "t4"}[t]
                    st = q_st[before][b]
                    dve.wait_ge(st.sem, st.at(0, m, before if t > 9 else None))
                    dve.wait_ge(q_p[b].sem, q_p[b].at(0, m, f"r{t}"))
                    v.tensor_copy(PRO[b][r], pair(4 * b + 2)).then_inc(q_v[b].sem, 1)
                    if t == 11:
                        alone(dve, (q_v[b].sem, q_v[b].at(0, m, "r11")))
                        v.tensor_tensor(PYT[b], PYT[b], PRO[b][1][:, :, 0:D], ALU.add).then_inc(q_v[b].sem, 1)

            def x_step(m, ins, name):
                ins.then_inc(vd.sem, 1)
                alone(dve, (vd.sem, vd.at(0, m, name)))

            def x_sums(m):
                for j in range(4):
                    dve.wait_ge(gat[j].sem, gat[j].at(0, m, "rows"))
                for j in range(4):
                    i = v.bn_stats(stat[:, j, :], M[:, j, 0:D])
                x_step(m, i, "stats")
                for j in range(4):
                    i = v.bn_aggr(mv[:, j, :], stat[:, j, :])
                i.then_inc(vd.sem, 1)

            def x_coef(m):
                dve.wait_ge(ad.sem, ad.at(0, m, "sd"))
                x_step(m, v.reciprocal(rs[:, :], sd[:, :]), "rs")
                v.scalar_tensor_tensor(nb[:, :], mv[:, :, 0], -1.0, rs[:, :], ALU.mult, ALU.mult).then_inc(vd.sem, 1)

            def plain(m):
                at = m if isinstance(m, int) else 1
                if at:
                    out_bias(m - 1, 1)
                sums1(m, 0)
                if at:
                    attention(m - 1, 1, 8)
                norm_coef(q_v[0], m, 0, 1)
                if at:
                    attention(m - 1, 1, 9, 10, 11)
                sums1(m, 1)
                hidden(m, 0)
                norm_coef(q_v[1], m, 1, 1)
                convolution(m, 0)
                x_sums(m)
                sums2(m, 0)
                hidden(m, 1)
                norm_coef(q_v[0], m, 0, 2)
                convolution(m, 1)
                x_coef(m)
                sums2(m, 1)
                constant(m, 0)
                norm_coef(q_v[1], m, 1, 2)
                sums3(m, 0)
                constant(m, 1)
                norm_coef(q_v[0], m, 0, 3)
                sums3(m, 1)
                out_bias(m, 0)
                attention(m, 0, 8)
                norm_coef(q_v[1], m, 1, 3)
                attention(m, 0, 9, 10, 11)

            plain(0)
            with dve.Fori(1, PLAIN_TURNS) as m:
                plain(m)
            out_bias(PLAIN_TURNS - 1, 1)
            attention(PLAIN_TURNS - 1, 1, 8, 9, 10, 11)

            dve.wait_ge(n_cp, QUADS)
            pos, degs = node_src[:, :, 0], node_src[:, :, 1]
            v.tensor_copy(te4[:, :], idx_src[:, :])
            link(v.tensor_scalar(te2[:, :], pos, 0.0, None, ALU.is_lt))
            link(v.scalar_tensor_tensor(te3[:, :], te4[:, :], float(EP + 1), te2[:, :], ALU.add, ALU.mult))
            link(v.tensor_tensor(idx_all[:, :], pos, te3[:, :], ALU.add))
            link(v.scalar_tensor_tensor(te3[:, :], te1[:, :], 1.0, te2[:, :], ALU.add, ALU.mult))
            link(v.tensor_tensor(idx_l2[:, :], pos, te3[:, :], ALU.add))
            link(v.tensor_scalar_add(dis2[:, :], deg[:, :], 1.0))
            link(v.scalar_tensor_tensor(te3[:, :], degs, 1.0, dis2[:, :], ALU.add, ALU.mult))
            link(v.scalar_tensor_tensor(te4[:, :], degs, 1.0, deg[:, :], ALU.max, ALU.mult))
            v.tensor_scalar(te2[:, :], te2[:, :], -1.0, 1.0, ALU.mult, ALU.add).then_inc(p_va, 1)
            dve.wait_ge(p_a, 2)
            link(v.reciprocal(wgcn[:, :], te3[:, :]))
            link(v.reciprocal(te4[:, :], te4[:, :]))
            link(v.tensor_tensor(wl2[:, :], te4[:, :], te2[:, :], ALU.mult))
            link(v.reciprocal(winv[:, :], deg[:, :]))
            link(v.reciprocal(dis2[:, :], dis2[:, :]))
            v.memset(te4[:, 0:1], 0.0).then_inc(p_ready, 1)

            def select(s, n, h, j):
                Q4 = n * (-4) + 4 * LAST
                weight = {"C": wgcn, "S": winv}.get(KINDS[s][0])
                dve.wait_ge(agg.sem, agg.at(s, n, f"t{0 if j == 3 else j}") - 8)
                if j == 3:
                    v.tensor_tensor(LO[:, 4 * h:4 * h + 4, :], iota_row[0:1, :].unsqueeze(1).to_broadcast([1, 4, P]),
                                    wide(relL[:, ds(Q4, 4)], P), ALU.is_equal)
                to = S[:, 4 * h + j, :]
                if weight is None:
                    i = v.tensor_scalar(to, iota_row[:, :], rel[:, ds(Q4 + j, 1)], None, ALU.is_equal)
                else:
                    i = v.tensor_scalar(to, iota_row[:, :], rel[:, ds(Q4 + j, 1)], weight[:, ds(Q4 + j, 1)],
                                        ALU.is_equal, ALU.mult)
                i.then_inc(sel.sem, 1)

            def messages(s, n, h):
                dve.wait_ge(pd_e.sem, pd_e.at(s, n, "em"))
                for j in (3, 2, 1, 0):
                    dve.wait_ge(gat[j].sem, gat[j].at(s, n, "rows"))
                    v.scalar_tensor_tensor(MP[:, 4 * h + j, :], M[:, j, 0:D], wl2[:, ds(n * (-4) + (4 * LAST + j), 1)],
                                           bank(5)[:, j, :], ALU.mult, ALU.add).then_inc(mprod.sem, 1)

            def step(s, n, ins, name, *meanwhile):
                ins.then_inc(vd.sem, 1)
                for work in meanwhile:
                    work()
                alone(dve, (vd.sem, vd.at(s, n, name)))

            def sums(s, n, x_, k="", w1_=(), w2_=()):
                for j in range(4):
                    i = v.bn_stats(stat[:, j, :], x_[:, j, :])
                step(s, n, i, "stats" + k, *w1_)
                for j in range(4):
                    i = v.bn_aggr(mv[:, j, :], stat[:, j, :])
                i.then_inc(vd.sem, 1)
                for work in w2_:
                    work()

            def coef(s, n, k="", w1_=()):
                dve.wait_ge(ad.sem, ad.at(s, n, "sd" + k))
                step(s, n, v.reciprocal(rs[:, :], sd[:, :]), "rs" + k, *w1_)
                v.scalar_tensor_tensor(nb[:, :], mv[:, :, 0], -1.0, rs[:, :], ALU.mult, ALU.mult).then_inc(vd.sem, 1)

            def aggregated(s, n):
                dve.wait_ge(agg.sem, agg.at(s, n, "t0"))
                dve.wait_ge(carry.sem, carry.at(s, n, "t0"))

            def over4(v_):
                return v_.unsqueeze(1).unsqueeze(1).to_broadcast([P, 2, 2, D])

            def finish(s, kind, n, h, ahead):
                Q4 = n * (-4) + 4 * LAST
                s3, s2, s1, s0 = ahead
                A, U4 = all_sums(h), by_bank(U[:, :, :])
                if kind in ("C1", "C2"):
                    dve.wait_ge(own.sem, own.at(s, n, "rows"))
                    ins = v.tensor_tensor(OWN[:, :, 0:D], OWN[:, :, 0:D], wide(dis2[:, ds(Q4, 4)], D), ALU.mult)
                    if kind == "C1":
                        step(s, n, ins, "own")
                        dve.wait_ge(pd.sem, pd.last(s, n, "uT"))
                    else:
                        ins.then_inc(vd.sem, 1)
                        dve.wait_ge(xin.sem, xin.at(s, n, "rows"))
                        step(s, n, v.tensor_tensor(XIN[:, :, :], XIN[:, :, :], on4(b2_r[:, :]), ALU.add), "bias")
                    aggregated(s, n)
                if kind == "C1":
                    v.tensor_tensor(U4, A, by_bank(OWN[:, :, 0:D]), ALU.add).then_inc(vd.sem, 1)
                    for work in (s3, s2, s1, s0):
                        work()
                    dve.wait_ge(pd.sem, pd.at(s, n, "h1b"))
                    v.tensor_scalar(H1T[:, 1, :], PS[:, 6, :], b1[:, 1:2], 0.0, ALU.add, ALU.max).then_inc(vd.sem, 1)
                elif kind == "C2":
                    step(s, n, v.tensor_tensor(U4, A, by_bank(OWN[:, :, 0:D]), ALU.add), "comb", s3)
                    dve.wait_ge(st_x.sem, st_x.at(s, n))
                    dve.wait_ge(ad.sem, ad.last(s, n, "g"))
                    step(s, n, v.tensor_tensor(RB[:, :, :], U[:, :, :], XIN[:, :, :], ALU.add), "x", s2)
                    sums(s, n, RB, "", (s1,), (s0,))
                    coef(s, n)
                elif kind == "S1":
                    dve.wait_ge(pd.sem, pd.last(s, n, "uT"))
                    aggregated(s, n)
                    v.tensor_copy(U4, A).then_inc(vd.sem, 1)
                    for work in (s3, s2, s1, s0):
                        work()
                    dve.wait_ge(pd.sem, pd.at(s, n, "rB"))
                    dve.wait_ge(st_x.sem, st_x.at(s, n))
                    v.tensor_tensor(RB[:, :, :], bank(4), on4(b2l_r[:, :]), ALU.add).then_inc(vd.sem, 1)
                elif kind == "S2":
                    dve.wait_ge(own.sem, own.at(s, n, "rows"))
                    aggregated(s, n)
                    step(s, n, v.tensor_tensor(U4, A, by_bank(OWN[:, :, 0:D]), ALU.add), "comb", s3)
                    dve.wait_ge(xin.sem, xin.at(s, n, "rows"))
                    dve.wait_ge(st_x.sem, st_x.at(s, n))
                    dve.wait_ge(ad.sem, ad.last(s, n, "g"))
                    step(s, n, v.scalar_tensor_tensor(RB[:, :, :], U[:, :, :], 0.0, XIN[:, :, :], ALU.max, ALU.add),
                         "x", s2)
                    sums(s, n, RB, "", (s1,), (s0,))
                    coef(s, n)
                elif kind in ("LA", "LB"):
                    if kind == "LA":
                        dve.wait_ge(ad.sem, ad.last(s, n, "n"))
                    aggregated(s, n)
                    step(s, n, v.tensor_tensor(U4, A, over4(bias_r[:, s - 5, :]), ALU.add), "comb", s3)
                    sums(s, n, U, "", (s2,), (s1,))
                    coef(s, n, "", (s0,))
                else:
                    aggregated(s, n)
                    ps = PT[:, 2:4, ds(Q4, 4)].rearrange("p h j -> p j h")
                    dve.wait_ge(vd.sem, vd.at(s, n))
                    v.tensor_tensor(by_bank(den[:, :, :]), all_sums(h, D, GW), by_bank(ps), ALU.add).then_inc(vd.sem, 1)
                    dve.wait_ge(hself.sem, hself.at(s, n, "own"))
                    if kind == "GA":
                        dve.wait_ge(pd.sem, pd.last(s, n, "uT"))
                    step(s, n, v.tensor_tensor(U4, A, by_bank(OWN[:, :, 0:D]), ALU.add), "comb", s3)
                    step(s, n, v.tensor_scalar_add(den[:, :, :], den[:, :, :], 1e-16), "dene", s2)
                    step(s, n, v.reciprocal(den[:, :, :], den[:, :, :]), "rden", s1)
                    for k in (0, 1):
                        uh = U[:, :, 64 * k:64 * k + 64]
                        i = v.tensor_tensor(uh, uh, wide(den[:, :, k], 64), ALU.mult)
                    if kind == "GA":
                        i.then_inc(vd.sem, 1)
                        s0()
                    else:
                        step(s, n, i, "norm", s0)
                        step(s, n, v.tensor_tensor(U[:, :, :], U[:, :, :], on4(gout_r[:, :]), ALU.add), "bias")
                        dve.wait_ge(xin.sem, xin.at(s, n, "rows"))
                        for j in range(4):
                            dve.wait_ge(st_o[j].sem, st_o[j].at(s, n))
                        v.tensor_tensor(RO[:, :, 0:D], U[:, :, :], XIN[:, :, :], ALU.add).then_inc(vd.sem, 1)

            def finish_lb(s, n):
                dve.wait_ge(ad.sem, ad.at(s, n, "n"))
                step(s, n, v.tensor_tensor(U[:, :, :], U[:, :, :], on4(lnw_r[:, :]), ALU.mult), "lnw")
                step(s, n, v.tensor_tensor(U[:, :, :], U[:, :, :], on4(lnb_r[:, :]), ALU.add), "lnb")
                dve.wait_ge(xin.sem, xin.at(s, n, "rows"))
                dve.wait_ge(st_x.sem, st_x.at(s, n))
                dve.wait_ge(ad.sem, ad.last(s, n, "g"))
                step(s, n, v.scalar_tensor_tensor(RB[:, :, :], U[:, :, :], 0.0, XIN[:, :, :], ALU.max, ALU.add), "x")
                sums(s, n, RB, "2")
                coef(s, n, "2")

            for s, kind in STAGES:
                if kind == "X":
                    continue
                if kind in hself.order:
                    with dve.Fori(0, QUADS) as n:
                        Q4 = n * (-4) + 4 * LAST
                        for j in (3, 2, 1, 0):
                            dve.wait_ge(gat[j].sem, gat[j].at(s, n, "rows"))
                            v.tensor_copy(G[:, ds(Q4 + j, 1), :], M[:, j:j + 1, :]).then_inc(m_free.sem, 1)
                    attention_middle(dve, v, link, s)

                def quad(n, h, s=s, kind=kind):
                    more = not isinstance(n, int) or n < LAST - 1
                    ahead = [(lambda j=j: select(s, n + 2, h, j)) if more else (lambda: None) for j in (3, 2, 1, 0)]
                    finish(s, kind, n, h, ahead)
                    if more and kind in ("LA", "LB"):
                        messages(s, n + 2, h)
                    if kind == "LB":
                        finish_lb(s, n)

                for n in (0, 1):
                    for j in (3, 2, 1, 0):
                        select(s, n, n, j)
                if kind in ("LA", "LB"):
                    messages(s, 0, 0)
                    messages(s, 1, 1)
                quad(0, 0)
                with dve.Fori(0, LAST // 2 - 1) as m:
                    quad(m * 2 + 1, 1)
                    quad(m * 2 + 2, 0)
                quad(LAST - 1, 1)
                quad(LAST, 0)

        @block.tensor
        def _(pe):
            def turn(o, i):
                k = i.shape[0]
                return nc.tensor.transpose(o, i, ident[0:k, 0:k])

            def mm(o, l, r, start=True, stop=True):
                return nc.tensor.matmul(o, l, r, start=start, stop=stop)

            pe.wait_ge(c_pool, 5)
            pe.wait_ge(p_v, 1)
            for c, (lo, hi) in enumerate(((0, 1), (1, 2), (2, 6), (6, 8), (8, 9))):
                for b in (0, 1):
                    i = turn(PS[0:hi - lo, c, HALF * b:HALF * b + HALF], ends[:, b, lo:hi])
            i.then_inc(p_p, 1)
            pe.wait_ge(p_v, 2)
            for b in (0, 1):
                turn(PS[0:HALF, 5, b:b + 1], crow[0:1, HALF * b:HALF * b + HALF])
                i = turn(PS[0:HALF, 6, b:b + 1], brow[0:1, HALF * b + 1:HALF * b + HALF + 1])
            i.then_inc(p_p, 1)
            pe.wait_ge(p_v, 3)
            for c, t in enumerate((V[:, 1], V[:, 2], FI4[:, 0], V[:, 3], V[:, 4])):
                for b in (0, 1):
                    turn(PS[:, c, HALF * b:HALF * b + HALF], t[:, b, :])
            for b in (0, 1):
                i = turn(PS[0:1, 5, HALF * b:HALF * b + HALF], V[:, 2, b, P - 1:P])
            i.then_inc(p_p, 1)
            pe.wait_ge(c_load, LOADED)
            pe.wait_ge(p_ready, 1)

            def turn4(o, rows):
                for j in range(4):
                    i = turn(o[:, P * j:P * j + P], rows[:, j, :])
                return i

            def rows4(o, hT, w):
                for j in range(4):
                    i = mm(o[:, j, :], hT[:, P * j:P * j + P], w)
                return i

            def turned(m, b, k):
                if k == 1 and not (isinstance(m, int) and m == 0):
                    pe.wait_ge(q_v[b].sem, q_v[b].at(0, m))
                for j in range(4):
                    if j % 2 == 0:
                        pe.wait_ge(q_a[b].sem, q_a[b].at(0, m, (f"half{k}", f"g{k}")[j // 2]))
                    i = turn(PS[:, 4 * b, P * j:P * j + P], PGN[b][:, j, :])
                i.then_inc(q_p[b].sem, 1)
                pe.wait_ge(q_a[b].sem, q_a[b].at(0, m, f"gT{k}"))

            def convolutions(m, b):
                turned(m, b, 1)
                mm(PS[:, 4 * b + 1], w1[:, 0:P], PTT[b]).then_inc(q_p[b].sem, 1)
                mm(PS[:, 4 * b + 2], w1[:, P:2 * P], PTT[b]).then_inc(q_p[b].sem, 1)
                pe.wait_ge(q_a[b].sem, q_a[b].at(0, m, "h1a"))
                pe.wait_ge(q_v[b].sem, q_v[b].at(0, m, "h1b"))
                for j in range(4):
                    for k in (0, 1):
                        i = mm(bank(4 * b + 3)[:, j, :], PHT[b][:, k, P * j:P * j + P], w2[:, k, :], k == 0, k == 1)
                i.then_inc(q_p[b].sem, 1)

            def sage(m, b):
                turned(m, b, 2)
                mm(PS[:, 4 * b + 1], w1r[:, :], PTT[b]).then_inc(q_p[b].sem, 1)
                pe.wait_ge(q_a[b].sem, q_a[b].at(0, m, "h2"))
                rows4(bank(4 * b + 2), PHT[b][:, 0, :], w2l[:, :]).then_inc(q_p[b].sem, 1)
                rows4(bank(4 * b + 3), PHT[b][:, 0, :], w2r[:, :]).then_inc(q_p[b].sem, 1)

            def attention(m, b):
                turned(m, b, 3)
                for l, hT, at in ((0, PTT[b], None), (1, PHT[b][:, 0, :], "h8"), (2, PHT[b][:, 1, :], "h9"),
                                  (3, PHT[b][:, 0, :], "h10")):
                    if l:
                        pe.wait_ge(q_a[b].sem, q_a[b].at(0, m, at))
                    if l < 3:
                        mm(PS[:, 4 * b + 1], WX[:, l, 0:D], hT).then_inc(q_p[b].sem, 1)
                    if l:
                        pe.wait_ge(q_v[b].sem, q_v[b].at(0, m, f"r{7 + l}"))
                    rows4(pair(4 * b + 2), hT, WX[:, l, 0:GW]).then_inc(q_p[b].sem, 1)

            def plain(m):
                if not (isinstance(m, int) and m == 0):
                    attention(m - 1, 1)
                convolutions(m, 0)
                convolutions(m, 1)
                alone(pe, (e_split.sem, e_split.at(0, m, "placed")))
                turn4(PS[:, 5], E8).then_inc(e_tr, 1)
                sage(m, 0)
                pe.wait_ge(e_cp, m + 1)
                sage(m, 1)
                attention(m, 0)

            plain(0)
            with pe.Fori(1, PLAIN_TURNS) as m:
                plain(m)
            attention(PLAIN_TURNS - 1, 1)
            for b in (0, 1):
                pe.wait_ge(q_v[b].sem, q_v[b].at(0, PLAIN_TURNS - 1, "xf"))

            def edge_hidden(s, n):
                pe.wait_ge(eas.sem, eas.at(s, n, "attr"))
                mm(PS[:, 4, :], ew1[:, s - 5, :], eat[:, :]).then_inc(pd_e.sem, 1)

            def edge_terms(s, n):
                l = s - 5
                pe.wait_ge(ad_e.sem, ad_e.at(s, n, "rT"))
                pe.wait_ge(mprod.sem, mprod.at(s, n))
                mm(PS[:, 5, :], ones_row[:, :], eb2[:, l, :, :].rearrange("p j c -> p (j c)"), True, False)
                for j in range(4):
                    i = mm(bank(5)[:, j, :], H1T[:, 0, P * j:P * j + P], ew2[:, l, :], False, j == 3)
                i.then_inc(pd_e.sem, 1)

            def tile(s, n, h, j, between=None):
                kind = KINDS[s]
                w = GW if kind in hself.order else D
                if j == 3:
                    if kind in hself.order:
                        pe.wait_ge(mprod.sem, mprod.at(s, n, "quad"))
                    pe.wait_ge(vd.sem, vd.at(s, n, "comb") - 2 * len(vd.order[kind]))
                A = sums_of(h, j, w)
                slot = 4 * h + j
                pe.wait_ge(sel.sem, sel.at(s, n, f"t{j}"))
                if kind in hself.order:
                    mm(A, S[:, slot, :], G[:, ds(n * (-4) + (4 * LAST + j), 1), :].rearrange("p t c -> p (t c)"), True, False)
                elif kind in ("LA", "LB"):
                    pe.wait_ge(mprod.sem, mprod.at(s, n, f"t{j}"))
                    mm(A, S[:, slot, :], MP[:, slot, :], True, False)
                else:
                    pe.wait_ge(gat[j].sem, gat[j].at(s, n, "rows"))
                    mm(A, S[:, slot, :], M[:, j, 0:D], True, False).then_inc(m_free.sem, 1)
                if between:
                    between()
                pe.wait_ge(carry.sem, carry.at(s, n) + (3 - j))
                mm(A, LO[:, slot, :], C[:, 0:w], False, True).then_inc(agg.sem, 1)

            def finish(s, kind, n, ahead):
                t3, t2, t1, t0 = ahead

                if kind == "C1":
                    t3()
                    pe.wait_ge(vd.sem, vd.at(s, n, "comb"))
                    turn4(PS[:, 4], U).then_inc(pd.sem, 1)
                    t2()
                    pe.wait_ge(ad.sem, ad.at(s, n, "uT"))
                    mm(PS[:, 5, :], w1[:, 0:P], UT[:, :]).then_inc(pd.sem, 1)
                    mm(PS[:, 6, :], w1[:, P:2 * P], UT[:, :]).then_inc(pd.sem, 1)
                    t1()
                    pe.wait_ge(ad.sem, ad.at(s, n, "h1a"))
                    pe.wait_ge(vd.sem, vd.at(s, n, "h1b"))
                    for j in range(4):
                        for k in (0, 1):
                            i = mm(bank(7)[:, j, :], H1T[:, k, P * j:P * j + P], w2[:, k, :], k == 0, k == 1)
                        if j == 1:
                            t0()
                    i.then_inc(pd.sem, 1)
                elif kind == "C2":
                    for t in ahead:
                        t()
                elif kind == "S1":
                    pe.wait_ge(own.sem, own.at(s, n, "rows"))
                    turn4(PS[:, 5], OWN[:, :, 0:D]).then_inc(pd.sem, 1)
                    t3()
                    pe.wait_ge(vd.sem, vd.at(s, n, "comb"))
                    turn4(PS[:, 4], U).then_inc(pd.sem, 1)
                    t2()
                    pe.wait_ge(ad.sem, ad.at(s, n, "uT"))
                    mm(PS[:, 6, :], w1l[:, :], UT[:, :], True, False)
                    mm(PS[:, 6, :], w1r[:, :], OT[:, :], False, True).then_inc(pd.sem, 1)
                    t1()
                    pe.wait_ge(ad.sem, ad.at(s, n, "hT"))
                    rows4(bank(7), H1T[:, 0, :], w2l[:, :]).then_inc(pd.sem, 1)
                    t0()
                    rows4(bank(4), H1T[:, 0, :], w2r[:, :]).then_inc(pd.sem, 1)
                elif kind == "LA":
                    for t in ahead:
                        t()
                    pe.wait_ge(ad.sem, ad.at(s, n, "n"))
                    turn4(PS[:, 6], GN).then_inc(pd.sem, 1)
                elif kind == "GA":
                    for t in ahead:
                        t()
                    pe.wait_ge(vd.sem, vd.at(s, n, "norm"))
                    turn4(PS[:, 4], U).then_inc(pd.sem, 1)
                else:
                    for t in ahead:
                        t()

            def late_rows(s, n, j):
                if j == 3:
                    done, name = (ad_t, "nT") if KINDS[s] == "LA" else (ad, "uT")
                    pe.wait_ge(done.sem, done.at(s, n, name))
                o, w = (bank(7), linw[:, s - 4, :]) if KINDS[s] == "LA" else (pair(6, GW + 2), WX[:, s - 7, :])
                i = mm(o[:, 3 - j, :], OT[:, P * (3 - j):P * (3 - j) + P], w)
                if j == 0:
                    i.then_inc(pd.sem, 1)

            def tail_turn(s, n):
                pe.wait_ge(ad.sem, ad.at(s, n, "g"))
                if KINDS[s] == "LB":
                    pe.wait_ge(ad_t.sem, ad_t.at(s, n))
                turn4(PS[:, 6 if KINDS[s] == "LB" else 4], GN).then_inc(pd.sem, 1)

            def tail_rows(s, n):
                pe.wait_ge(ad_t.sem, ad_t.at(s, n, "gT"))
                if KINDS[s] == "S2":
                    rows4(bank(7), OT[:, :], linw[:, 0, :]).then_inc(pd.sem, 1)
                else:
                    rows4(pair(6, GW + 2), OT[:, :], WX[:, 0, :]).then_inc(pd.sem, 1)

            for s, kind in STAGES:
                if kind == "X":
                    continue
                pe.wait_ge(vd.sem, vd.at(s, 0))
                pe.wait_ge(ad.sem, ad.at(s, 0))
                pe.wait_ge(ad_t.sem, ad_t.at(s, 0))
                if kind in hself.order:
                    attention_turns(pe, turn, s)

                def quad(n, h, s=s, kind=kind):
                    at = n if isinstance(n, int) else 1
                    edge = kind in ("LA", "LB")

                    def next_tile(j):
                        if at < LAST:
                            late = kind in LATE and at
                            tile(s, n + 1, 1 - h, j, (lambda: late_rows(s, n - 1, j)) if late else None)
                            if j == 3 and edge and at < LAST - 1:
                                edge_hidden(s, n + 2)
                            if j == (2 if kind == "LB" else 1) and edge and at < LAST - 1:
                                edge_terms(s, n + 2)
                            if j == 2 and kind in BEHIND and at:
                                tail_turn(s, n - 1)
                            if j == 0 and kind in BEHIND and at:
                                tail_rows(s, n - 1)

                    if kind in BEHIND and at == LAST:
                        tail_turn(s, n - 1)
                    if kind in LATE and at == LAST:
                        for j in (3, 2, 1, 0):
                            late_rows(s, n - 1, j)
                    finish(s, kind, n, [lambda j=j: next_tile(j) for j in (3, 2, 1, 0)])
                    if kind in LATE and at == LAST:
                        for j in (3, 2, 1, 0):
                            late_rows(s, n, j)
                    if kind in BEHIND and at == LAST:
                        tail_rows(s, n - 1)
                        tail_turn(s, n)
                        tail_rows(s, n)

                if kind in ("LA", "LB"):
                    edge_hidden(s, 0)
                    edge_terms(s, 0)
                    edge_hidden(s, 1)
                tile(s, 0, 0, 3)
                if kind in ("LA", "LB"):
                    edge_terms(s, 1)
                for j in (2, 1, 0):
                    tile(s, 0, 0, j)
                quad(0, 0)
                with pe.Fori(0, LAST // 2 - 1) as m:
                    quad(m * 2 + 1, 1)
                    quad(m * 2 + 2, 0)
                quad(LAST - 1, 1)
                quad(LAST, 0)

        @block.scalar
        def _(act):
            def f(o, i, fn, **kw):
                return nc.scalar.activation(o, i, fn, **kw)

            nc.scalar.preload_act_table(ACT.Sqrt)
            act.wait_ge(c_pool, 5)
            act.wait_ge(p_va, 1)
            f(sd[:, 0:1], te4[:, 0:1], ACT.Sqrt, bias=eps[:, :]).then_inc(p_a, 1)
            act.wait_ge(c_load, LOADED)

            def norm(m, b, k):
                act.wait_ge(q_v[b].sem, q_v[b].at(0, m, f"aggr{k}"))
                f(PSD[b], PMV[b][:, :, 1], ACT.Sqrt, bias=eps[:, :]).then_inc(q_a[b].sem, 1)

            def apply(m, b, k, st):
                act.wait_ge(q_v[b].sem, q_v[b].at(0, m, f"nb{k}"))
                act.wait_ge(*st)
                for j in range(4):
                    i = f(PGN[b][:, j, :], PXT[b][:, j, :], ACT.Relu, scale=PRS[b][:, j:j + 1], bias=PNB[b][:, j:j + 1])
                    if j % 2:
                        i.then_inc(q_a[b].sem, 1)

            def applied(m, b, k):
                st = q_st["t1" if k == 2 else "t3"][b]
                apply(m, b, k, (st.sem, st.at(0, m, st.order["P"][0]) if k > 1 else st.at(0, m)))

            def turned(m, b, k):
                act.wait_ge(q_p[b].sem, q_p[b].at(0, m, f"gT{k}"))
                f(PTT[b], PS[:, 4 * b, :], ACT.Copy).then_inc(q_a[b].sem, 1)

            def hidden(m, b, name, to, bias):
                act.wait_ge(q_p[b].sem, q_p[b].at(0, m, name))
                f(PHT[b][:, to, :], PS[:, 4 * b + 1, :], ACT.Relu, bias=bias).then_inc(q_a[b].sem, 1)

            def convolved(m, b):
                act.wait_ge(q_v[b].sem, q_v[b].at(0, m, "x1"))
                st = q_st["t10"][b]
                act.wait_ge(st.sem, st.at(0, m))
                f(PRO[b][0][:, :, 0:D], bank(4 * b + 3), ACT.Copy).then_inc(q_a[b].sem, 1)

            def sampled(m, b):
                act.wait_ge(q_p[b].sem, q_p[b].at(0, m, "rA"))
                st = q_st["t11"][b]
                act.wait_ge(st.sem, st.at(0, m))
                act.wait_ge(q_v[b].sem, q_v[b].at(0, m))
                f(PRO[b][1][:, :, 0:D], bank(4 * b + 2), ACT.Copy).then_inc(q_a[b].sem, 1)

            def attention(m, b, *layers):
                for l in layers:
                    hidden(m, b, f"h{8 + l}", l % 2, gb_c[:, l:l + 1])

            def plain(m):
                at = m if isinstance(m, int) else 1
                if at:
                    turned(m - 1, 1, 3)
                    attention(m - 1, 1, 0)
                norm(m, 0, 1)
                if at:
                    attention(m - 1, 1, 1)
                applied(m, 0, 1)
                if at:
                    attention(m - 1, 1, 2)
                turned(m, 0, 1)
                norm(m, 1, 1)
                hidden(m, 0, "h1a", 0, b1[:, 0:1])
                applied(m, 1, 1)
                act.wait_ge(vd.sem, vd.at(0, m, "aggr"))
                f(sd[:, :], mv[:, :, 1], ACT.Sqrt, bias=eps[:, :]).then_inc(ad.sem, 1)
                turned(m, 1, 1)
                convolved(m, 0)
                norm(m, 0, 2)
                hidden(m, 1, "h1a", 0, b1[:, 0:1])
                applied(m, 0, 2)
                turned(m, 0, 2)
                convolved(m, 1)
                norm(m, 1, 2)
                hidden(m, 0, "h2", 0, b1l[:, 0:1])
                applied(m, 1, 2)
                act.wait_ge(vd.sem, vd.at(0, m, "nb"))
                act.wait_ge(st_t.sem, st_t.at(0, m))
                for j in range(4):
                    i = f(GN[:, j, :], M[:, j, 0:D], ACT.Relu, scale=rs[:, j:j + 1], bias=nb[:, j:j + 1])
                i.then_inc(ad.sem, 1)
                act.wait_ge(e_tr, m + 1)
                act.wait_ge(e_st, m * 16)
                f(eat[:, :].rearrange("c (p j) -> c j p", j=4), PS[:, 5, :].rearrange("c (j p) -> c j p", j=4),
                  ACT.Copy).then_inc(e_cp, 1)
                sampled(m, 0)
                turned(m, 1, 2)
                norm(m, 0, 3)
                hidden(m, 1, "h2", 0, b1l[:, 0:1])
                applied(m, 0, 3)
                sampled(m, 1)
                turned(m, 0, 3)
                attention(m, 0, 0)
                norm(m, 1, 3)
                attention(m, 0, 1)
                applied(m, 1, 3)
                attention(m, 0, 2)

            plain(0)
            with act.Fori(1, PLAIN_TURNS) as m:
                plain(m)
            turned(PLAIN_TURNS - 1, 1, 3)
            attention(PLAIN_TURNS - 1, 1, 0, 1, 2)
            act.wait_ge(p_va, 2)
            f(te3[:, :], te3[:, :], ACT.Sqrt)
            f(te4[:, :], te4[:, :], ACT.Sqrt).then_inc(p_a, 1)

            def sqrts(s, n, k=""):
                act.wait_ge(vd.sem, vd.at(s, n, "aggr" + k))
                f(sd[:, :], mv[:, :, 1], ACT.Sqrt, bias=eps[:, :]).then_inc(ad.sem, 1)

            def scaled(s, n, fn, k="", from_=RB, to=GN):
                act.wait_ge(vd.sem, vd.at(s, n, "nb" + k))
                for j in range(4):
                    i = f(to[:, j, :], from_[:, j, :], fn, scale=rs[:, j:j + 1], bias=nb[:, j:j + 1])
                i.then_inc(ad.sem, 1)

            def edge_relu(s, n):
                act.wait_ge(pd_e.sem, pd_e.at(s, n, "rT"))
                f(H1T[:, 0, :], PS[:, 4, :], ACT.Relu, bias=eb1[:, s - 5:s - 4]).then_inc(ad_e.sem, 1)

            def carried(s, n, h, *tiles):
                w = GW if KINDS[s] in hself.order else D
                for j in tiles:
                    act.wait_ge(agg.sem, agg.at(s, n, f"t{j}"))
                    f(C[:, 0:w], sums_of(h, j, w, 1), ACT.Copy).then_inc(carry.sem, 1)

            def finish(s, kind, n, ahead):
                late = not isinstance(n, int) or n > 0

                def out_rows():
                    act.wait_ge(st_t.sem, st_t.at(s, n))
                    act.wait_ge(pd.sem, pd.at(s, n, "rA" if kind == "S1" else "rows"))
                    f(RO[:, :, 0:D], bank(7), ACT.Copy).then_inc(ad.sem, 1)

                if kind == "C2":
                    ahead(3, 2, 1)
                    sqrts(s, n)
                    ahead(0)
                    act.wait_ge(st_t.sem, st_t.at(s, n))
                    scaled(s, n, ACT.Relu)
                elif kind == "C1":
                    ahead(3)
                    act.wait_ge(pd.sem, pd.at(s, n, "uT"))
                    f(UT[:, :], PS[:, 4, :], ACT.Copy).then_inc(ad.sem, 1)
                    ahead(2)
                    act.wait_ge(pd.sem, pd.at(s, n, "h1a"))
                    f(H1T[:, 0, :], PS[:, 5, :], ACT.Relu, bias=b1[:, 0:1]).then_inc(ad.sem, 1)
                    ahead(1, 0)
                    out_rows()
                elif kind == "S1":
                    act.wait_ge(pd.sem, pd.at(s, n, "oT"))
                    f(OT[:, :], PS[:, 5, :], ACT.Copy).then_inc(ad.sem, 1)
                    ahead(3)
                    act.wait_ge(pd.sem, pd.at(s, n, "uT"))
                    f(UT[:, :], PS[:, 4, :], ACT.Copy).then_inc(ad.sem, 1)
                    ahead(2)
                    act.wait_ge(pd.sem, pd.at(s, n, "hT"))
                    f(H1T[:, 0, :], PS[:, 6, :], ACT.Relu, bias=b1l[:, 0:1]).then_inc(ad.sem, 1)
                    ahead(1, 0)
                    out_rows()
                elif kind == "S2":
                    ahead(3, 2)
                    sqrts(s, n)
                    ahead(1, 0)
                    scaled(s, n, ACT.Relu)
                elif kind == "LA":
                    l = s - 5
                    ahead(3)
                    sqrts(s, n)
                    ahead(2, 1)
                    scaled(s, n, ACT.Identity, "", U)
                    ahead(0)
                    if late:
                        tail_out(s, n - 1)
                    act.wait_ge(pd.sem, pd.at(s, n, "nT"))
                    f(OT[:, :], PS[:, 6, :], ACT.Relu, scale=lnw_c[:, l:l + 1],
                      bias=lnb_c[:, l:l + 1]).then_inc(ad_t.sem, 1)
                elif kind == "LB":
                    ahead(3)
                    sqrts(s, n)
                    scaled(s, n, ACT.Identity, "", U, U)
                    ahead(2, 1, 0)
                    sqrts(s, n, "2")
                    scaled(s, n, ACT.Relu, "2")
                elif kind == "GA":
                    ahead(3, 2, 1, 0)
                    if late:
                        attention_rows(s, n - 1, ad)
                    act.wait_ge(pd.sem, pd.at(s, n, "uT"))
                    f(OT[:, :], PS[:, 4, :], ACT.Relu, bias=gb_c[:, s - 8:s - 7]).then_inc(ad.sem, 1)
                else:
                    ahead(3, 2, 1, 0)

            def attention_rows(s, n, done):
                Q4 = n * (-4) + 4 * LAST
                act.wait_ge(st_t.sem, st_t.at(s, n))
                act.wait_ge(pd.sem, pd.at(s, n, "rows"))
                f(RO[:, :, :], pair(6), ACT.Copy).then_inc(done.sem, 1)
                f(NV[:, :, ds(Q4, 4)].rearrange("p k j -> p j k"), pair(6, GW + 2)[:, :, D:GW + 2],
                  ACT.Copy).then_inc(done.sem, 1)

            def tail_turned(s, n):
                act.wait_ge(pd.sem, pd.at(s, n, "gT"))
                f(OT[:, :], PS[:, 6 if KINDS[s] == "LB" else 4, :], ACT.Copy).then_inc(ad_t.sem, 1)

            def tail_out(s, n):
                if KINDS[s] in ("S2", "LA"):
                    act.wait_ge(st_t.sem, st_t.at(s, n))
                    act.wait_ge(pd.sem, pd.at(s, n, "rows"))
                    f(RO[:, :, 0:D], bank(7), ACT.Copy).then_inc(ad_t.sem, 1)
                else:
                    attention_rows(s, n, ad_t)

            for s, kind in STAGES:
                if kind == "X":
                    continue
                if kind in hself.order:
                    attention_exp(act, f, s)

                def quad(n, h, s=s, kind=kind):
                    at = n if isinstance(n, int) else 1
                    edge = kind in ("LA", "LB")
                    behind = kind in BEHIND

                    def next_tiles(*tiles):
                        for j in tiles:
                            if at < LAST:
                                carried(s, n + 1, 1 - h, j)
                            if j == 3 and edge and at < LAST - 1:
                                edge_relu(s, n + 2)
                            if j == 2 and behind and 0 < at < LAST:
                                tail_turned(s, n - 1)

                    if behind and at == LAST:
                        tail_turned(s, n - 1)
                    finish(s, kind, n, next_tiles)
                    if behind and at:
                        tail_out(s, n - 1)
                    if behind and at == LAST:
                        tail_turned(s, n)
                        tail_out(s, n)
                    if kind == "LA" and at == LAST:
                        tail_out(s, n)
                    if kind == "GA" and at == LAST:
                        attention_rows(s, n, ad)

                if kind in ("LA", "LB"):
                    edge_relu(s, 0)
                    edge_relu(s, 1)
                carried(s, 0, 0, 3, 2, 1, 0)
                quad(0, 0)
                with act.Fori(0, LAST // 2 - 1) as m:
                    quad(m * 2 + 1, 1)
                    quad(m * 2 + 2, 0)
                quad(LAST - 1, 1)
                quad(LAST, 0)


_INS = ["x", "src", "dst", "edge_attr_16", "L0_gnn_W1", "L0_gnn_b1", "L0_gnn_W2", "L0_gnn_b2",
        "L1_gnn_w1l", "L1_gnn_b1l", "L1_gnn_w1r", "L1_gnn_w2l", "L1_gnn_b2l", "L1_gnn_w2r",
        "L2_gnn_lin_w", "L2_gnn_edge_w1", "L2_gnn_edge_b1", "L2_gnn_edge_w2", "L2_gnn_edge_b2",
        "L2_gnn_bias", "L2_gnn_ln_w", "L2_gnn_ln_b", "L3_gnn_W_in", "L3_gnn_a_src_in", "L3_gnn_a_dst_in",
        "L3_gnn_b_in", "L3_gnn_W_h", "L3_gnn_a_src_h", "L3_gnn_a_dst_h", "L3_gnn_b_h", "L3_gnn_W_out",
        "L3_gnn_a_src_out", "L3_gnn_a_dst_out", "L3_gnn_b_out"]


def kernel(**inputs):
    import numpy as _np
    import concourse.bacc as _bacc
    from concourse.bass_utils import run_bass_kernel_spmd as _run

    nc = _bacc.Bacc("TRN2", target_bir_lowering=False, num_devices=1)
    arrays, aps = {}, {}
    for name in _INS:
        arr = _np.ascontiguousarray(inputs[name])
        arrays[f"in_{name}"] = arr
        aps[name] = nc.dram_tensor(f"in_{name}", arr.shape, mybir.dt.from_np(arr.dtype), kind="ExternalInput").ap()
    out = nc.dram_tensor("out_x", (N, D), mybir.dt.float32, kind="ExternalOutput").ap()
    gnn_program(nc, aps, out)
    r = _run(nc, [arrays], core_ids=[0])
    return r.results[0]["out_x"]
```
